# Optimizing a Trainium2 kernel written in Bass

```python
import numpy as np
import jax
import jax.numpy as jnp

def _softmax(x, axis=-1):
    return jax.nn.softmax(x, axis=axis)

def _gelu(x):
    return jax.nn.gelu(x, approximate=True)

def _silu(x):
    return jax.nn.silu(x)

def _sigmoid(x):
    return jax.nn.sigmoid(x)

def _layernorm(x, axis=-1, eps=1e-05):
    m = jnp.mean(x, axis=axis, keepdims=True)
    v = jnp.var(x, axis=axis, keepdims=True)
    return (x - m) / jnp.sqrt(v + eps)

def _scatter_add(tgt, idx, src, axis=0):
    return tgt.at[idx].add(src)

def _segment_sum(src, seg, n):
    return jax.ops.segment_sum(src, seg, n)
kernel_name = 'mk_early_fusion_d1_tok_img1024_r4_c20d71'

def setup_inputs(seed: int=0):
    np.random.seed(seed)
    _w = jnp.asarray

    def _rec_inputs():
        import jax
        import jax.numpy as jnp
        _rk = jax.random.key(seed)
        x = -0.000222058 + 0.999998 * jax.random.normal(jax.random.fold_in(_rk, 1), (64, 3, 112, 112), jnp.float32)
        txt = 0.00193382 + 0.183443 * jax.random.normal(jax.random.fold_in(_rk, 2), (64, 32, 256), jnp.float32)
        return (x, txt)
    x, txt = _rec_inputs()

    def _L0_tok_setup():
        import jax, jax.numpy as jnp
        import numpy as np
        P = 16
        C = 3
        D = 256

        def _patchify(x, p):
            B, Cc, H, W = x.shape
            gh, gw = (H // p, W // p)
            x = x.reshape(B, Cc, gh, p, gw, p)
            x = x.transpose(0, 2, 4, 1, 3, 5)
            return x.reshape(B, gh * gw, Cc * p * p)
        key = jax.random.key(seed)
        k1, k2, k3, k4, k5 = jax.random.split(key, 5)
        patch_dim = C * P * P
        s1 = 1.0 / np.sqrt(patch_dim)
        s2 = 1.0 / np.sqrt(D)
        return {'x': jax.random.normal(k1, (32, C, 128, 128), dtype=jnp.float32), 'W1': jax.random.uniform(k2, (patch_dim, D), jnp.float32, -s1, s1), 'b1': jax.random.uniform(k3, (D,), jnp.float32, -s1, s1), 'W2': jax.random.uniform(k4, (D, D), jnp.float32, -s2, s2), 'b2': jax.random.uniform(k5, (D,), jnp.float32, -s2, s2)}
    _L0_tok_all = _L0_tok_setup()
    _L0_tok_in = {k: v for k, v in _L0_tok_all.items() if k in ('W1', 'b1', 'W2', 'b2')}
    del _L0_tok_all

    def _L0_attn_setup():
        import math
        import jax, jax.numpy as jnp
        import numpy as np
        N_EMBD = 256
        N_HEAD = 16
        HEAD_DIM = N_EMBD // N_HEAD

        def alibi_slopes(n_heads):
            start = 2.0 ** (-2.0 ** (-(math.log2(n_heads) - 3)))
            return np.array([start * start ** i for i in range(n_heads)], dtype=np.float32)
        key = jax.random.key(seed)
        k1, k2, k3 = jax.random.split(key, 3)
        B, T, C = (2, 512, N_EMBD)
        x = jax.random.normal(k1, (B, T, C), dtype=jnp.float32)
        w_attn = jax.random.normal(k2, (3 * C, C), dtype=jnp.float32) * (1.0 / math.sqrt(C))
        w_proj = jax.random.normal(k3, (C, C), dtype=jnp.float32) * (1.0 / math.sqrt(C))
        return {'x': x, 'w_attn': w_attn, 'w_proj': w_proj}
    _L0_attn_all = _L0_attn_setup()
    _L0_attn_in = {k: v for k, v in _L0_attn_all.items() if k in ('w_attn', 'w_proj')}
    del _L0_attn_all

    def _L0_ffn_setup():
        import jax, jax.numpy as jnp
        import numpy as np
        D = 256
        HD = 128
        EA = 8
        KA = 2
        EF = 16
        KF = 2
        FH = 128
        MAXP = 64
        B, S = (4, 256)
        EPS = 1e-05

        def _layer_norm(x, w, b):
            mu = x.mean(-1, keepdims=True)
            var = ((x - mu) ** 2).mean(-1, keepdims=True)
            return (x - mu) * jax.lax.rsqrt(var + EPS) * w + b

        def _topk_gates(logits, k):
            top_vals, top_idx = jax.lax.top_k(logits, k)
            g = jax.nn.softmax(top_vals, axis=-1)
            onehot = jax.nn.one_hot(top_idx, logits.shape[-1], dtype=logits.dtype)
            return jnp.einsum('...k,...ke->...e', g, onehot)

        def _moa(x, gate_w, q_w, q_b, k_w, k_b, v_w, v_b, o_w, o_b, rel_table):
            S_ = x.shape[1]
            gates = _topk_gates(x @ gate_w, KA)
            q = (jnp.einsum('bsd,edh->bseh', x, q_w) + q_b) * HD ** (-0.5)
            k = x @ k_w + k_b
            v = x @ v_w + v_b
            scores = jnp.einsum('bqeh,bkh->beqk', q, k)
            rel_s = jnp.einsum('bqeh,rh->beqr', q, rel_table)
            pos = jnp.arange(S_)
            rel_idx = jnp.clip(pos[None, :] - pos[:, None], -MAXP, MAXP) + MAXP
            scores = scores + jnp.take_along_axis(rel_s, rel_idx[None, None], axis=-1)
            p = jax.nn.softmax(scores, axis=-1)
            ctx = jnp.einsum('beqk,bkh->bqeh', p, v)
            out = jnp.einsum('bqeh,ehd,bqe->bqd', ctx, o_w, gates)
            return out + jnp.einsum('bqe,ed->bqd', gates, o_b)

        def _moe_ffn(x, gate_w, w1, b1, w2, b2):
            gates = _topk_gates(x @ gate_w, KF)
            h = jax.nn.relu(jnp.einsum('bsd,edh->bseh', x, w1) + b1)
            out = jnp.einsum('bseh,ehd,bse->bsd', h, w2, gates)
            return out + jnp.einsum('bse,ed->bsd', gates, b2)
        key = jax.random.key(seed)
        ks = jax.random.split(key, 12)
        r = lambda i, shape, scale=0.02: jax.random.normal(ks[i], shape, jnp.float32) * scale
        return {'src': jax.random.normal(ks[0], (B, S, D), jnp.float32), 'ln1_w': jnp.ones((D,), jnp.float32), 'ln1_b': jnp.zeros((D,), jnp.float32), 'ln2_w': jnp.ones((D,), jnp.float32), 'ln2_b': jnp.zeros((D,), jnp.float32), 'attn_gate_w': r(1, (D, EA)), 'q_w': r(2, (EA, D, HD)), 'q_b': jnp.zeros((EA, HD), jnp.float32), 'k_w': r(3, (D, HD)), 'k_b': jnp.zeros((HD,), jnp.float32), 'v_w': r(4, (D, HD)), 'v_b': jnp.zeros((HD,), jnp.float32), 'o_w': r(5, (EA, HD, D)), 'o_b': jnp.zeros((EA, D), jnp.float32), 'rel_table': r(6, (2 * MAXP + 1, HD)), 'ff_gate_w': r(7, (D, EF)), 'ff_w1': r(8, (EF, D, FH)), 'ff_b1': jnp.zeros((EF, FH), jnp.float32), 'ff_w2': r(9, (EF, FH, D)), 'ff_b2': jnp.zeros((EF, D), jnp.float32)}
    _L0_ffn_all = _L0_ffn_setup()
    _L0_ffn_in = {k: v for k, v in _L0_ffn_all.items() if k in ('ln1_w', 'ln1_b', 'ln2_w', 'ln2_b', 'attn_gate_w', 'q_w', 'q_b', 'k_w', 'k_b', 'v_w', 'v_b', 'o_w', 'o_b', 'rel_table', 'ff_gate_w', 'ff_w1', 'ff_b1', 'ff_w2', 'ff_b2')}
    del _L0_ffn_all
    return {'x': x, 'txt': txt, 'L0_tok_W1': _L0_tok_in['W1'], 'L0_tok_b1': _L0_tok_in['b1'], 'L0_tok_W2': _L0_tok_in['W2'], 'L0_tok_b2': _L0_tok_in['b2'], 'L0_attn_w_attn': _L0_attn_in['w_attn'], 'L0_attn_w_proj': _L0_attn_in['w_proj'], 'L0_ffn_ln1_w': _L0_ffn_in['ln1_w'], 'L0_ffn_ln1_b': _L0_ffn_in['ln1_b'], 'L0_ffn_ln2_w': _L0_ffn_in['ln2_w'], 'L0_ffn_ln2_b': _L0_ffn_in['ln2_b'], 'L0_ffn_attn_gate_w': _L0_ffn_in['attn_gate_w'], 'L0_ffn_q_w': _L0_ffn_in['q_w'], 'L0_ffn_q_b': _L0_ffn_in['q_b'], 'L0_ffn_k_w': _L0_ffn_in['k_w'], 'L0_ffn_k_b': _L0_ffn_in['k_b'], 'L0_ffn_v_w': _L0_ffn_in['v_w'], 'L0_ffn_v_b': _L0_ffn_in['v_b'], 'L0_ffn_o_w': _L0_ffn_in['o_w'], 'L0_ffn_o_b': _L0_ffn_in['o_b'], 'L0_ffn_rel_table': _L0_ffn_in['rel_table'], 'L0_ffn_ff_gate_w': _L0_ffn_in['ff_gate_w'], 'L0_ffn_ff_w1': _L0_ffn_in['ff_w1'], 'L0_ffn_ff_b1': _L0_ffn_in['ff_b1'], 'L0_ffn_ff_w2': _L0_ffn_in['ff_w2'], 'L0_ffn_ff_b2': _L0_ffn_in['ff_b2']}

def reference(x, txt, L0_tok_W1, L0_tok_b1, L0_tok_W2, L0_tok_b2, L0_attn_w_attn, L0_attn_w_proj, L0_ffn_ln1_w, L0_ffn_ln1_b, L0_ffn_ln2_w, L0_ffn_ln2_b, L0_ffn_attn_gate_w, L0_ffn_q_w, L0_ffn_q_b, L0_ffn_k_w, L0_ffn_k_b, L0_ffn_v_w, L0_ffn_v_b, L0_ffn_o_w, L0_ffn_o_b, L0_ffn_rel_table, L0_ffn_ff_gate_w, L0_ffn_ff_w1, L0_ffn_ff_b1, L0_ffn_ff_w2, L0_ffn_ff_b2):
    import jax
    import jax.numpy as jnp

    def _L0_tok_ref(x, W1, b1, W2, b2):
        import jax, jax.numpy as jnp
        import numpy as np
        P = 16
        C = 3
        D = 256

        def _patchify(x, p):
            B, Cc, H, W = x.shape
            gh, gw = (H // p, W // p)
            x = x.reshape(B, Cc, gh, p, gw, p)
            x = x.transpose(0, 2, 4, 1, 3, 5)
            return x.reshape(B, gh * gw, Cc * p * p)
        patches = _patchify(x, P)
        h = jax.nn.silu(jnp.einsum('blk,kd->bld', patches, W1) + b1)
        return jnp.einsum('bld,de->ble', h, W2) + b2

    def _L0_attn_ref(x, w_attn, w_proj):
        import math
        import jax, jax.numpy as jnp
        import numpy as np
        N_EMBD = 256
        N_HEAD = 16
        HEAD_DIM = N_EMBD // N_HEAD

        def alibi_slopes(n_heads):
            start = 2.0 ** (-2.0 ** (-(math.log2(n_heads) - 3)))
            return np.array([start * start ** i for i in range(n_heads)], dtype=np.float32)
        B, T, C = x.shape
        H, D = (N_HEAD, HEAD_DIM)
        qkv = x @ w_attn.T
        q, k, v = jnp.split(qkv, 3, axis=-1)
        q = q.reshape(B, T, H, D).transpose(0, 2, 1, 3)
        k = k.reshape(B, T, H, D).transpose(0, 2, 1, 3)
        v = v.reshape(B, T, H, D).transpose(0, 2, 1, 3)
        att = jnp.einsum('bhqd,bhkd->bhqk', q, k) * (1.0 / math.sqrt(D))
        pos = jnp.arange(T)
        rel = pos[None, :] - pos[:, None]
        slopes = jnp.asarray(alibi_slopes(H))[:, None, None]
        causal = rel <= 0
        bias = jnp.where(causal, slopes * rel, -jnp.inf)
        att = att + bias[None]
        att = jax.nn.softmax(att, axis=-1)
        y = jnp.einsum('bhqk,bhkd->bhqd', att, v)
        y = y.transpose(0, 2, 1, 3).reshape(B, T, C)
        return y @ w_proj.T

    def _L0_ffn_ref(src, ln1_w, ln1_b, ln2_w, ln2_b, attn_gate_w, q_w, q_b, k_w, k_b, v_w, v_b, o_w, o_b, rel_table, ff_gate_w, ff_w1, ff_b1, ff_w2, ff_b2):
        import jax, jax.numpy as jnp
        import numpy as np
        D = 256
        HD = 128
        EA = 8
        KA = 2
        EF = 16
        KF = 2
        FH = 128
        MAXP = 64
        B, S = (4, 256)
        EPS = 1e-05

        def _layer_norm(x, w, b):
            mu = x.mean(-1, keepdims=True)
            var = ((x - mu) ** 2).mean(-1, keepdims=True)
            return (x - mu) * jax.lax.rsqrt(var + EPS) * w + b

        def _topk_gates(logits, k):
            top_vals, top_idx = jax.lax.top_k(logits, k)
            g = jax.nn.softmax(top_vals, axis=-1)
            onehot = jax.nn.one_hot(top_idx, logits.shape[-1], dtype=logits.dtype)
            return jnp.einsum('...k,...ke->...e', g, onehot)

        def _moa(x, gate_w, q_w, q_b, k_w, k_b, v_w, v_b, o_w, o_b, rel_table):
            S_ = x.shape[1]
            gates = _topk_gates(x @ gate_w, KA)
            q = (jnp.einsum('bsd,edh->bseh', x, q_w) + q_b) * HD ** (-0.5)
            k = x @ k_w + k_b
            v = x @ v_w + v_b
            scores = jnp.einsum('bqeh,bkh->beqk', q, k)
            rel_s = jnp.einsum('bqeh,rh->beqr', q, rel_table)
            pos = jnp.arange(S_)
            rel_idx = jnp.clip(pos[None, :] - pos[:, None], -MAXP, MAXP) + MAXP
            scores = scores + jnp.take_along_axis(rel_s, rel_idx[None, None], axis=-1)
            p = jax.nn.softmax(scores, axis=-1)
            ctx = jnp.einsum('beqk,bkh->bqeh', p, v)
            out = jnp.einsum('bqeh,ehd,bqe->bqd', ctx, o_w, gates)
            return out + jnp.einsum('bqe,ed->bqd', gates, o_b)

        def _moe_ffn(x, gate_w, w1, b1, w2, b2):
            gates = _topk_gates(x @ gate_w, KF)
            h = jax.nn.relu(jnp.einsum('bsd,edh->bseh', x, w1) + b1)
            out = jnp.einsum('bseh,ehd,bse->bsd', h, w2, gates)
            return out + jnp.einsum('bse,ed->bsd', gates, b2)
        res = src
        xn = _layer_norm(src, ln1_w, ln1_b)
        x = res + _moa(xn, attn_gate_w, q_w, q_b, k_w, k_b, v_w, v_b, o_w, o_b, rel_table)
        res = x
        xn = _layer_norm(x, ln2_w, ln2_b)
        return res + _moe_ffn(xn, ff_gate_w, ff_w1, ff_b1, ff_w2, ff_b2)
    h = _L0_tok_ref(x, L0_tok_W1, L0_tok_b1, L0_tok_W2, L0_tok_b2)
    h = jnp.concatenate([h, txt], axis=1)
    h = h + _L0_attn_ref(_layernorm(h, axis=-1), L0_attn_w_attn, L0_attn_w_proj)
    h = h + _L0_ffn_ref(_layernorm(h, axis=-1), L0_ffn_ln1_w, L0_ffn_ln1_b, L0_ffn_ln2_w, L0_ffn_ln2_b, L0_ffn_attn_gate_w, L0_ffn_q_w, L0_ffn_q_b, L0_ffn_k_w, L0_ffn_k_b, L0_ffn_v_w, L0_ffn_v_b, L0_ffn_o_w, L0_ffn_o_b, L0_ffn_rel_table, L0_ffn_ff_gate_w, L0_ffn_ff_w1, L0_ffn_ff_b1, L0_ffn_ff_w2, L0_ffn_ff_b2)
    return h

_drawn_inputs = setup_inputs


def setup_inputs(seed=0):
    import zlib

    import numpy as np

    out = dict(_drawn_inputs(seed))
    spreads = {'L0_ffn_ln1_w': (1.0, 0.569),
     'L0_ffn_ln1_b': (0.0, 0.507),
     'L0_ffn_ln2_w': (1.0, 0.573),
     'L0_ffn_ln2_b': (0.0, 0.458),
     'L0_ffn_q_b': (0.0, 2.0),
     'L0_ffn_k_b': (0.0, 2.0),
     'L0_ffn_v_b': (0.0, 0.644),
     'L0_ffn_o_b': (0.0, 0.1),
     'L0_ffn_ff_b1': (0.0, 0.8),
     'L0_ffn_ff_b2': (0.0, 0.1)}
    factors = {'L0_ffn_q_w': 8.0, 'L0_ffn_k_w': 8.0, 'L0_ffn_rel_table': 52.288}
    for name, (base, spread) in spreads.items():
        noise = np.random.default_rng([zlib.crc32(name.encode()), seed]).standard_normal(out[name].shape)
        drawn = base * np.exp(spread * noise) if base else spread * noise
        out[name] = jnp.asarray(drawn.astype(out[name].dtype))
    for name, factor in factors.items():
        out[name] = (out[name] * factor).astype(out[name].dtype)
    return out
```

```python
from contextlib import ExitStack
from itertools import islice

import concourse.bass as bass
from concourse import mybir

F32 = mybir.dt.float32
BF16 = mybir.dt.bfloat16
ALU = mybir.AluOpType
ACT = mybir.ActivationFunctionType
AX = mybir.AxisListType

NSEQ, NPATCH, NTEXT = 64, 49, 32
T = NPATCH + NTEXT
D = 256
DC = D // 128
PATCH = 3 * 16 * 16
PC = PATCH // 128
NB = 4
G = NSEQ // NB
GT = NB * T
GP = NB * NPATCH
NT = 3
TT = GT // NT
NH, HD1 = 16, 16
HR = NH // 4
EA, HD = 8, 128
MAXP = 64
NREL = 2 * MAXP + 1
RW = 2 * T - 1
KW = T + RW
EF, FH = 16, 128
EPS = 1e-5
BIG = 1e30
UNITS = [("up", 0)] + [u for e in range(1, EF) for u in (("up", e), ("down", e - 1))] + [("down", EF - 1)]


class Signal:

    def __init__(self, handle, per):
        self.sem, self.per = handle, per

    def at(self, g, n):
        return g * self.per + n


def build(nc, A, out):
    ctx = ExitStack()
    with ctx:
        def sb(name, shape, dt=F32):
            return ctx.enter_context(nc.sbuf_tensor(name, shape, dt))

        def bank(name):
            return ctx.enter_context(nc.psum_tensor(name, [128, 512], F32))

        def signal(name, per=1):
            return Signal(ctx.enter_context(nc.semaphore(name)), per)

        tok_w1 = sb("tok_w1", [128, PC, D])
        tok_w2 = sb("tok_w2", [128, DC, D])
        tok_b1 = sb("tok_b1", [128, DC])
        tok_b1h = sb("tok_b1h", [128, DC])
        tok_b2 = sb("tok_b2", [128, DC])
        wqkv = sb("wqkv", [128, DC, 3 * D])
        wproj = sb("wproj", [128, DC, D])
        ln1 = sb("ln1", [128, 2, DC])
        ln2 = sb("ln2", [128, 2, DC])
        moa_gw = sb("moa_gw", [128, DC, EA])
        moa_qw = sb("moa_qw", [128, DC, EA, HD])
        moa_qb = sb("moa_qb", [128, EA])
        moa_kw = sb("moa_kw", [128, DC, HD])
        moa_kb = sb("moa_kb", [128, 1])
        moa_vw = sb("moa_vw", [128, DC, HD])
        moa_vb = sb("moa_vb", [T, HD])
        moa_ow = sb("moa_ow", [128, EA, D])
        moa_ob = sb("moa_ob", [EA, D])
        rel = sb("rel", [128, NREL])
        ff_gw = sb("ff_gw", [128, DC, EF])
        ff_w1 = sb("ff_w1", [128, DC, EF, FH])
        ff_b1 = sb("ff_b1", [128, EF])
        ff_w2 = sb("ff_w2", [128, EF, D])
        ff_b2 = sb("ff_b2", [3 * EF, D])
        ident = sb("ident", [128, 128])
        alibi = sb("alibi", [T, NH * T])
        parity = sb("parity", [128, 2])
        rank = sb("rank", [128, EF])
        sel = sb("sel", [3 * EF, EF, FH], BF16)
        neg_half = sb("neg_half", [TT, NT])

        xT = sb("xT", [128, PC, GP])
        tanh_t = sb("tanh_t", [128, DC, GP])
        pre_t = sb("pre_t", [128, DC, GP])
        h1T = sb("h1T", [128, DC, GP])
        hT = sb("hT", [128, DC, NB, T])
        h_res = sb("h_res", [TT, NT, D])
        pad = sb("pad", [TT, 1])
        stats = sb("stats", [TT, NT, 6])
        meanvar = sb("meanvar", [TT, NT, 2])
        vareps = sb("vareps", [TT, NT])
        rstd = sb("rstd", [TT, NT])
        normed = sb("normed", [TT, NT, D])
        nT = sb("nT", [128, DC, GT])
        qT = sb("qT", [128, DC, 2, GT])
        kT = sb("kT", [128, DC, GT])
        v_aug = sb("v_aug", [T, NB, NH, HD1 + 1])
        s1 = sb("s1", [T, 2, NH, T])
        s1max = sb("s1max", [T, 2, NH])
        p1T = sb("p1T", [T, NH, T])
        y_rec = sb("y_rec", [T, NH])
        y1 = sb("y1", [T, NB, D])
        yT = sb("yT", [128, DC, GT])
        src = sb("src", [TT, NT, D])
        qeT = sb("qeT", [128, EA, GT])
        krel = sb("krel", [128, NB, KW])
        v2 = sb("v2", [T, NB, HD])
        lg = sb("lg", [TT, NT * EF])
        one1 = sb("one1", [TT, NT * EF])
        one2 = sb("one2", [TT, NT * EF])
        tmp = sb("tmp", [TT, NT * EF])
        lg2 = sb("lg2", [TT, NT * EF])
        top1 = sb("top1", [TT, NB])
        top2 = sb("top2", [TT, NB])
        pick = sb("pick", [TT, NB])
        gdiff = sb("gdiff", [TT, NB])
        gexp = sb("gexp", [TT, NB])
        gone = sb("gone", [TT, NB])
        g1 = sb("g1", [TT, NB])
        g2 = sb("g2", [TT, NB])
        gates1 = sb("gates1", [T, NB, EA])
        gates1T = sb("gates1T", [EA, GT])
        sr = sb("sr", [T, 2, EA, KW])
        relb = s1[:, 1].rearrange("p (s e) t -> p s e t", s=2)
        s2 = s1[:, 0].rearrange("p (s e) t -> p s e t", s=2)
        s2max = sb("s2max", [T, 2, EA])
        s2sum = sb("s2sum", [T, 2, EA])
        s2rec = sb("s2rec", [T, 2, EA])
        s2fac = sb("s2fac", [T, 2, EA])
        p2T = p1T[:, 0:EA, :]
        ctxT = sb("ctxT", [128, EA, GT])
        moa_x = sb("moa_x", [TT, NT, D])
        gates2 = sb("gates2", [TT, NT, EF])
        ghi = sb("ghi", [TT, NT, EF], BF16)
        gmid = sb("gmid", [TT, NT, EF], BF16)
        gparts = sb("gparts", [TT, NT, 3, EF])
        sel32 = ctxT[0:3 * EF].rearrange("p e t -> p (e t)")[:, 0:EF * FH]
        base = sb("base", [TT, NT, D])
        xn2T = sb("xn2T", [128, DC, GT])
        g2T = sb("g2T", [3 * EF, GT])
        g2Tb = sb("g2Tb", [3 * EF, GT], BF16)
        relu_t = sb("relu_t", [128, 2, GT])
        hid = sb("hid", [128, 2, GT])
        moeT = sb("moeT", [128, DC, GT])
        out_t = sb("out_t", [TT, NT, D])

        pa = [bank(f"pa{i}") for i in range(4)]
        p_up = bank("p_up")
        p_gate = bank("p_gate")
        p_acc = [bank(f"p_acc{i}") for i in range(2)]

        rel_dram = nc.dram_tensor("rel_scratch", [NB, T, EA, RW], F32, kind="Internal")

        w_early = signal("w_early")
        w_late = signal("w_late")
        const_done = signal("const_done")
        pool_const = signal("pool_const")
        x_in = signal("x_in", 16)
        txt_in = signal("txt_in", 16 * DC)
        rel_out = signal("rel_out", 16 * NB)
        relb_in = [signal(f"relb_in{i}", 16 * NB // 2) for i in range(2)]
        out_free = signal("out_free", 16)
        u_ps = signal("u_ps", DC)
        emb_ps = signal("emb_ps", DC)
        htok_ps = signal("htok_ps", 2)
        nT_ps = signal("nT_ps", 2)
        qk_ps = signal("qk_ps", 4)
        v_ps = signal("v_ps", NB)
        s1_ps = signal("s1_ps", NB)
        p1T_ps = signal("p1T_ps", 3 * NB)
        y1_ps = signal("y1_ps", NB)
        yT_ps = signal("yT_ps", DC)
        proj_ps = signal("proj_ps", 2)
        xnT_ps = signal("xnT_ps", 2)
        qe_ps = signal("qe_ps", EA)
        k2_ps = signal("k2_ps")
        v2_ps = signal("v2_ps")
        lg1_ps = signal("lg1_ps")
        g1T_ps = signal("g1T_ps")
        sr_ps = signal("sr_ps", 4 * NB)
        p2T_ps = signal("p2T_ps", 2 * NB)
        ctx_ps = signal("ctx_ps", 2 * NB)
        moa_ps = signal("moa_ps", 2)
        xn2T_ps = signal("xn2T_ps", 2)
        lg2_ps = signal("lg2_ps")
        g2T_ps = signal("g2T_ps")
        up_ps = signal("up_ps", EF)
        acc_ps = signal("acc_ps", DC)
        out_ps = signal("out_ps", 2)
        u_act = signal("u_act", DC)
        hT_act = signal("hT_act", DC)
        nT_act = signal("nT_act", 2)
        k_act = signal("k_act", 2)
        v_act = signal("v_act", NB)
        s1_exp = signal("s1_exp", NB)
        p1T_act = signal("p1T_act", 3 * NB)
        yT_act = signal("yT_act", DC)
        xnT_act = signal("xnT_act", 2)
        qe_act = signal("qe_act", EA)
        k2_act = signal("k2_act")
        g1T_act = signal("g1T_act")
        gexp_act = signal("gexp_act", 2)
        sr_act = signal("sr_act", 2 * NB)
        s2_exp = signal("s2_exp", NB)
        p2T_act = signal("p2T_act", 2 * NB)
        ctx_act = signal("ctx_act", NB)
        xn2T_act = signal("xn2T_act", 2)
        g2T_act = signal("g2T_act")
        relu_act = signal("relu_act", EF)
        acc_act = signal("acc_act", DC)
        a_step = signal("a_step", 0)
        h1_dve = signal("h1_dve", DC)
        hres_dve = signal("hres_dve", 2)
        var_dve = signal("var_dve", 4)
        norm_dve = signal("norm_dve", 3)
        q_dve = signal("q_dve", 2)
        s1_max = signal("s1_max", NB)
        s1_add = signal("s1_add", NB)
        y1_dve = signal("y1_dve", NB)
        res_dve = signal("res_dve", 2)
        v2_dve = signal("v2_dve")
        lg_dve = signal("lg_dve", 2)
        gdiff_dve = signal("gdiff_dve", 2)
        gates1_dve = signal("gates1_dve")
        sr_dve = signal("sr_dve", 2 * NB)
        s2_max = signal("s2_max", NB)
        s2_fac = signal("s2_fac", NB)
        ctx_dve = signal("ctx_dve", NB)
        moa_dve = signal("moa_dve", 2)
        gparts_dve = signal("gparts_dve")
        hid_dve = signal("hid_dve", EF)
        out_dve = signal("out_dve", 2)
        rstd_pool = signal("rstd_pool", 4)
        s1_sub = signal("s1_sub", NB)
        s2_add = signal("s2_add", NB)
        s2_sub = signal("s2_sub", NB)
        p2_pool = signal("p2_pool", NB)

        EARLY = [(tok_w1, "tok_w1"), (tok_w2, "tok_w2"), (tok_b1, "tok_b1"), (tok_b2, "tok_b2"), (ident, "ident"),
                 (wqkv, "wqkv"), (parity, "parity"), (alibi, "alibi"), (wproj, "wproj")]
        LATE = [(ln1, "ln1"), (ln2, "ln2"), (moa_gw, "moa_gw"), (moa_qw, "moa_qw"), (moa_qb, "moa_qb"),
                (moa_kw, "moa_kw"), (moa_kb, "moa_kb"), (moa_vw, "moa_vw"), (moa_ow, "moa_ow"),
                (moa_ob, "moa_ob"), (rel, "rel"), (rank, "rank"), (ff_gw, "ff_gw"), (ff_w1, "ff_w1"),
                (ff_b1, "ff_b1"), (ff_w2, "ff_w2"), (sel32, "sel32")]
        W_EARLY, W_LATE = 16 * len(EARLY), 16 * (len(LATE) + 4)

        def loop(engine, body):
            body(0, True, False)
            with engine.Fori(1, G) as g:
                body(g, True, True)
            body(G, False, True)

        block = ctx.enter_context(nc.Block())

        @block.sync
        def _(sp):
            sp.sem_inc(out_free.sem, 16)
            for t, name in EARLY[:1]:
                sp.dma_start(t[:], A[name]).then_inc(w_early.sem, 16)
            sp.dma_start(xT[:, :, :], A["x"][0]).then_inc(x_in.sem, 16)
            for t, name in EARLY[1:]:
                sp.dma_start(t[:], A[name]).then_inc(w_early.sem, 16)
            sp.dma_start(hT[:, 0, :, NPATCH:T], A["txt"][0, :, 0]).then_inc(txt_in.sem, 16)
            sp.dma_start(hT[:, 1, :, NPATCH:T], A["txt"][0, :, 1]).then_inc(txt_in.sem, 16)
            for t, name in LATE:
                sp.dma_start(t[:], A[name]).then_inc(w_late.sem, 16)
            sp.dma_start(moa_vb[:, :], A["moa_vb"].broadcast_to((T, HD))).then_inc(w_late.sem, 16)
            for i in range(3):
                sp.dma_start(ff_b2[i * EF:(i + 1) * EF, :], A["ff_b2"]).then_inc(w_late.sem, 16)

            def body(g, do_a, do_b):
                if not do_a:
                    return
                if do_b:
                    sp.wait_ge(u_ps.sem, u_ps.at(g - 1, DC))
                    sp.dma_start(xT[:, :, :], A["x"][g]).then_inc(x_in.sem, 16)
                    sp.wait_ge(htok_ps.sem, htok_ps.at(g - 1, 2))
                    for c in range(DC):
                        sp.dma_start(hT[:, c, :, NPATCH:T], A["txt"][g, :, c]).then_inc(txt_in.sem, 16)
                for b in range(NB):
                    sp.wait_ge(sr_act.sem, sr_act.at(g, 2 * b + 2))
                    sp.wait_ge(sr_dve.sem, sr_dve.at(g, 2 * b + 2))
                    sp.dma_start(rel_dram.ap()[b], sr[:, b % 2, :, T:KW]).then_inc(rel_out.sem, 16)
                    sp.wait_ge(rel_out.sem, rel_out.at(g, 16 * (b + 1)))
                    skewed = bass.AP(tensor=rel_dram, offset=b * T * EA * RW + T - 1,
                                     ap=[[EA * RW - 1, T], [RW, EA], [1, T]])
                    sp.dma_start(relb[:, b % 2], skewed).then_inc(relb_in[b % 2].sem, 16)

            loop(sp, body)
            sp.wait_ge(out_free.sem, 16 * (G + 1))
            sp.wait_ge(rel_out.sem, 16 * NB * G)

        @block.tensor
        def _(pe):
            mm = nc.tensor.matmul

            def transpose_tiles(source, rows):
                for m in range(DC):
                    for t in range(NT):
                        last = nc.tensor.transpose(pa[rows + m][:, t * TT:(t + 1) * TT],
                                                   source[:, t, m * 128:(m + 1) * 128], ident[0:TT, 0:TT])
                    yield last

            def body(g, do_a, do_b):
                left = iter(UNITS if do_b else [])
                gb = g - 1

                def fill(n):
                    for kind, e in islice(left, n):
                        if kind == "up":
                            if e == 0:
                                pe.wait_ge(xn2T_act.sem, xn2T_act.at(gb, 2))
                                pe.wait_ge(g2T_act.sem, g2T_act.at(gb, 1))
                            if e:
                                pe.wait_ge(hid_dve.sem, hid_dve.at(gb, e))
                            mm(p_gate[:, 0:GT], sel[:, e, :], g2Tb[:, :], start=True, stop=True)
                            if e:
                                pe.wait_ge(relu_act.sem, relu_act.at(gb, e))
                            for c in range(DC):
                                last = mm(p_up[:, 0:GT], ff_w1[:, c, e, :], xn2T[:, c, :],
                                          start=(c == 0), stop=(c == DC - 1))
                            last.then_inc(up_ps.sem, 1)
                        else:
                            pe.wait_ge(hid_dve.sem, hid_dve.at(gb, e + 1))
                            for m in range(DC):
                                mm(p_acc[m][:, 0:GT], ff_w2[:, e, m * 128:(m + 1) * 128], hid[:, e % 2, :],
                                   start=(e == 0), stop=False)
                            if e == EF - 1:
                                for m in range(DC):
                                    mm(p_acc[m][:, 0:GT], ff_b2[:, m * 128:(m + 1) * 128], g2T[:, :],
                                       start=False, stop=True).then_inc(acc_ps.sem, 1)

                def b_end():
                    if not do_b:
                        return
                    pe.wait_ge(acc_act.sem, acc_act.at(gb, DC))
                    for t in range(NT):
                        dst = (p_up, p_up, p_gate)[t][0:TT, (t % 2) * D:(t % 2 + 1) * D]
                        for m in range(DC):
                            last = nc.tensor.transpose(dst[:, m * 128:(m + 1) * 128],
                                                       moeT[:, m, t * TT:(t + 1) * TT], ident[:, :])
                        if t:
                            last.then_inc(out_ps.sem, 1)

                if not do_a:
                    fill(2 * EF)
                    b_end()
                    return

                pe.wait_ge(x_in.sem, x_in.at(g, 16))
                if not do_b:
                    pe.wait_ge(w_early.sem, W_EARLY)
                if do_b:
                    pe.wait_ge(g2T_act.sem, g2T_act.at(g - 1, 1))
                for m in range(DC):
                    for c in range(PC):
                        last = mm(pa[m][:, 0:GP], tok_w1[:, c, m * 128:(m + 1) * 128], xT[:, c, :],
                                  start=(c == 0), stop=(c == PC - 1))
                    last.then_inc(u_ps.sem, 1)
                fill(1)
                for m in range(DC):
                    if m == 0:
                        pe.wait_ge(h1_dve.sem, h1_dve.at(g, DC))
                    for c in range(DC):
                        last = mm(pa[2 + m][:, 0:GP], tok_w2[:, c, m * 128:(m + 1) * 128], h1T[:, c, :],
                                  start=(c == 0), stop=(c == DC - 1))
                    last.then_inc(emb_ps.sem, 1)
                fill(1)
                pe.wait_ge(txt_in.sem, txt_in.at(g, 16 * DC))
                pe.wait_ge(hT_act.sem, hT_act.at(g, DC))
                flat = hT[:, :, :, :].rearrange("p c b t -> p c (b t)")
                for t in range(NT):
                    for m in range(DC):
                        last = nc.tensor.transpose(pa[t // 2][0:TT, (t % 2) * D + m * 128:(t % 2) * D + (m + 1) * 128],
                                                   flat[:, m, t * TT:(t + 1) * TT], ident[:, :])
                    if t:
                        last.then_inc(htok_ps.sem, 1)
                fill(3)
                pe.wait_ge(norm_dve.sem, norm_dve.at(g, 1))
                for last in transpose_tiles(normed, 2):
                    last.then_inc(nT_ps.sem, 1)
                fill(1)
                pe.wait_ge(nT_act.sem, nT_act.at(g, 2))
                for i in range(4):
                    for c in range(DC):
                        last = mm(pa[i][:, 0:GT], wqkv[:, c, i * 128:(i + 1) * 128], nT[:, c, :],
                                  start=(c == 0), stop=(c == DC - 1))
                    last.then_inc(qk_ps.sem, 1)
                for b in range(NB):
                    if b < 2:
                        pe.wait_ge(q_dve.sem, q_dve.at(g, b + 1))
                    else:
                        pe.wait_ge(k_act.sem, k_act.at(g, b - 1))
                    for c in range(DC):
                        last = mm(pa[b][0:T, 0:D], nT[:, c, b * T:(b + 1) * T], wqkv[:, c, 2 * D:3 * D],
                                  start=(c == 0), stop=(c == DC - 1))
                    last.then_inc(v_ps.sem, 1)

                def s1_scores(b):
                    if b == 0:
                        pe.wait_ge(v_act.sem, v_act.at(g, NB))
                    else:
                        pe.wait_ge(s1_add.sem, s1_add.at(g, b))
                        if b >= 2:
                            pe.wait_ge(y1_dve.sem, y1_dve.at(g, b - 1))
                    for i in range(HR):
                        for r in range(4):
                            c, par = i // 2, i % 2
                            rows = slice(32 * r, 32 * r + 32)
                            last = mm(pa[r][0:T, i * T:(i + 1) * T], qT[rows, c, par, b * T:(b + 1) * T],
                                      kT[rows, c, b * T:(b + 1) * T], start=True, stop=True,
                                      tile_position=(32 * r, 0))
                    last.then_inc(s1_ps.sem, 1)

                def p1_transposes(b):
                    pe.wait_ge(s1_exp.sem, s1_exp.at(g, b + 1))
                    if b + 1 < NB:
                        pe.wait_ge(s1_add.sem, s1_add.at(g, b + 2))
                    else:
                        pe.wait_ge(p1T_act.sem, p1T_act.at(g, 3 * b))
                    for j in range(NH):
                        last = nc.tensor.transpose(pa[j // 6][0:T, (j % 6) * T:(j % 6 + 1) * T],
                                                   s1[:, b % 2, j, :], ident[0:T, 0:T])
                        if j in (5, 11, NH - 1):
                            last.then_inc(p1T_ps.sem, 1)

                def y1_product(b):
                    for j in range(NH):
                        if j % 6 == 0:
                            pe.wait_ge(p1T_act.sem, p1T_act.at(g, 3 * b + j // 6 + 1))
                            if j == 0 and b == NB - 1:
                                pe.wait_ge(y1_dve.sem, y1_dve.at(g, b))
                        r, c, par = j // HR, (j % HR) // 2, j % 2
                        head = c * 8 + 2 * r + par
                        last = mm(pa[3][0:T, head * (HD1 + 1):(head + 1) * (HD1 + 1)], p1T[:, j, :],
                                  v_aug[:, b, head, :], start=True, stop=True)
                    last.then_inc(y1_ps.sem, 1)

                s1_scores(0)
                fill(1)
                s1_scores(1)
                fill(1)
                for b in range(NB):
                    p1_transposes(b)
                    fill(1)
                    y1_product(b)
                    if b + 2 < NB:
                        s1_scores(b + 2)
                        fill(1)
                fill(1)
                pe.wait_ge(y1_dve.sem, y1_dve.at(g, NB))
                for m in range(DC):
                    for b in range(NB):
                        last = nc.tensor.transpose(pa[m][:, b * T:(b + 1) * T], y1[:, b, m * 128:(m + 1) * 128],
                                                   ident[0:T, 0:T])
                    last.then_inc(yT_ps.sem, 1)
                fill(1)
                pe.wait_ge(yT_act.sem, yT_act.at(g, DC))
                for t in range(NT):
                    for c in range(DC):
                        last = mm(pa[2 + t // 2][0:TT, (t % 2) * D:(t % 2 + 1) * D], yT[:, c, t * TT:(t + 1) * TT],
                                  wproj[:, c, :], start=(c == 0), stop=(c == DC - 1))
                    if t:
                        last.then_inc(proj_ps.sem, 1)
                fill(5)
                pe.wait_ge(norm_dve.sem, norm_dve.at(g, 2))
                for last in transpose_tiles(normed, 0):
                    last.then_inc(xnT_ps.sem, 1)
                fill(1)
                pe.wait_ge(xnT_act.sem, xnT_act.at(g, 2))
                if not do_b:
                    pe.wait_ge(w_late.sem, W_LATE)
                    pe.wait_ge(const_done.sem, 2)
                for b in range(NB):
                    for c in range(DC):
                        last = mm(pa[0][0:T, b * EA:(b + 1) * EA], nT[:, c, b * T:(b + 1) * T], moa_gw[:, c, :],
                                  start=(c == 0), stop=(c == DC - 1))
                last.then_inc(lg1_ps.sem, 1)
                for c in range(DC):
                    last = mm(pa[1][:, 0:GT], moa_kw[:, c, :], nT[:, c, :], start=(c == 0), stop=(c == DC - 1))
                last.then_inc(k2_ps.sem, 1)
                for b in range(NB):
                    for c in range(DC):
                        last = mm(pa[2][0:T, b * HD:(b + 1) * HD], nT[:, c, b * T:(b + 1) * T], moa_vw[:, c, :],
                                  start=(c == 0), stop=(c == DC - 1))
                last.then_inc(v2_ps.sem, 1)
                for e in range(EA):
                    i = (e + 3) % 4
                    if e == 1:
                        pe.wait_ge(lg_dve.sem, lg_dve.at(g, 1))
                    elif e == 2:
                        pe.wait_ge(k2_act.sem, k2_act.at(g, 1))
                    elif e == 3:
                        pe.wait_ge(v2_dve.sem, v2_dve.at(g, 1))
                    elif e >= 4:
                        pe.wait_ge(qe_act.sem, qe_act.at(g, e - 3))
                    for c in range(DC):
                        last = mm(pa[i][:, 0:GT], moa_qw[:, c, e, :], nT[:, c, :], start=(c == 0), stop=(c == DC - 1))
                    last.then_inc(qe_ps.sem, 1)

                def s2_scores(b):
                    for e in range(EA):
                        i = e // 2
                        if e % 2 == 0:
                            if b == 0:
                                pe.wait_ge(qe_act.sem, qe_act.at(g, EA))
                            elif i < 2:
                                pe.wait_ge(sr_act.sem, sr_act.at(g, 2 * (b - 1) + i + 1))
                                if b >= 2:
                                    pe.wait_ge(p2T_act.sem, p2T_act.at(g, 2 * (b - 2) + i + 1))
                            else:
                                pe.wait_ge(sr_dve.sem, sr_dve.at(g, 2 * (b - 1) + i - 1))
                                if b >= 2 and i == 2:
                                    pe.wait_ge(ctx_act.sem, ctx_act.at(g, b - 1))
                                elif b >= 2:
                                    pe.wait_ge(ctx_dve.sem, ctx_dve.at(g, b - 1))
                        last = mm(pa[i][0:T, (e % 2) * KW:(e % 2 + 1) * KW], qeT[:, e, b * T:(b + 1) * T],
                                  krel[:, b, :], start=True, stop=True)
                        if e % 2:
                            last.then_inc(sr_ps.sem, 1)

                def p2_transposes(b):
                    pe.wait_ge(p2_pool.sem, p2_pool.at(g, b + 1))
                    for i in range(2):
                        if b + 1 < NB:
                            pe.wait_ge(sr_act.sem, sr_act.at(g, 2 * (b + 1) + i + 1))
                        else:
                            pe.wait_ge(p2T_act.sem, p2T_act.at(g, 2 * (b - 1) + i + 1))
                        for j in range(4):
                            last = nc.tensor.transpose(pa[i][0:T, j * T:(j + 1) * T], s2[:, b % 2, 4 * i + j, :],
                                                       ident[0:T, 0:T])
                        last.then_inc(p2T_ps.sem, 1)

                def ctx_product(b):
                    for i in range(2):
                        pe.wait_ge(p2T_act.sem, p2T_act.at(g, 2 * b + i + 1))
                        if b + 1 < NB:
                            pe.wait_ge(sr_dve.sem, sr_dve.at(g, 2 * (b + 1) + i + 1))
                        elif i == 0:
                            pe.wait_ge(ctx_act.sem, ctx_act.at(g, b))
                        else:
                            pe.wait_ge(ctx_dve.sem, ctx_dve.at(g, b))
                        mm(pa[2 + i][:, 0:4 * T], v2[:, b, :],
                           p2T[:, 4 * i:4 * i + 4, :].rearrange("p e t -> p (e t)"),
                           start=True, stop=True).then_inc(ctx_ps.sem, 1)

                s2_scores(0)
                fill(1)
                s2_scores(1)
                fill(1)
                for b in range(NB):
                    fill(1)
                    p2_transposes(b)
                    fill(1)
                    ctx_product(b)
                    if b + 2 < NB:
                        s2_scores(b + 2)
                fill(2 * EF)
                pe.wait_ge(gates1_dve.sem, gates1_dve.at(g, 1))
                pe.wait_ge(p2T_act.sem, p2T_act.at(g, 2 * NB))
                for b in range(NB):
                    last = mm(pa[1][0:EA, b * T:(b + 1) * T], gates1[:, b, :], ident[0:T, 0:T], start=True, stop=True)
                last.then_inc(g1T_ps.sem, 1)
                pe.wait_ge(ctx_act.sem, ctx_act.at(g, NB))
                pe.wait_ge(ctx_dve.sem, ctx_dve.at(g, NB))
                pe.wait_ge(g1T_act.sem, g1T_act.at(g, 1))
                for t in range(NT):
                    dst = pa[2 + t // 2][0:TT, (t % 2) * D:(t % 2 + 1) * D]
                    for e in range(EA):
                        mm(dst, ctxT[:, e, t * TT:(t + 1) * TT], moa_ow[:, e, :], start=(e == 0), stop=False)
                    last = mm(dst, gates1T[:, t * TT:(t + 1) * TT], moa_ob[:, :], start=False, stop=True)
                    if t:
                        last.then_inc(moa_ps.sem, 1)
                b_end()
                pe.wait_ge(norm_dve.sem, norm_dve.at(g, 3))
                for last in transpose_tiles(normed, 0):
                    last.then_inc(xn2T_ps.sem, 1)
                pe.wait_ge(xn2T_act.sem, xn2T_act.at(g, 2))
                for t in range(NT):
                    for c in range(DC):
                        last = mm(pa[2][0:TT, t * EF:(t + 1) * EF], xn2T[:, c, t * TT:(t + 1) * TT], ff_gw[:, c, :],
                                  start=(c == 0), stop=(c == DC - 1))
                last.then_inc(lg2_ps.sem, 1)
                pe.wait_ge(gparts_dve.sem, gparts_dve.at(g, 1))
                for t in range(NT):
                    last = mm(pa[3][0:3 * EF, t * TT:(t + 1) * TT], gparts[:, t].rearrange("p k e -> p (k e)"),
                              ident[0:TT, 0:TT], start=True, stop=True)
                last.then_inc(g2T_ps.sem, 1)

            loop(pe, body)

        @block.scalar
        def _(act):
            A_ = nc.scalar.activation

            def body(g, do_a, do_b):
                left = iter(UNITS if do_b else [])
                gb = g - 1

                def fill(n):
                    for kind, e in islice(left, n):
                        if kind == "up":
                            act.wait_ge(up_ps.sem, up_ps.at(gb, e + 1))
                            A_(relu_t[:, e % 2, :], p_up[:, 0:GT], ACT.Relu, bias=ff_b1[:, e:e + 1]).then_inc(relu_act.sem, 1)

                def b_end():
                    if do_b:
                        for m in range(DC):
                            act.wait_ge(acc_ps.sem, acc_ps.at(gb, m + 1))
                            A_(moeT[:, m, :], p_acc[m][:, 0:GT], ACT.Copy).then_inc(acc_act.sem, 1)

                def store():
                    if do_b:
                        act.wait_ge(out_dve.sem, out_dve.at(gb, 2))
                        act.dma_start(out[gb], out_t[:, :, :]).then_inc(out_free.sem, 16)

                if not do_a:
                    fill(2 * EF)
                    b_end()
                    store()
                    return

                if not do_b:
                    act.wait_ge(const_done.sem, 1)
                for m in range(DC):
                    act.wait_ge(u_ps.sem, u_ps.at(g, m + 1))
                    A_(tanh_t[:, m, :], pa[m][:, 0:GP], ACT.Tanh, bias=tok_b1h[:, m:m + 1], scale=0.5)
                    A_(pre_t[:, m, :], pa[m][:, 0:GP], ACT.Identity, bias=tok_b1[:, m:m + 1]).then_inc(u_act.sem, 1)
                fill(1)
                for m in range(DC):
                    act.wait_ge(emb_ps.sem, emb_ps.at(g, m + 1))
                    A_(hT[:, m, :, 0:NPATCH], pa[2 + m][:, 0:GP].rearrange("p (b t) -> p b t", b=NB), ACT.Identity,
                       bias=tok_b2[:, m:m + 1], scale=0.5).then_inc(hT_act.sem, 1)
                fill(1)
                fill(3)
                for m in range(DC):
                    act.wait_ge(nT_ps.sem, nT_ps.at(g, m + 1))
                    A_(nT[:, m, :], pa[2 + m][:, 0:GT], ACT.Copy).then_inc(nT_act.sem, 1)
                fill(1)
                for m in range(DC):
                    act.wait_ge(qk_ps.sem, qk_ps.at(g, 3 + m))
                    A_(kT[:, m, :], pa[2 + m][:, 0:GT], ACT.Copy).then_inc(k_act.sem, 1)
                for b in range(NB):
                    act.wait_ge(v_ps.sem, v_ps.at(g, b + 1))
                    A_(v_aug[:, b, :, 0:HD1], pa[b][0:T, 0:D].rearrange("p (h d) -> p h d", h=NH), ACT.Copy).then_inc(v_act.sem, 1)

                def s1_soft(b):
                    act.wait_ge(s1_sub.sem, s1_sub.at(g, b + 1))
                    A_(s1[:, b % 2], s1[:, b % 2], ACT.Exp).then_inc(s1_exp.sem, 1)

                def p1_out(b):
                    for i in range(3):
                        act.wait_ge(p1T_ps.sem, p1T_ps.at(g, 3 * b + i + 1))
                        n = (6, 6, NH - 12)[i]
                        A_(p1T[:, 6 * i:6 * i + n, :], pa[i][0:T, 0:n * T].rearrange("p (h t) -> p h t", h=n),
                           ACT.Copy).then_inc(p1T_act.sem, 1)

                fill(1)
                fill(1)
                s1_soft(0)
                for b in range(NB):
                    p1_out(b)
                    fill(1)
                    if b + 1 < NB:
                        s1_soft(b + 1)
                    if b + 2 < NB:
                        fill(1)
                fill(1)
                for m in range(DC):
                    act.wait_ge(yT_ps.sem, yT_ps.at(g, m + 1))
                    A_(yT[:, m, :], pa[m][:, 0:GT], ACT.Copy).then_inc(yT_act.sem, 1)
                fill(1)
                fill(5)
                for m in range(DC):
                    act.wait_ge(xnT_ps.sem, xnT_ps.at(g, m + 1))
                    if not do_b:
                        act.wait_ge(w_late.sem, W_LATE)
                    A_(nT[:, m, :], pa[m][:, 0:GT], ACT.Identity, scale=ln1[:, 0, m:m + 1],
                       bias=ln1[:, 1, m:m + 1]).then_inc(xnT_act.sem, 1)
                fill(1)
                act.wait_ge(k2_ps.sem, k2_ps.at(g, 1))
                A_(krel[:, :, 0:T], pa[1][:, 0:GT].rearrange("p (b t) -> p b t", b=NB), ACT.Identity,
                   bias=moa_kb[:, 0:1]).then_inc(k2_act.sem, 1)
                for e in range(EA):
                    act.wait_ge(qe_ps.sem, qe_ps.at(g, e + 1))
                    A_(qeT[:, e, :], pa[(e + 3) % 4][:, 0:GT], ACT.Identity, scale=HD ** -0.5,
                       bias=moa_qb[:, e:e + 1]).then_inc(qe_act.sem, 1)

                def s2_out(b):
                    for i in range(2):
                        act.wait_ge(sr_ps.sem, sr_ps.at(g, 4 * b + i + 1))
                        if i == 0 and (b >= 2 or do_b):
                            act.wait_ge(rel_out.sem, rel_out.at(g, 16 * (b - 1)))
                            act.wait_ge(s2_add.sem, s2_add.at(g, b - 1))
                        A_(sr[:, b % 2, 2 * i:2 * i + 2, :],
                           pa[i][0:T, 0:2 * KW].rearrange("p (e k) -> p e k", e=2), ACT.Copy).then_inc(sr_act.sem, 1)

                def s2_soft(b):
                    act.wait_ge(s2_sub.sem, s2_sub.at(g, b + 1))
                    A_(s2[:, b % 2], s2[:, b % 2], ACT.Exp).then_inc(s2_exp.sem, 1)

                def p2_out(b):
                    for i in range(2):
                        act.wait_ge(p2T_ps.sem, p2T_ps.at(g, 2 * b + i + 1))
                        A_(p2T[:, 4 * i:4 * i + 4, :], pa[i][0:T, 0:4 * T].rearrange("p (e t) -> p e t", e=4),
                           ACT.Copy).then_inc(p2T_act.sem, 1)

                def ctx_out(b):
                    act.wait_ge(ctx_ps.sem, ctx_ps.at(g, 2 * b + 1))
                    A_(ctxT[:, 0:4, b * T:(b + 1) * T], pa[2][:, 0:4 * T].rearrange("p (e t) -> p e t", e=4),
                       ACT.Copy).then_inc(ctx_act.sem, 1)

                s2_out(0)
                act.wait_ge(gdiff_dve.sem, gdiff_dve.at(g, 1))
                A_(gexp[0:T, 0:NB], gdiff[0:T, 0:NB], ACT.Exp).then_inc(gexp_act.sem, 1)
                fill(1)
                s2_out(1)
                fill(1)
                s2_soft(0)
                for b in range(NB):
                    fill(1)
                    p2_out(b)
                    fill(1)
                    ctx_out(b)
                    if b + 2 < NB:
                        s2_out(b + 2)
                    if b + 1 < NB:
                        s2_soft(b + 1)
                fill(2 * EF)
                act.wait_ge(g1T_ps.sem, g1T_ps.at(g, 1))
                A_(gates1T[:, :], pa[1][0:EA, 0:GT], ACT.Copy).then_inc(g1T_act.sem, 1)
                b_end()
                for m in range(DC):
                    act.wait_ge(xn2T_ps.sem, xn2T_ps.at(g, m + 1))
                    A_(xn2T[:, m, :], pa[m][:, 0:GT], ACT.Identity, scale=ln2[:, 0, m:m + 1],
                       bias=ln2[:, 1, m:m + 1]).then_inc(xn2T_act.sem, 1)
                store()
                act.wait_ge(gdiff_dve.sem, gdiff_dve.at(g, 2))
                A_(gexp[:, 0:NT], gdiff[:, 0:NT], ACT.Exp).then_inc(gexp_act.sem, 1)
                act.wait_ge(g2T_ps.sem, g2T_ps.at(g, 1))
                A_(g2T[:, :], pa[3][0:3 * EF, 0:GT], ACT.Copy)
                A_(g2Tb[:, :], pa[3][0:3 * EF, 0:GT], ACT.Copy).then_inc(g2T_act.sem, 1)

            loop(act, body)

        @block.gpsimd
        def _(pool):
            nc.gpsimd.memset(neg_half[:, :], -0.5).then_inc(pool_const.sem, 1)
            nc.gpsimd.memset(v_aug[:, :, :, HD1:HD1 + 1], 1.0).then_inc(pool_const.sem, 1)

            def body(g, do_a, do_b):
                if not do_a:
                    return
                if not do_b:
                    pool.wait_ge(pool_const.sem, 2)

                def power(n):
                    pool.wait_ge(var_dve.sem, var_dve.at(g, n))
                    nc.gpsimd.tensor_tensor(rstd[:, :], vareps[:, :], neg_half[:, :], ALU.pow).then_inc(rstd_pool.sem, 1)

                power(1)
                for b in range(NB):
                    pool.wait_ge(s1_max.sem, s1_max.at(g, b + 1))
                    nc.gpsimd.tensor_tensor(s1[:, b % 2], s1[:, b % 2],
                                            s1max[:, b % 2].unsqueeze(2).broadcast_to((T, NH, T)),
                                            ALU.subtract).then_inc(s1_sub.sem, 1)
                power(2)
                power(3)

                def s2_sum(b):
                    pool.wait_ge(relb_in[b % 2].sem, relb_in[b % 2].at(g, 16 * (b // 2 + 1)))
                    if b >= 2 or do_b:
                        pool.wait_ge(p2T_ps.sem, p2T_ps.at(g, 2 * (b - 1)))
                    nc.gpsimd.tensor_tensor(s2[:, b % 2], sr[:, b % 2, :, 0:T], relb[:, b % 2],
                                            ALU.add).then_inc(s2_add.sem, 1)

                def s2_less_max(b):
                    pool.wait_ge(s2_max.sem, s2_max.at(g, b + 1))
                    nc.gpsimd.tensor_tensor(s2[:, b % 2], s2[:, b % 2],
                                            s2max[:, b % 2].unsqueeze(2).broadcast_to((T, EA, T)),
                                            ALU.subtract).then_inc(s2_sub.sem, 1)

                def p2_scale(b):
                    pool.wait_ge(s2_fac.sem, s2_fac.at(g, b + 1))
                    nc.gpsimd.tensor_tensor(s2[:, b % 2], s2[:, b % 2],
                                            s2fac[:, b % 2].unsqueeze(2).broadcast_to((T, EA, T)),
                                            ALU.mult).then_inc(p2_pool.sem, 1)

                s2_sum(0)
                s2_less_max(0)
                for b in range(NB):
                    if b + 1 < NB:
                        if b == 0:
                            s2_sum(1)
                    p2_scale(b)
                    if b + 1 < NB:
                        s2_less_max(b + 1)
                    if b + 2 < NB:
                        s2_sum(b + 2)
                power(4)

            loop(pool, body)

        @block.vector
        def _(dve):
            V = nc.vector

            dve.wait_ge(w_early.sem, W_EARLY)
            V.tensor_scalar(tok_b1h[:, :], tok_b1[:, :], 0.5, None, ALU.mult).then_inc(const_done.sem, 1)

            A_STEPS = count_steps
            steps = [0]

            def body(g, do_a, do_b):
                left = iter(UNITS if do_b else [])
                gb = g - 1
                steps[0] = 0

                def step(ins):
                    steps[0] += 1
                    ins.then_inc(a_step.sem, 1)
                    dve.wait_ge(a_step.sem, g * A_STEPS + steps[0])

                def fill(n):
                    for kind, e in islice(left, n):
                        if kind == "up":
                            dve.wait_ge(relu_act.sem, relu_act.at(gb, e + 1))
                            V.tensor_tensor(hid[:, e % 2, :], relu_t[:, e % 2, :], p_gate[:, 0:GT],
                                            ALU.mult).then_inc(hid_dve.sem, 1)

                def b_end():
                    if do_b:
                        dve.wait_ge(out_ps.sem, out_ps.at(gb, 1))
                        dve.wait_ge(out_free.sem, out_free.at(gb, 16))
                        V.tensor_tensor(out_t[:, 0:2, :], base[:, 0:2, :], p_up[0:TT, :].rearrange("p (t d) -> p t d", t=2),
                                        ALU.add).then_inc(out_dve.sem, 1)
                        dve.wait_ge(out_ps.sem, out_ps.at(gb, 2))
                        V.tensor_tensor(out_t[:, 2, :], base[:, 2, :], p_gate[0:TT, 0:D], ALU.add).then_inc(out_dve.sem, 1)

                def normalise(source, target, n, done):
                    for t in range(NT):
                        last = V.bn_stats(stats[:, t, :], source[:, t, :])
                    step(last)
                    V.memset(pad[:, :], 0.0)
                    for t in range(NT):
                        last = V.bn_aggr(meanvar[:, t, :], stats[:, t, :])
                    step(last)
                    V.tensor_scalar(vareps[:, :], meanvar[:, :, 1], EPS, None, ALU.add).then_inc(var_dve.sem, 1)
                    dve.wait_ge(rstd_pool.sem, rstd_pool.at(g, n))
                    for t in range(NT):
                        last = V.tensor_scalar(target[:, t, :], source[:, t, :], meanvar[:, t, 0:1], rstd[:, t:t + 1],
                                               ALU.subtract, ALU.mult)
                    if done is None:
                        step(last)
                    else:
                        last.then_inc(done.sem, 1)

                def two_best(P, n, E, k):
                    def v(t):
                        return t[0:P, 0:n * E].rearrange("p (n e) -> p n e", n=n)

                    def wide(t):
                        return t[0:P, 0:n].unsqueeze(2).broadcast_to((P, n, E))

                    ranks = rank[0:P, 0:E].unsqueeze(1).broadcast_to((P, n, E))
                    for logits, top, one in ((lg, top1, one1), (lg2, top2, one2)):
                        step(V.tensor_reduce(top[0:P, 0:n], v(logits), AX.X, ALU.max))
                        step(V.tensor_tensor(v(tmp), v(logits), wide(top), ALU.is_equal))
                        step(V.tensor_tensor(v(tmp), v(tmp), ranks, ALU.mult))
                        step(V.tensor_reduce(pick[0:P, 0:n], v(tmp), AX.X, ALU.max))
                        step(V.tensor_tensor(v(one), v(tmp), wide(pick), ALU.is_equal))
                        if one is one1:
                            step(V.scalar_tensor_tensor(lg2[0:P, 0:n * E], one1[0:P, 0:n * E], -BIG, lg[0:P, 0:n * E],
                                                        ALU.mult, ALU.add))
                    V.tensor_tensor(gdiff[0:P, 0:n], top2[0:P, 0:n], top1[0:P, 0:n],
                                    ALU.subtract).then_inc(gdiff_dve.sem, 1)

                def gate_values(P, n, E, k, target, done):
                    def v(t):
                        return t[0:P, 0:n * E].rearrange("p (n e) -> p n e", n=n)

                    def wide(t):
                        return t[0:P, 0:n].unsqueeze(2).broadcast_to((P, n, E))

                    dve.wait_ge(gexp_act.sem, gexp_act.at(g, k))
                    step(V.tensor_scalar(gone[0:P, 0:n], gexp[0:P, 0:n], 1.0, None, ALU.add))
                    step(V.reciprocal(g1[0:P, 0:n], gone[0:P, 0:n]))
                    V.tensor_tensor(g2[0:P, 0:n], g1[0:P, 0:n], gexp[0:P, 0:n], ALU.mult)
                    step(V.tensor_tensor(v(one1), v(one1), wide(g1), ALU.mult))
                    step(V.tensor_tensor(v(one2), v(one2), wide(g2), ALU.mult))
                    last = V.tensor_tensor(target, v(one1), v(one2), ALU.add)
                    if done is None:
                        step(last)
                    else:
                        last.then_inc(done.sem, 1)

                if not do_a:
                    fill(2 * EF)
                    b_end()
                    return

                for m in range(DC):
                    dve.wait_ge(u_act.sem, u_act.at(g, m + 1))
                    V.scalar_tensor_tensor(h1T[:, m, :], tanh_t[:, m, :], 1.0, pre_t[:, m, :], ALU.add,
                                           ALU.mult).then_inc(h1_dve.sem, 1)
                fill(1)
                fill(1)
                dve.wait_ge(htok_ps.sem, htok_ps.at(g, 1))
                V.tensor_copy(h_res[:, 0:2, :], pa[0][0:TT, :].rearrange("p (t d) -> p t d", t=2)).then_inc(hres_dve.sem, 1)
                dve.wait_ge(htok_ps.sem, htok_ps.at(g, 2))
                V.tensor_copy(h_res[:, 2, :], pa[1][0:TT, 0:D]).then_inc(hres_dve.sem, 1)
                dve.wait_ge(hres_dve.sem, hres_dve.at(g, 2))
                normalise(h_res, normed, 1, norm_dve)
                fill(3)
                fill(1)
                for m in range(DC):
                    dve.wait_ge(qk_ps.sem, qk_ps.at(g, m + 1))
                    for par in range(2):
                        last = V.tensor_scalar(qT[:, m, par, :], pa[m][:, 0:GT], parity[:, par:par + 1], None, ALU.mult)
                    last.then_inc(q_dve.sem, 1)

                def s1_bias(b):
                    dve.wait_ge(s1_ps.sem, s1_ps.at(g, b + 1))
                    if b >= 2 or do_b:
                        dve.wait_ge(p1T_ps.sem, p1T_ps.at(g, 3 * (b - 1)))
                    for r in range(4):
                        last = V.tensor_tensor(s1[:, b % 2, HR * r:HR * r + HR, :],
                                               pa[r][0:T, 0:HR * T].rearrange("p (h t) -> p h t", h=HR),
                                               alibi[:, HR * r * T:HR * (r + 1) * T].rearrange("p (h t) -> p h t", h=HR),
                                               ALU.add)
                    last.then_inc(s1_add.sem, 1)
                    dve.wait_ge(s1_add.sem, s1_add.at(g, b + 1))
                    V.tensor_reduce(s1max[:, b % 2, :], s1[:, b % 2], AX.X, ALU.max).then_inc(s1_max.sem, 1)

                def y1_out(b):
                    dve.wait_ge(y1_ps.sem, y1_ps.at(g, b + 1))
                    y = pa[3][0:T, 0:NH * (HD1 + 1)].rearrange("p (h d) -> p h d", h=NH)
                    step(V.reciprocal(y_rec[:, :], y[:, :, HD1]))
                    V.tensor_tensor(y1[:, b, :].rearrange("p (h d) -> p h d", h=NH), y[:, :, 0:HD1],
                                    y_rec[:, :].unsqueeze(2).broadcast_to((T, NH, HD1)), ALU.mult).then_inc(y1_dve.sem, 1)

                s1_bias(0)
                fill(1)
                s1_bias(1)
                fill(1)
                for b in range(NB):
                    fill(1)
                    y1_out(b)
                    if b + 2 < NB:
                        s1_bias(b + 2)
                        fill(1)
                fill(1)
                fill(1)
                if not do_b:
                    dve.wait_ge(w_late.sem, W_LATE)
                    V.tensor_scalar(moa_qb[:, :], moa_qb[:, :], HD ** -0.5, None, ALU.mult)
                    for b in range(NB):
                        V.tensor_copy(krel[:, b, T + T - 1 - MAXP:T + T + MAXP], rel[:, :])
                        V.tensor_copy(krel[:, b, T:T + T - 1 - MAXP], rel[:, 0:1].broadcast_to((128, T - 1 - MAXP)))
                        V.tensor_copy(krel[:, b, T + T + MAXP:KW], rel[:, NREL - 1:NREL].broadcast_to((128, T - 1 - MAXP)))
                    V.tensor_copy(sel[:, :, :].rearrange("p e f -> p (e f)"), sel32[:, :]).then_inc(const_done.sem, 1)
                dve.wait_ge(proj_ps.sem, proj_ps.at(g, 1))
                V.tensor_tensor(h_res[:, 0:2, :], h_res[:, 0:2, :], pa[2][0:TT, :].rearrange("p (t d) -> p t d", t=2),
                                ALU.add).then_inc(res_dve.sem, 1)
                dve.wait_ge(proj_ps.sem, proj_ps.at(g, 2))
                V.tensor_tensor(h_res[:, 2, :], h_res[:, 2, :], pa[3][0:TT, 0:D], ALU.add).then_inc(res_dve.sem, 1)
                dve.wait_ge(res_dve.sem, res_dve.at(g, 2))
                fill(1)
                normalise(h_res, src, 2, None)
                fill(2)
                normalise(src, normed, 3, norm_dve)
                fill(2)
                fill(1)
                dve.wait_ge(lg1_ps.sem, lg1_ps.at(g, 1))
                V.tensor_copy(lg[0:T, 0:NB * EA], pa[0][0:T, 0:NB * EA]).then_inc(lg_dve.sem, 1)
                dve.wait_ge(v2_ps.sem, v2_ps.at(g, 1))
                V.tensor_tensor(v2[:, :, :], pa[2][0:T, :].rearrange("p (b d) -> p b d", b=NB),
                                moa_vb[:, :].unsqueeze(1).broadcast_to((T, NB, HD)), ALU.add).then_inc(v2_dve.sem, 1)
                dve.wait_ge(lg_dve.sem, lg_dve.at(g, 1))
                two_best(T, NB, EA, 1)

                def s2_out(b):
                    for i in range(2):
                        dve.wait_ge(sr_ps.sem, sr_ps.at(g, 4 * b + i + 3))
                        if i == 0 and (b >= 2 or do_b):
                            dve.wait_ge(rel_out.sem, rel_out.at(g, 16 * (b - 1)))
                            dve.wait_ge(s2_add.sem, s2_add.at(g, b - 1))
                        V.tensor_copy(sr[:, b % 2, 4 + 2 * i:6 + 2 * i, :],
                                      pa[2 + i][0:T, 0:2 * KW].rearrange("p (e k) -> p e k", e=2)).then_inc(sr_dve.sem, 1)

                def s2_top(b):
                    dve.wait_ge(s2_add.sem, s2_add.at(g, b + 1))
                    V.tensor_reduce(s2max[:, b % 2, :], s2[:, b % 2], AX.X, ALU.max).then_inc(s2_max.sem, 1)

                def s2_factor(b):
                    dve.wait_ge(s2_exp.sem, s2_exp.at(g, b + 1))
                    step(V.tensor_reduce(s2sum[:, b % 2, :], s2[:, b % 2], AX.X, ALU.add))
                    step(V.reciprocal(s2rec[:, b % 2, :], s2sum[:, b % 2, :]))
                    V.tensor_tensor(s2fac[:, b % 2, :], s2rec[:, b % 2, :], gates1[:, b, :],
                                    ALU.mult).then_inc(s2_fac.sem, 1)

                def ctx_out(b):
                    dve.wait_ge(ctx_ps.sem, ctx_ps.at(g, 2 * b + 2))
                    V.tensor_copy(ctxT[:, 4:8, b * T:(b + 1) * T],
                                  pa[3][:, 0:4 * T].rearrange("p (e t) -> p e t", e=4)).then_inc(ctx_dve.sem, 1)

                s2_out(0)
                gate_values(T, NB, EA, 1, gates1[:, :, :], gates1_dve)
                fill(1)
                s2_out(1)
                fill(1)
                s2_top(0)
                dve.wait_ge(gates1_dve.sem, gates1_dve.at(g, 1))
                s2_factor(0)
                for b in range(NB):
                    if b + 1 < NB:
                        s2_top(b + 1)
                    fill(1)
                    fill(1)
                    ctx_out(b)
                    if b + 2 < NB:
                        s2_out(b + 2)
                    if b + 1 < NB:
                        s2_factor(b + 1)
                fill(2 * EF)
                dve.wait_ge(moa_ps.sem, moa_ps.at(g, 1))
                V.tensor_tensor(moa_x[:, 0:2, :], src[:, 0:2, :], pa[2][0:TT, :].rearrange("p (t d) -> p t d", t=2),
                                ALU.add).then_inc(moa_dve.sem, 1)
                dve.wait_ge(moa_ps.sem, moa_ps.at(g, 2))
                V.tensor_tensor(moa_x[:, 2, :], src[:, 2, :], pa[3][0:TT, 0:D], ALU.add).then_inc(moa_dve.sem, 1)
                b_end()
                dve.wait_ge(moa_dve.sem, moa_dve.at(g, 2))
                normalise(moa_x, normed, 4, norm_dve)
                V.tensor_tensor(base[:, :, :], h_res[:, :, :], moa_x[:, :, :], ALU.add)
                dve.wait_ge(lg2_ps.sem, lg2_ps.at(g, 1))
                V.tensor_copy(lg[:, 0:NT * EF], pa[2][0:TT, 0:NT * EF]).then_inc(lg_dve.sem, 1)
                dve.wait_ge(lg_dve.sem, lg_dve.at(g, 2))
                two_best(TT, NT, EF, 2)
                gate_values(TT, NT, EF, 2, gates2[:, :, :], None)
                step(V.tensor_copy(ghi[:, :, :], gates2[:, :, :]))
                V.tensor_copy(gparts[:, :, 0, :], ghi[:, :, :])
                step(V.tensor_tensor(gates2[:, :, :], gates2[:, :, :], ghi[:, :, :], ALU.subtract))
                step(V.tensor_copy(gmid[:, :, :], gates2[:, :, :]))
                V.tensor_copy(gparts[:, :, 1, :], gmid[:, :, :])
                V.tensor_tensor(gparts[:, :, 2, :], gates2[:, :, :], gmid[:, :, :],
                                ALU.subtract).then_inc(gparts_dve.sem, 1)
                assert steps[0] == A_STEPS, steps[0]

            loop(dve, body)


count_steps = 55


def kernel(x, txt, L0_tok_W1, L0_tok_b1, L0_tok_W2, L0_tok_b2, L0_attn_w_attn, L0_attn_w_proj, L0_ffn_ln1_w,
           L0_ffn_ln1_b, L0_ffn_ln2_w, L0_ffn_ln2_b, L0_ffn_attn_gate_w, L0_ffn_q_w, L0_ffn_q_b, L0_ffn_k_w,
           L0_ffn_k_b, L0_ffn_v_w, L0_ffn_v_b, L0_ffn_o_w, L0_ffn_o_b, L0_ffn_rel_table, L0_ffn_ff_gate_w,
           L0_ffn_ff_w1, L0_ffn_ff_b1, L0_ffn_ff_w2, L0_ffn_ff_b2):
    import numpy as np
    import concourse.bacc as bacc
    from concourse.bass_utils import run_bass_kernel_spmd

    def rows(a, *shape):
        a = np.asarray(a)
        a = a.reshape(-1, 128, *a.shape[1:]).swapaxes(0, 1)
        return a.reshape(shape) if shape else a

    patches = np.asarray(x).reshape(NSEQ, 3, 7, 16, 7, 16).transpose(0, 2, 4, 1, 3, 5).reshape(G, GP, PC, 128)
    text = np.asarray(txt).reshape(G, NB, NTEXT, DC, 128)
    arrays = {
        "x": patches.transpose(0, 3, 2, 1),
        "txt": text.transpose(0, 4, 3, 1, 2),
        "tok_w1": rows(L0_tok_W1), "tok_w2": rows(L0_tok_W2),
        "tok_b1": rows(L0_tok_b1), "tok_b2": rows(L0_tok_b2),
        "wqkv": rows(np.asarray(L0_attn_w_attn).T), "wproj": rows(np.asarray(L0_attn_w_proj).T),
        "ln1": np.stack([rows(L0_ffn_ln1_w), rows(L0_ffn_ln1_b)], 1),
        "ln2": np.stack([rows(L0_ffn_ln2_w), rows(L0_ffn_ln2_b)], 1),
        "moa_gw": rows(L0_ffn_attn_gate_w),
        "moa_qw": np.asarray(L0_ffn_q_w).reshape(EA, DC, 128, HD).transpose(2, 1, 0, 3),
        "moa_qb": np.asarray(L0_ffn_q_b).T,
        "moa_kw": rows(L0_ffn_k_w), "moa_kb": np.asarray(L0_ffn_k_b).reshape(HD, 1),
        "moa_vw": rows(L0_ffn_v_w), "moa_vb": np.asarray(L0_ffn_v_b).reshape(1, HD),
        "moa_ow": np.asarray(L0_ffn_o_w).transpose(1, 0, 2), "moa_ob": np.asarray(L0_ffn_o_b),
        "rel": np.asarray(L0_ffn_rel_table).T,
        "ff_gw": rows(L0_ffn_ff_gate_w),
        "ff_w1": np.asarray(L0_ffn_ff_w1).reshape(EF, DC, 128, FH).transpose(2, 1, 0, 3),
        "ff_b1": np.asarray(L0_ffn_ff_b1).T,
        "ff_w2": np.asarray(L0_ffn_ff_w2).transpose(1, 0, 2), "ff_b2": np.asarray(L0_ffn_ff_b2),
    }
    q, k = np.arange(T)[:, None], np.arange(T)[None, :]
    slopes = (2.0 ** -0.5 * (2.0 ** -0.5) ** np.arange(NH)).astype(np.float32)
    order = [(j % HR) // 2 * 8 + 2 * (j // HR) + j % 2 for j in range(NH)]
    bias = np.where((k <= q)[:, None, :], slopes[order][None, :, None] * (k - q).astype(np.float32)[:, None, :],
                    np.float32(-BIG))
    odd = (np.arange(128) // HD1) % 2
    selectors = np.tile(np.repeat(np.eye(EF, dtype=np.float32), FH, axis=1), (3, 1))
    arrays |= {
        "ident": np.eye(128, dtype=np.float32),
        "alibi": bias.reshape(T, NH * T).astype(np.float32),
        "parity": np.stack([(odd == 0) * HD1 ** -0.5, (odd == 1) * HD1 ** -0.5], 1).astype(np.float32),
        "rank": np.tile(np.arange(EF, 0, -1, dtype=np.float32), (128, 1)),
        "sel32": selectors,
    }
    arrays = {name: np.ascontiguousarray(a) for name, a in arrays.items()}
    nc = bacc.Bacc("TRN2", target_bir_lowering=False, num_devices=1)
    A = {name: nc.dram_tensor(name + "_in", a.shape, F32, kind="ExternalInput").ap() for name, a in arrays.items()}
    o = nc.dram_tensor("out", (G, TT, NT, D), F32, kind="ExternalOutput").ap()
    build(nc, A, o)
    r = run_bass_kernel_spmd(nc, [{name + "_in": a for name, a in arrays.items()}], core_ids=[0])
    got = r.results[0]["out"]
    return got.transpose(0, 2, 1, 3).reshape(NSEQ, T, D)
```

```python
from contextlib import ExitStack
from itertools import islice

import concourse.bass as bass
from concourse import mybir

F32 = mybir.dt.float32
BF16 = mybir.dt.bfloat16
ALU = mybir.AluOpType
ACT = mybir.ActivationFunctionType
AX = mybir.AxisListType

NSEQ, NPATCH, NTEXT = 64, 49, 32
T = NPATCH + NTEXT
D = 256
DC = D // 128
PATCH = 3 * 16 * 16
PC = PATCH // 128
NB = 4
G = NSEQ // NB
GT = NB * T
GP = NB * NPATCH
NT = 3
TT = GT // NT
NH, HD1 = 16, 16
HR = NH // 4
EA, HD = 8, 128
MAXP = 64
NREL = 2 * MAXP + 1
RW = 2 * T - 1
KW = T + RW
EF, FH = 16, 128
EPS = 1e-5
BIG = 1e30
FIRST_STEPS, BODY_STEPS = 2, 55
UNITS = [("up", 0)] + [u for e in range(1, EF) for u in (("up", e), ("down", e - 1))] + [("down", EF - 1)]


class Signal:

    def __init__(self, handle, per):
        self.sem, self.per = handle, per

    def at(self, g, n):
        return g * self.per + n


def build(nc, A, out):
    ctx = ExitStack()
    with ctx:
        def sb(name, shape, dt=F32):
            return ctx.enter_context(nc.sbuf_tensor(name, shape, dt))

        def bank(name):
            return ctx.enter_context(nc.psum_tensor(name, [128, 512], F32))

        def signal(name, per=1):
            return Signal(ctx.enter_context(nc.semaphore(name)), per)

        tok_w1 = sb("tok_w1", [128, PC, D])
        tok_w2 = sb("tok_w2", [128, DC, D])
        tok_b1 = sb("tok_b1", [128, DC])
        tok_b1h = sb("tok_b1h", [128, DC])
        tok_b2 = sb("tok_b2", [128, DC])
        wqkv = sb("wqkv", [128, DC, 3 * D])
        wproj = sb("wproj", [128, DC, D])
        ln1 = sb("ln1", [128, 2, DC])
        ln2 = sb("ln2", [128, 2, DC])
        moa_gw = sb("moa_gw", [128, DC, EA])
        moa_qw = sb("moa_qw", [128, DC, EA, HD])
        moa_qb = sb("moa_qb", [128, EA])
        moa_kw = sb("moa_kw", [128, DC, HD])
        moa_kb = sb("moa_kb", [128, 1])
        moa_vw = sb("moa_vw", [128, DC, HD])
        moa_vb = sb("moa_vb", [T, HD])
        moa_ow = sb("moa_ow", [128, EA, D])
        moa_ob = sb("moa_ob", [EA, D])
        rel = sb("rel", [128, NREL])
        ff_gw = sb("ff_gw", [128, DC, EF])
        ff_w1 = sb("ff_w1", [128, DC, EF, FH])
        ff_b1 = sb("ff_b1", [128, EF])
        ff_w2 = sb("ff_w2", [128, EF, D])
        ff_b2 = sb("ff_b2", [3 * EF, D])
        ident = sb("ident", [128, 128])
        alibi = sb("alibi", [T, NH * T])
        parity = sb("parity", [128, 2])
        rank = sb("rank", [128, EF])
        sel = sb("sel", [3 * EF, EF, FH], BF16)
        neg_half = sb("neg_half", [TT, NT])

        xT = sb("xT", [128, PC, GP])
        tanh_t = sb("tanh_t", [128, DC, GP])
        pre_t = sb("pre_t", [128, DC, GP])
        h1T = tanh_t
        hT = sb("hT", [128, DC, NB, T])
        h_res = sb("h_res", [TT, NT, D])
        pad = sb("pad", [TT, 1])
        stats = sb("stats", [TT, NT, 6])
        meanvar = sb("meanvar", [TT, NT, 2])
        vareps = sb("vareps", [TT, NT])
        rstd = sb("rstd", [TT, NT])
        normed = sb("normed", [TT, NT, D])
        h_new = sb("h_new", [TT, NT, D])
        normed1 = sb("normed1", [TT, NT, D])
        nT = sb("nT", [128, DC, GT])
        v_aug = sb("v_aug", [T, NB, NH, HD1 + 1])
        s1 = sb("s1", [T, 2, NH, T])
        s1max = sb("s1max", [T, 2, NH])
        p1T = sb("p1T", [T, NH, T])
        y_rec = sb("y_rec", [T, NH])
        yT = sb("yT", [128, DC, GT])
        src = sb("src", [TT, NT, D])
        qeT = sb("qeT", [128, EA, GT])
        qT = qeT[:, 0:2 * DC, :].rearrange("p (c k) t -> p c k t", c=DC)
        kT = qeT[:, 2 * DC:3 * DC, :]
        krel = sb("krel", [128, NB, KW])
        v2 = sb("v2", [T, NB, HD])
        lg = sb("lg", [TT, NT * EF])
        one1 = sb("one1", [TT, NT * EF])
        one2 = sb("one2", [TT, NT * EF])
        tmp = sb("tmp", [TT, NT * EF])
        lg2 = sb("lg2", [TT, NT * EF])
        top1 = sb("top1", [TT, NB])
        top2 = sb("top2", [TT, NB])
        pick = sb("pick", [TT, NB])
        gdiff = sb("gdiff", [TT, NB])
        gexp = sb("gexp", [TT, NB])
        gone = sb("gone", [TT, NB])
        g1 = sb("g1", [TT, NB])
        g2 = sb("g2", [TT, NB])
        gates1 = sb("gates1", [T, NB, EA])
        gates1T = sb("gates1T", [EA, GT])
        sr = sb("sr", [T, NB, EA, KW])
        relb = s1[:, :].rearrange("p s (b e) t -> p (s b) e t", e=EA)
        s2max = sb("s2max", [T, NB, EA])
        s2sum = sb("s2sum", [T, NB, EA])
        s2rec = sb("s2rec", [T, NB, EA])
        s2fac = sb("s2fac", [T, NB, EA])
        p2T = p1T[:, 0:EA, :]
        ctxT = sb("ctxT", [128, EA, GT])
        moa_x = sb("moa_x", [TT, NT, D])
        gates2 = sb("gates2", [TT, NT, EF])
        ghi = sb("ghi", [TT, NT, EF], BF16)
        gmid = sb("gmid", [TT, NT, EF], BF16)
        gparts = sb("gparts", [TT, NT, 3, EF])
        y1 = ctxT[0:T].rearrange("p e t -> p (e t)")[:, 0:NB * D].rearrange("p (b d) -> p b d", b=NB)
        sel32 = sr[0:3 * EF].rearrange("p b e t -> p (b e t)")[:, 0:EF * FH]
        base = sb("base", [TT, NT, D])
        xn2T = sb("xn2T", [128, DC, GT])
        g2T = sb("g2T", [3 * EF, GT])
        g2Tb = sb("g2Tb", [3 * EF, GT], BF16)
        relu_t = sb("relu_t", [128, 2, GT])
        hid = sb("hid", [128, 2, GT])
        moeT = yT
        out_t = src

        pa = [bank(f"pa{i}") for i in range(4)]
        p_up = bank("p_up")
        p_gate = bank("p_gate")
        p_acc = [bank(f"p_acc{i}") for i in range(2)]

        rel_dram = nc.dram_tensor("rel_scratch", [NB, T, EA, RW], F32, kind="Internal")

        w_early = signal("w_early")
        w_late = signal("w_late")
        const_done = signal("const_done")
        pool_const = signal("pool_const")
        x_in = signal("x_in", 16)
        txt_in = signal("txt_in", 16 * DC)
        rel_out = signal("rel_out", 16 * NB)
        relb_in = [signal(f"relb_in{b}", 16) for b in range(NB)]
        out_free = signal("out_free", 16)
        u_ps = signal("u_ps", DC)
        emb_ps = signal("emb_ps", DC)
        htok_ps = signal("htok_ps", 2)
        nT_ps = signal("nT_ps", 2)
        qk_ps = signal("qk_ps", 4)
        v_ps = signal("v_ps", NB)
        s1_ps = signal("s1_ps", NB)
        p1T_ps = signal("p1T_ps", 3 * NB)
        y1_ps = signal("y1_ps", NB)
        yT_ps = signal("yT_ps", DC)
        proj_ps = signal("proj_ps", 2)
        xnT_ps = signal("xnT_ps", 2)
        qe_ps = signal("qe_ps", EA)
        k2_ps = signal("k2_ps")
        v2_ps = signal("v2_ps")
        lg1_ps = signal("lg1_ps")
        g1T_ps = signal("g1T_ps")
        sr_ps = signal("sr_ps", 4 * NB)
        p2T_ps = signal("p2T_ps", 2 * NB)
        ctx_ps = signal("ctx_ps", 2 * NB)
        moa_ps = signal("moa_ps", 2)
        xn2T_ps = signal("xn2T_ps", 2)
        lg2_ps = signal("lg2_ps")
        g2T_ps = signal("g2T_ps")
        up_ps = signal("up_ps", EF)
        acc_ps = signal("acc_ps", DC)
        out_ps = signal("out_ps", 2)
        u_act = signal("u_act", DC)
        hT_act = signal("hT_act", DC)
        nT_act = signal("nT_act", 2)
        qk_act = signal("qk_act", 4)
        v_act = signal("v_act", NB)
        s1_exp = signal("s1_exp", NB)
        p1T_act = signal("p1T_act", 3 * NB)
        yT_act = signal("yT_act", DC)
        xnT_act = signal("xnT_act", 2)
        qe_act = signal("qe_act", EA)
        k2_act = signal("k2_act")
        g1T_act = signal("g1T_act")
        gexp_act = signal("gexp_act", 2)
        sr_act = signal("sr_act", 2 * NB)
        s2_exp = signal("s2_exp", NB)
        p2T_act = signal("p2T_act", 2 * NB)
        ctx_act = signal("ctx_act", NB)
        xn2T_act = signal("xn2T_act", 2)
        g2T_act = signal("g2T_act")
        relu_act = signal("relu_act", EF)
        acc_act = signal("acc_act", DC)
        a_step = signal("a_step", 0)
        h1_dve = signal("h1_dve", DC)
        hres_dve = signal("hres_dve", 2)
        var_dve = signal("var_dve", 4)
        norm1_dve = signal("norm1_dve")
        norm_dve = signal("norm_dve", 2)
        s1_max = signal("s1_max", NB)
        s1_add = signal("s1_add", NB)
        y1_dve = signal("y1_dve", NB)
        res_dve = signal("res_dve", 2)
        v2_dve = signal("v2_dve")
        lg_dve = signal("lg_dve", 2)
        gdiff_dve = signal("gdiff_dve", 2)
        gates1_dve = signal("gates1_dve")
        sr_dve = signal("sr_dve", 2 * NB)
        s2_max = signal("s2_max", NB)
        s2_fac = signal("s2_fac", NB)
        ctx_dve = signal("ctx_dve", NB)
        moa_dve = signal("moa_dve", 2)
        gparts_dve = signal("gparts_dve")
        hid_dve = signal("hid_dve", EF)
        out_dve = signal("out_dve", 2)
        rstd_pool = signal("rstd_pool", 4)
        s1_sub = signal("s1_sub", NB)
        s2_add = signal("s2_add", NB)
        s2_sub = signal("s2_sub", NB)
        p2_pool = signal("p2_pool", NB)

        EARLY = [(tok_w1, "tok_w1"), (tok_w2, "tok_w2"), (tok_b1, "tok_b1"), (tok_b2, "tok_b2"), (ident, "ident"),
                 (wqkv, "wqkv"), (parity, "parity"), (alibi, "alibi"), (wproj, "wproj")]
        LATE = [(ln1, "ln1"), (ln2, "ln2"), (moa_gw, "moa_gw"), (moa_qw, "moa_qw"), (moa_qb, "moa_qb"),
                (moa_kw, "moa_kw"), (moa_kb, "moa_kb"), (moa_vw, "moa_vw"), (moa_ow, "moa_ow"),
                (moa_ob, "moa_ob"), (rel, "rel"), (rank, "rank"), (ff_gw, "ff_gw"), (ff_w1, "ff_w1"),
                (ff_b1, "ff_b1"), (ff_w2, "ff_w2"), (sel32, "sel32")]
        W_EARLY, W_LATE = 16 * len(EARLY), 16 * (len(LATE) + 4)

        def loop(engine, body):
            body(0, False, True)
            with engine.Fori(1, G - 1) as g:
                body(g, True, True)
            body(G - 1, True, False)

        block = ctx.enter_context(nc.Block())

        @block.sync
        def _(sp):
            sp.sem_inc(out_free.sem, 16)
            for t, name in EARLY[:1]:
                sp.dma_start(t[:], A[name]).then_inc(w_early.sem, 16)
            sp.dma_start(xT[:, :, :], A["x"][0]).then_inc(x_in.sem, 16)
            for t, name in EARLY[1:]:
                sp.dma_start(t[:], A[name]).then_inc(w_early.sem, 16)
            sp.dma_start(hT[:, 0, :, NPATCH:T], A["txt"][0, :, 0]).then_inc(txt_in.sem, 16)
            sp.dma_start(hT[:, 1, :, NPATCH:T], A["txt"][0, :, 1]).then_inc(txt_in.sem, 16)
            for t, name in LATE:
                sp.dma_start(t[:], A[name]).then_inc(w_late.sem, 16)
            sp.dma_start(moa_vb[:, :], A["moa_vb"].broadcast_to((T, HD))).then_inc(w_late.sem, 16)
            for i in range(3):
                sp.dma_start(ff_b2[i * EF:(i + 1) * EF, :], A["ff_b2"]).then_inc(w_late.sem, 16)

            def body(g, do_b, do_next):
                if do_next:
                    sp.wait_ge(u_ps.sem, u_ps.at(g, DC))
                    sp.dma_start(xT[:, :, :], A["x"][g + 1]).then_inc(x_in.sem, 16)
                    sp.wait_ge(htok_ps.sem, htok_ps.at(g, 2))
                    for c in range(DC):
                        sp.dma_start(hT[:, c, :, NPATCH:T], A["txt"][g + 1, :, c]).then_inc(txt_in.sem, 16)
                for b in range(NB):
                    sp.wait_ge(sr_act.sem, sr_act.at(g, 2 * b + 2))
                    sp.wait_ge(sr_dve.sem, sr_dve.at(g, 2 * b + 2))
                    sp.dma_start(rel_dram.ap()[b], sr[:, b, :, T:KW]).then_inc(rel_out.sem, 16)
                    sp.wait_ge(rel_out.sem, rel_out.at(g, 16 * (b + 1)))
                    skewed = bass.AP(tensor=rel_dram, offset=b * T * EA * RW + T - 1,
                                     ap=[[EA * RW - 1, T], [RW, EA], [1, T]])
                    sp.dma_start(relb[:, b], skewed).then_inc(relb_in[b].sem, 16)

            loop(sp, body)
            sp.wait_ge(out_free.sem, 16 * (G + 1))
            sp.wait_ge(rel_out.sem, 16 * NB * G)

        @block.tensor
        def _(pe):
            mm = nc.tensor.matmul

            def transpose_tiles(source, banks):
                for m in range(DC):
                    for t in range(NT):
                        last = nc.tensor.transpose(banks[m][:, t * TT:(t + 1) * TT],
                                                   source[:, t, m * 128:(m + 1) * 128], ident[0:TT, 0:TT])
                    yield last

            def patches(g):
                pe.wait_ge(x_in.sem, x_in.at(g, 16))
                for m in range(DC):
                    for c in range(PC):
                        last = mm(pa[m][:, 0:GP], tok_w1[:, c, m * 128:(m + 1) * 128], xT[:, c, :],
                                  start=(c == 0), stop=(c == PC - 1))
                    last.then_inc(u_ps.sem, 1)

            def embeddings(g):
                pe.wait_ge(h1_dve.sem, h1_dve.at(g, DC))
                for m in range(DC):
                    for c in range(DC):
                        last = mm(pa[m][:, 0:GP], tok_w2[:, c, m * 128:(m + 1) * 128], h1T[:, c, :],
                                  start=(c == 0), stop=(c == DC - 1))
                    last.then_inc(emb_ps.sem, 1)

            def token_major(g):
                pe.wait_ge(txt_in.sem, txt_in.at(g, 16 * DC))
                pe.wait_ge(hT_act.sem, hT_act.at(g, DC))
                flat = hT[:, :, :, :].rearrange("p c b t -> p c (b t)")
                for t in range(NT):
                    for m in range(DC):
                        last = nc.tensor.transpose(pa[t // 2][0:TT, (t % 2) * D + m * 128:(t % 2) * D + (m + 1) * 128],
                                                   flat[:, m, t * TT:(t + 1) * TT], ident[:, :])
                    if t:
                        last.then_inc(htok_ps.sem, 1)

            def normed_tokens(g):
                pe.wait_ge(norm1_dve.sem, norm1_dve.at(g, 1))
                for last in transpose_tiles(normed1, pa[0:2]):
                    last.then_inc(nT_ps.sem, 1)

            def queries_keys(g, chunks):
                for i in chunks:
                    for c in range(DC):
                        last = mm(pa[i][:, 0:GT], wqkv[:, c, i * 128:(i + 1) * 128], nT[:, c, :],
                                  start=(c == 0), stop=(c == DC - 1))
                    last.then_inc(qk_ps.sem, 1)

            def values(g):
                for n, b in enumerate((2, 3, 0, 1)):
                    pe.wait_ge(qk_act.sem, qk_act.at(g, n + 1))
                    for c in range(DC):
                        last = mm(pa[b][0:T, 0:D], nT[:, c, b * T:(b + 1) * T], wqkv[:, c, 2 * D:3 * D],
                                  start=(c == 0), stop=(c == DC - 1))
                    last.then_inc(v_ps.sem, 1)

            def body(g, do_b, do_next):
                left = iter(UNITS if do_b else [])
                gb = g - 1

                def fill(n):
                    nonlocal left, gb
                    """The next n units of stage B of the group before."""
                    for kind, e in islice(left, n):
                        if kind == "up":
                            if e == 0:
                                pe.wait_ge(xn2T_act.sem, xn2T_act.at(gb, 2))
                                pe.wait_ge(g2T_act.sem, g2T_act.at(gb, 1))
                            if e:
                                pe.wait_ge(hid_dve.sem, hid_dve.at(gb, e))
                            mm(p_gate[:, 0:GT], sel[:, e, :], g2Tb[:, :], start=True, stop=True)
                            if e:
                                pe.wait_ge(relu_act.sem, relu_act.at(gb, e))
                            for c in range(DC):
                                last = mm(p_up[:, 0:GT], ff_w1[:, c, e, :], xn2T[:, c, :],
                                          start=(c == 0), stop=(c == DC - 1))
                            last.then_inc(up_ps.sem, 1)
                        else:
                            pe.wait_ge(hid_dve.sem, hid_dve.at(gb, e + 1))
                            for m in range(DC):
                                mm(p_acc[m][:, 0:GT], ff_w2[:, e, m * 128:(m + 1) * 128], hid[:, e % 2, :],
                                   start=(e == 0), stop=False)
                            if e == EF - 1:
                                for m in range(DC):
                                    mm(p_acc[m][:, 0:GT], ff_b2[:, m * 128:(m + 1) * 128], g2T[:, :],
                                       start=False, stop=True).then_inc(acc_ps.sem, 1)

                def gates_transposed(gb):
                    pe.wait_ge(gparts_dve.sem, gparts_dve.at(gb, 1))
                    for t in range(NT):
                        last = mm(p_acc[1][0:3 * EF, t * TT:(t + 1) * TT], gparts[:, t].rearrange("p k e -> p (k e)"),
                                  ident[0:TT, 0:TT], start=True, stop=True)
                    last.then_inc(g2T_ps.sem, 1)

                def b_end():
                    if not do_b:
                        return
                    pe.wait_ge(acc_act.sem, acc_act.at(gb, DC))
                    for t in range(NT):
                        dst = (p_up, p_up, p_gate)[t][0:TT, (t % 2) * D:(t % 2 + 1) * D]
                        for m in range(DC):
                            last = nc.tensor.transpose(dst[:, m * 128:(m + 1) * 128],
                                                       moeT[:, m, t * TT:(t + 1) * TT], ident[:, :])
                        if t:
                            last.then_inc(out_ps.sem, 1)

                def s1_scores(b):
                    if b == 0:
                        pe.wait_ge(v_act.sem, v_act.at(g, NB))
                    else:
                        pe.wait_ge(s1_add.sem, s1_add.at(g, b))
                        if b >= 2:
                            pe.wait_ge(y1_dve.sem, y1_dve.at(g, b - 1))
                    for i in range(HR):
                        for r in range(4):
                            c, par = i // 2, i % 2
                            rows = slice(32 * r, 32 * r + 32)
                            last = mm(pa[r][0:T, i * T:(i + 1) * T], qT[rows, c, par, b * T:(b + 1) * T],
                                      kT[rows, c, b * T:(b + 1) * T], start=True, stop=True,
                                      tile_position=(32 * r, 0))
                    last.then_inc(s1_ps.sem, 1)

                def p1_transposes(b):
                    pe.wait_ge(s1_exp.sem, s1_exp.at(g, b + 1))
                    if b + 1 < NB:
                        pe.wait_ge(s1_add.sem, s1_add.at(g, b + 2))
                    else:
                        pe.wait_ge(p1T_act.sem, p1T_act.at(g, 3 * b))
                    for j in range(NH):
                        last = nc.tensor.transpose(pa[j // 6][0:T, (j % 6) * T:(j % 6 + 1) * T],
                                                   s1[:, b % 2, j, :], ident[0:T, 0:T])
                        if j in (5, 11, NH - 1):
                            last.then_inc(p1T_ps.sem, 1)

                def y1_product(b):
                    for j in range(NH):
                        if j % 6 == 0:
                            pe.wait_ge(p1T_act.sem, p1T_act.at(g, 3 * b + j // 6 + 1))
                            if j == 0 and b == NB - 1:
                                pe.wait_ge(y1_dve.sem, y1_dve.at(g, b))
                        r, c, par = j // HR, (j % HR) // 2, j % 2
                        head = c * 8 + 2 * r + par
                        last = mm(pa[3][0:T, head * (HD1 + 1):(head + 1) * (HD1 + 1)], p1T[:, j, :],
                                  v_aug[:, b, head, :], start=True, stop=True)
                    last.then_inc(y1_ps.sem, 1)

                s1_scores(0)
                if do_b:
                    gates_transposed(gb)
                fill(1)
                s1_scores(1)
                fill(1)
                for b in range(NB):
                    p1_transposes(b)
                    fill(1)
                    y1_product(b)
                    if b + 2 < NB:
                        s1_scores(b + 2)
                    fill(1)
                pe.wait_ge(y1_dve.sem, y1_dve.at(g, NB))
                for m in range(DC):
                    for b in range(NB):
                        last = nc.tensor.transpose(pa[m][:, b * T:(b + 1) * T], y1[:, b, m * 128:(m + 1) * 128],
                                                   ident[0:T, 0:T])
                    last.then_inc(yT_ps.sem, 1)
                fill(1)
                pe.wait_ge(yT_act.sem, yT_act.at(g, DC))
                for t in range(NT):
                    for c in range(DC):
                        last = mm(pa[2 + t // 2][0:TT, (t % 2) * D:(t % 2 + 1) * D], yT[:, c, t * TT:(t + 1) * TT],
                                  wproj[:, c, :], start=(c == 0), stop=(c == DC - 1))
                    if t:
                        last.then_inc(proj_ps.sem, 1)
                fill(7)
                pe.wait_ge(norm_dve.sem, norm_dve.at(g, 1))
                for last in transpose_tiles(normed, pa[0:2]):
                    last.then_inc(xnT_ps.sem, 1)
                fill(1)
                pe.wait_ge(xnT_act.sem, xnT_act.at(g, 2))
                if not do_b:
                    pe.wait_ge(w_late.sem, W_LATE)
                    pe.wait_ge(const_done.sem, 2)
                for b in range(NB):
                    for c in range(DC):
                        last = mm(pa[0][0:T, b * EA:(b + 1) * EA], nT[:, c, b * T:(b + 1) * T], moa_gw[:, c, :],
                                  start=(c == 0), stop=(c == DC - 1))
                last.then_inc(lg1_ps.sem, 1)
                for c in range(DC):
                    last = mm(pa[1][:, 0:GT], moa_kw[:, c, :], nT[:, c, :], start=(c == 0), stop=(c == DC - 1))
                last.then_inc(k2_ps.sem, 1)
                for b in range(NB):
                    for c in range(DC):
                        last = mm(pa[2][0:T, b * HD:(b + 1) * HD], nT[:, c, b * T:(b + 1) * T], moa_vw[:, c, :],
                                  start=(c == 0), stop=(c == DC - 1))
                last.then_inc(v2_ps.sem, 1)
                for e in range(EA):
                    i = (e + 3) % 4
                    if e == 1:
                        pe.wait_ge(lg_dve.sem, lg_dve.at(g, 1))
                    elif e == 2:
                        pe.wait_ge(k2_act.sem, k2_act.at(g, 1))
                    elif e == 3:
                        pe.wait_ge(v2_dve.sem, v2_dve.at(g, 1))
                    elif e >= 4:
                        pe.wait_ge(qe_act.sem, qe_act.at(g, e - 3))
                    for c in range(DC):
                        last = mm(pa[i][:, 0:GT], moa_qw[:, c, e, :], nT[:, c, :], start=(c == 0), stop=(c == DC - 1))
                    last.then_inc(qe_ps.sem, 1)

                def s2_scores(b):
                    for e in range(EA):
                        i = e // 2
                        if e % 2 == 0:
                            if b == 0:
                                pe.wait_ge(qe_act.sem, qe_act.at(g, EA))
                            elif i < 2:
                                pe.wait_ge(sr_act.sem, sr_act.at(g, 2 * (b - 1) + i + 1))
                            else:
                                pe.wait_ge(sr_dve.sem, sr_dve.at(g, 2 * (b - 1) + i - 1))
                        last = mm(pa[i][0:T, (e % 2) * KW:(e % 2 + 1) * KW], qeT[:, e, b * T:(b + 1) * T],
                                  krel[:, b, :], start=True, stop=True)
                        if e % 2:
                            last.then_inc(sr_ps.sem, 1)

                def p2_transposes(b):
                    pe.wait_ge(p2_pool.sem, p2_pool.at(g, b + 1))
                    for i in range(2):
                        if b == 0:
                            pe.wait_ge(sr_act.sem, sr_act.at(g, 2 * (NB - 1) + i + 1))
                        for j in range(4):
                            last = nc.tensor.transpose(pa[i][0:T, j * T:(j + 1) * T], sr[:, b, 4 * i + j, 0:T],
                                                       ident[0:T, 0:T])
                        last.then_inc(p2T_ps.sem, 1)

                def ctx_product(b):
                    for i in range(2):
                        pe.wait_ge(p2T_act.sem, p2T_act.at(g, 2 * b + i + 1))
                        if b == 0:
                            pe.wait_ge(sr_dve.sem, sr_dve.at(g, 2 * (NB - 1) + i + 1))
                        elif i == 0:
                            pe.wait_ge(ctx_act.sem, ctx_act.at(g, b))
                        else:
                            pe.wait_ge(ctx_dve.sem, ctx_dve.at(g, b))
                        mm(pa[2 + i][:, 0:4 * T], v2[:, b, :],
                           p2T[:, 4 * i:4 * i + 4, :].rearrange("p e t -> p (e t)"),
                           start=True, stop=True).then_inc(ctx_ps.sem, 1)

                for b in range(NB):
                    s2_scores(b)
                fill(3)
                for b in range(NB):
                    fill(1)
                    p2_transposes(b)
                    fill(1)
                    ctx_product(b)
                pe.wait_ge(gates1_dve.sem, gates1_dve.at(g, 1))
                pe.wait_ge(p2T_act.sem, p2T_act.at(g, 2 * NB))
                for b in range(NB):
                    last = mm(pa[1][0:EA, b * T:(b + 1) * T], gates1[:, b, :], ident[0:T, 0:T], start=True, stop=True)
                last.then_inc(g1T_ps.sem, 1)
                pe.wait_ge(ctx_act.sem, ctx_act.at(g, NB))
                pe.wait_ge(ctx_dve.sem, ctx_dve.at(g, NB))
                pe.wait_ge(g1T_act.sem, g1T_act.at(g, 1))
                if do_next:
                    patches(g + 1)

                def moa_output(t):
                    dst = pa[2 + t // 2][0:TT, (t % 2) * D:(t % 2 + 1) * D]
                    for e in range(EA):
                        mm(dst, ctxT[:, e, t * TT:(t + 1) * TT], moa_ow[:, e, :], start=(e == 0), stop=False)
                    last = mm(dst, gates1T[:, t * TT:(t + 1) * TT], moa_ob[:, :], start=False, stop=True)
                    if t:
                        last.then_inc(moa_ps.sem, 1)

                moa_output(0)
                if do_next:
                    embeddings(g + 1)
                moa_output(1)
                if do_next:
                    token_major(g + 1)
                moa_output(2)
                fill(2 * EF)
                b_end()
                if do_next:
                    normed_tokens(g + 1)
                    pe.wait_ge(moa_dve.sem, moa_dve.at(g, 2))
                    pe.wait_ge(nT_act.sem, nT_act.at(g + 1, 2))
                    queries_keys(g + 1, (2, 3))
                pe.wait_ge(norm_dve.sem, norm_dve.at(g, 2))
                if do_b:
                    pe.wait_ge(out_dve.sem, out_dve.at(gb, 2))
                for last in transpose_tiles(normed, (p_up, p_gate)):
                    last.then_inc(xn2T_ps.sem, 1)
                if do_next:
                    queries_keys(g + 1, (0, 1))
                pe.wait_ge(xn2T_act.sem, xn2T_act.at(g, 2))
                for t in range(NT):
                    for c in range(DC):
                        last = mm(p_acc[0][0:TT, t * EF:(t + 1) * EF], xn2T[:, c, t * TT:(t + 1) * TT], ff_gw[:, c, :],
                                  start=(c == 0), stop=(c == DC - 1))
                last.then_inc(lg2_ps.sem, 1)
                if do_next:
                    values(g + 1)
                else:
                    gb = g
                    left = iter(UNITS)
                    gates_transposed(gb)
                    fill(2 * EF)
                    b_end()

            pe.wait_ge(w_early.sem, W_EARLY)
            patches(0)
            embeddings(0)
            token_major(0)
            normed_tokens(0)
            pe.wait_ge(nT_act.sem, nT_act.at(0, 2))
            queries_keys(0, (2, 3, 0, 1))
            values(0)
            loop(pe, body)

        @block.scalar
        def _(act):
            A_ = nc.scalar.activation

            def hidden(g):
                for m in range(DC):
                    act.wait_ge(u_ps.sem, u_ps.at(g, m + 1))
                    A_(tanh_t[:, m, :], pa[m][:, 0:GP], ACT.Tanh, bias=tok_b1h[:, m:m + 1], scale=0.5)
                    A_(pre_t[:, m, :], pa[m][:, 0:GP], ACT.Identity, bias=tok_b1[:, m:m + 1]).then_inc(u_act.sem, 1)

            def embedded(g):
                for m in range(DC):
                    act.wait_ge(emb_ps.sem, emb_ps.at(g, m + 1))
                    A_(hT[:, m, :, 0:NPATCH], pa[m][:, 0:GP].rearrange("p (b t) -> p b t", b=NB), ACT.Identity,
                       bias=tok_b2[:, m:m + 1], scale=0.5).then_inc(hT_act.sem, 1)

            def normed_tokens(g):
                for m in range(DC):
                    act.wait_ge(nT_ps.sem, nT_ps.at(g, m + 1))
                    A_(nT[:, m, :], pa[m][:, 0:GT], ACT.Copy).then_inc(nT_act.sem, 1)

            def queries_keys(g, first, chunks):
                for n, i in enumerate(chunks):
                    act.wait_ge(qk_ps.sem, qk_ps.at(g, first + n))
                    if i < 2:
                        for par in range(2):
                            last = A_(qT[:, i, par, :], pa[i][:, 0:GT], ACT.Copy, scale=parity[:, par:par + 1])
                    else:
                        last = A_(kT[:, i - 2, :], pa[i][:, 0:GT], ACT.Copy)
                    last.then_inc(qk_act.sem, 1)

            def values(g):
                for n, b in enumerate((2, 3, 0, 1)):
                    act.wait_ge(v_ps.sem, v_ps.at(g, n + 1))
                    A_(v_aug[:, b, :, 0:HD1], pa[b][0:T, 0:D].rearrange("p (h d) -> p h d", h=NH),
                       ACT.Copy).then_inc(v_act.sem, 1)

            def body(g, do_b, do_next):
                left = iter(UNITS if do_b else [])
                gb = g - 1

                def fill(n):
                    nonlocal left, gb
                    for kind, e in islice(left, n):
                        if kind == "up":
                            act.wait_ge(up_ps.sem, up_ps.at(gb, e + 1))
                            A_(relu_t[:, e % 2, :], p_up[:, 0:GT], ACT.Relu, bias=ff_b1[:, e:e + 1]).then_inc(relu_act.sem, 1)

                def b_end():
                    if do_b:
                        for m in range(DC):
                            act.wait_ge(acc_ps.sem, acc_ps.at(gb, m + 1))
                            A_(moeT[:, m, :], p_acc[m][:, 0:GT], ACT.Copy).then_inc(acc_act.sem, 1)

                def store():
                    if do_b:
                        act.wait_ge(out_dve.sem, out_dve.at(gb, 2))
                        act.dma_start(out[gb], out_t[:, :, :]).then_inc(out_free.sem, 16)

                def s1_soft(b):
                    act.wait_ge(s1_sub.sem, s1_sub.at(g, b + 1))
                    A_(s1[:, b % 2], s1[:, b % 2], ACT.Exp).then_inc(s1_exp.sem, 1)

                def p1_out(b):
                    for i in range(3):
                        act.wait_ge(p1T_ps.sem, p1T_ps.at(g, 3 * b + i + 1))
                        n = (6, 6, NH - 12)[i]
                        A_(p1T[:, 6 * i:6 * i + n, :], pa[i][0:T, 0:n * T].rearrange("p (h t) -> p h t", h=n),
                           ACT.Copy).then_inc(p1T_act.sem, 1)

                def gates2_out():
                    act.wait_ge(g2T_ps.sem, g2T_ps.at(gb, 1))
                    A_(g2T[:, :], p_acc[1][0:3 * EF, 0:GT], ACT.Copy)
                    A_(g2Tb[:, :], p_acc[1][0:3 * EF, 0:GT], ACT.Copy).then_inc(g2T_act.sem, 1)

                if do_b:
                    gates2_out()
                s1_soft(0)
                fill(1)
                fill(1)
                for b in range(NB):
                    p1_out(b)
                    fill(1)
                    if b + 1 < NB:
                        s1_soft(b + 1)
                    fill(1)
                for m in range(DC):
                    act.wait_ge(yT_ps.sem, yT_ps.at(g, m + 1))
                    A_(yT[:, m, :], pa[m][:, 0:GT], ACT.Copy).then_inc(yT_act.sem, 1)
                fill(1)
                fill(7)
                for m in range(DC):
                    act.wait_ge(xnT_ps.sem, xnT_ps.at(g, m + 1))
                    if not do_b:
                        act.wait_ge(w_late.sem, W_LATE)
                    A_(nT[:, m, :], pa[m][:, 0:GT], ACT.Identity, scale=ln1[:, 0, m:m + 1],
                       bias=ln1[:, 1, m:m + 1]).then_inc(xnT_act.sem, 1)
                fill(1)
                act.wait_ge(k2_ps.sem, k2_ps.at(g, 1))
                A_(krel[:, :, 0:T], pa[1][:, 0:GT].rearrange("p (b t) -> p b t", b=NB), ACT.Identity,
                   bias=moa_kb[:, 0:1]).then_inc(k2_act.sem, 1)
                for e in range(EA):
                    act.wait_ge(qe_ps.sem, qe_ps.at(g, e + 1))
                    A_(qeT[:, e, :], pa[(e + 3) % 4][:, 0:GT], ACT.Identity, scale=HD ** -0.5,
                       bias=moa_qb[:, e:e + 1]).then_inc(qe_act.sem, 1)

                def s2_out(b):
                    for i in range(2):
                        act.wait_ge(sr_ps.sem, sr_ps.at(g, 4 * b + i + 1))
                        A_(sr[:, b, 2 * i:2 * i + 2, :],
                           pa[i][0:T, 0:2 * KW].rearrange("p (e k) -> p e k", e=2), ACT.Copy).then_inc(sr_act.sem, 1)

                def s2_soft(b):
                    act.wait_ge(s2_sub.sem, s2_sub.at(g, b + 1))
                    A_(sr[:, b, :, 0:T], sr[:, b, :, 0:T], ACT.Exp).then_inc(s2_exp.sem, 1)

                def p2_out(b):
                    for i in range(2):
                        act.wait_ge(p2T_ps.sem, p2T_ps.at(g, 2 * b + i + 1))
                        A_(p2T[:, 4 * i:4 * i + 4, :], pa[i][0:T, 0:4 * T].rearrange("p (e t) -> p e t", e=4),
                           ACT.Copy).then_inc(p2T_act.sem, 1)

                def ctx_out(b):
                    act.wait_ge(ctx_ps.sem, ctx_ps.at(g, 2 * b + 1))
                    A_(ctxT[:, 0:4, b * T:(b + 1) * T], pa[2][:, 0:4 * T].rearrange("p (e t) -> p e t", e=4),
                       ACT.Copy).then_inc(ctx_act.sem, 1)

                s2_out(0)
                act.wait_ge(gdiff_dve.sem, gdiff_dve.at(g, 1))
                A_(gexp[0:T, 0:NB], gdiff[0:T, 0:NB], ACT.Exp).then_inc(gexp_act.sem, 1)
                for b in range(1, NB):
                    s2_out(b)
                s2_soft(0)
                fill(3)
                for b in range(NB):
                    fill(1)
                    if b + 1 < NB:
                        s2_soft(b + 1)
                    p2_out(b)
                    fill(1)
                    ctx_out(b)
                act.wait_ge(g1T_ps.sem, g1T_ps.at(g, 1))
                A_(gates1T[:, :], pa[1][0:EA, 0:GT], ACT.Copy).then_inc(g1T_act.sem, 1)
                if do_next:
                    hidden(g + 1)
                    embedded(g + 1)
                fill(2 * EF)
                b_end()
                if do_next:
                    normed_tokens(g + 1)
                    queries_keys(g + 1, 1, (2, 3))
                for m in range(DC):
                    act.wait_ge(xn2T_ps.sem, xn2T_ps.at(g, m + 1))
                    A_(xn2T[:, m, :], (p_up, p_gate)[m][:, 0:GT], ACT.Identity, scale=ln2[:, 0, m:m + 1],
                       bias=ln2[:, 1, m:m + 1]).then_inc(xn2T_act.sem, 1)
                store()
                if do_next:
                    queries_keys(g + 1, 3, (0, 1))
                act.wait_ge(gdiff_dve.sem, gdiff_dve.at(g, 2))
                A_(gexp[:, 0:NT], gdiff[:, 0:NT], ACT.Exp).then_inc(gexp_act.sem, 1)
                if do_next:
                    values(g + 1)
                else:
                    gb = g
                    left = iter(UNITS)
                    gates2_out()
                    fill(2 * EF)
                    b_end()
                    store()

            act.wait_ge(w_early.sem, W_EARLY)
            act.wait_ge(const_done.sem, 1)
            hidden(0)
            embedded(0)
            normed_tokens(0)
            queries_keys(0, 1, (2, 3, 0, 1))
            values(0)
            loop(act, body)

        @block.gpsimd
        def _(pool):
            nc.gpsimd.memset(neg_half[:, :], -0.5).then_inc(pool_const.sem, 1)
            nc.gpsimd.memset(v_aug[:, :, :, HD1:HD1 + 1], 1.0).then_inc(pool_const.sem, 1)

            def power(g, n):
                pool.wait_ge(var_dve.sem, var_dve.at(g, n))
                nc.gpsimd.tensor_tensor(rstd[:, :], vareps[:, :], neg_half[:, :], ALU.pow).then_inc(rstd_pool.sem, 1)

            def body(g, do_b, do_next):
                for b in range(NB):
                    pool.wait_ge(s1_max.sem, s1_max.at(g, b + 1))
                    nc.gpsimd.tensor_tensor(s1[:, b % 2], s1[:, b % 2],
                                            s1max[:, b % 2].unsqueeze(2).broadcast_to((T, NH, T)),
                                            ALU.subtract).then_inc(s1_sub.sem, 1)
                power(g, 2)
                power(g, 3)

                def s2_sum(b):
                    pool.wait_ge(relb_in[b].sem, relb_in[b].at(g, 16))
                    nc.gpsimd.tensor_tensor(sr[:, b, :, 0:T], sr[:, b, :, 0:T], relb[:, b],
                                            ALU.add).then_inc(s2_add.sem, 1)

                def s2_less_max(b):
                    pool.wait_ge(s2_max.sem, s2_max.at(g, b + 1))
                    nc.gpsimd.tensor_tensor(sr[:, b, :, 0:T], sr[:, b, :, 0:T],
                                            s2max[:, b].unsqueeze(2).broadcast_to((T, EA, T)),
                                            ALU.subtract).then_inc(s2_sub.sem, 1)

                def p2_scale(b):
                    pool.wait_ge(s2_fac.sem, s2_fac.at(g, b + 1))
                    nc.gpsimd.tensor_tensor(sr[:, b, :, 0:T], sr[:, b, :, 0:T],
                                            s2fac[:, b].unsqueeze(2).broadcast_to((T, EA, T)),
                                            ALU.mult).then_inc(p2_pool.sem, 1)

                s2_sum(0)
                s2_less_max(0)
                for b in range(1, NB):
                    s2_sum(b)
                    p2_scale(b - 1)
                    s2_less_max(b)
                p2_scale(NB - 1)
                if do_next:
                    power(g, 4)
                power(g, 5 if do_next else 4)

            pool.wait_ge(pool_const.sem, 2)
            power(0, 1)
            loop(pool, body)

        @block.vector
        def _(dve):
            V = nc.vector

            dve.wait_ge(w_early.sem, W_EARLY)
            V.tensor_scalar(tok_b1h[:, :], tok_b1[:, :], 0.5, None, ALU.mult).then_inc(const_done.sem, 1)

            steps = [0]

            def step(g, ins):
                steps[0] += 1
                ins.then_inc(a_step.sem, 1)
                dve.wait_ge(a_step.sem, g * BODY_STEPS + steps[0])

            def normalise(g, source, target, n, done, meanwhile=None):
                for t in range(NT):
                    last = V.bn_stats(stats[:, t, :], source[:, t, :])
                step(g, last)
                V.memset(pad[:, :], 0.0)
                for t in range(NT):
                    last = V.bn_aggr(meanvar[:, t, :], stats[:, t, :])
                step(g, last)
                V.tensor_scalar(vareps[:, :], meanvar[:, :, 1], EPS, None, ALU.add).then_inc(var_dve.sem, 1)
                if meanwhile:
                    meanwhile()
                dve.wait_ge(rstd_pool.sem, rstd_pool.at(g, n))
                for t in range(NT):
                    last = V.tensor_scalar(target[:, t, :], source[:, t, :], meanvar[:, t, 0:1], rstd[:, t:t + 1],
                                           ALU.subtract, ALU.mult)
                if done is None:
                    step(g, last)
                else:
                    last.then_inc(done.sem, 1)

            def hidden(g):
                for m in range(DC):
                    dve.wait_ge(u_act.sem, u_act.at(g, m + 1))
                    V.scalar_tensor_tensor(h1T[:, m, :], tanh_t[:, m, :], 1.0, pre_t[:, m, :], ALU.add,
                                           ALU.mult).then_inc(h1_dve.sem, 1)

            def tokens(g):
                dve.wait_ge(htok_ps.sem, htok_ps.at(g, 1))
                V.tensor_copy(h_new[:, 0:2, :], pa[0][0:TT, :].rearrange("p (t d) -> p t d", t=2)).then_inc(hres_dve.sem, 1)
                dve.wait_ge(htok_ps.sem, htok_ps.at(g, 2))
                V.tensor_copy(h_new[:, 2, :], pa[1][0:TT, 0:D]).then_inc(hres_dve.sem, 1)

            def body(g, do_b, do_next):
                steps[0] = FIRST_STEPS
                left = iter(UNITS if do_b else [])
                gb = g - 1

                def fill(n):
                    nonlocal left, gb
                    for kind, e in islice(left, n):
                        if kind == "up":
                            dve.wait_ge(relu_act.sem, relu_act.at(gb, e + 1))
                            V.tensor_tensor(hid[:, e % 2, :], relu_t[:, e % 2, :], p_gate[:, 0:GT],
                                            ALU.mult).then_inc(hid_dve.sem, 1)

                def b_end():
                    if do_b:
                        dve.wait_ge(out_ps.sem, out_ps.at(gb, 1))
                        dve.wait_ge(out_free.sem, out_free.at(gb, 16))
                        V.tensor_tensor(out_t[:, 0:2, :], base[:, 0:2, :], p_up[0:TT, :].rearrange("p (t d) -> p t d", t=2),
                                        ALU.add).then_inc(out_dve.sem, 1)
                        dve.wait_ge(out_ps.sem, out_ps.at(gb, 2))
                        V.tensor_tensor(out_t[:, 2, :], base[:, 2, :], p_gate[0:TT, 0:D], ALU.add).then_inc(out_dve.sem, 1)

                def two_best(P, n, E, k):
                    def v(t):
                        return t[0:P, 0:n * E].rearrange("p (n e) -> p n e", n=n)

                    def wide(t):
                        return t[0:P, 0:n].unsqueeze(2).broadcast_to((P, n, E))

                    ranks = rank[0:P, 0:E].unsqueeze(1).broadcast_to((P, n, E))
                    for logits, top, one in ((lg, top1, one1), (lg2, top2, one2)):
                        step(g, V.tensor_reduce(top[0:P, 0:n], v(logits), AX.X, ALU.max))
                        step(g, V.tensor_tensor(v(tmp), v(logits), wide(top), ALU.is_equal))
                        step(g, V.tensor_tensor(v(tmp), v(tmp), ranks, ALU.mult))
                        step(g, V.tensor_reduce(pick[0:P, 0:n], v(tmp), AX.X, ALU.max))
                        step(g, V.tensor_tensor(v(one), v(tmp), wide(pick), ALU.is_equal))
                        if one is one1:
                            step(g, V.scalar_tensor_tensor(lg2[0:P, 0:n * E], one1[0:P, 0:n * E], -BIG, lg[0:P, 0:n * E],
                                                        ALU.mult, ALU.add))
                    V.tensor_tensor(gdiff[0:P, 0:n], top2[0:P, 0:n], top1[0:P, 0:n],
                                    ALU.subtract).then_inc(gdiff_dve.sem, 1)

                def gate_values(P, n, E, k, target, done):
                    def v(t):
                        return t[0:P, 0:n * E].rearrange("p (n e) -> p n e", n=n)

                    def wide(t):
                        return t[0:P, 0:n].unsqueeze(2).broadcast_to((P, n, E))

                    dve.wait_ge(gexp_act.sem, gexp_act.at(g, k))
                    step(g, V.tensor_scalar(gone[0:P, 0:n], gexp[0:P, 0:n], 1.0, None, ALU.add))
                    step(g, V.reciprocal(g1[0:P, 0:n], gone[0:P, 0:n]))
                    V.tensor_tensor(g2[0:P, 0:n], g1[0:P, 0:n], gexp[0:P, 0:n], ALU.mult)
                    step(g, V.tensor_tensor(v(one1), v(one1), wide(g1), ALU.mult))
                    step(g, V.tensor_tensor(v(one2), v(one2), wide(g2), ALU.mult))
                    last = V.tensor_tensor(target, v(one1), v(one2), ALU.add)
                    if done is None:
                        step(g, last)
                    else:
                        last.then_inc(done.sem, 1)

                def s1_bias(b):
                    dve.wait_ge(s1_ps.sem, s1_ps.at(g, b + 1))
                    if b >= 2 or do_b:
                        dve.wait_ge(p1T_ps.sem, p1T_ps.at(g, 3 * (b - 1)))
                    for r in range(4):
                        last = V.tensor_tensor(s1[:, b % 2, HR * r:HR * r + HR, :],
                                               pa[r][0:T, 0:HR * T].rearrange("p (h t) -> p h t", h=HR),
                                               alibi[:, HR * r * T:HR * (r + 1) * T].rearrange("p (h t) -> p h t", h=HR),
                                               ALU.add)
                    last.then_inc(s1_add.sem, 1)
                    dve.wait_ge(s1_add.sem, s1_add.at(g, b + 1))
                    V.tensor_reduce(s1max[:, b % 2, :], s1[:, b % 2], AX.X, ALU.max).then_inc(s1_max.sem, 1)

                def y1_out(b):
                    dve.wait_ge(y1_ps.sem, y1_ps.at(g, b + 1))
                    y = pa[3][0:T, 0:NH * (HD1 + 1)].rearrange("p (h d) -> p h d", h=NH)
                    step(g, V.reciprocal(y_rec[:, :], y[:, :, HD1]))
                    V.tensor_tensor(y1[:, b, :].rearrange("p (h d) -> p h d", h=NH), y[:, :, 0:HD1],
                                    y_rec[:, :].unsqueeze(2).broadcast_to((T, NH, HD1)), ALU.mult).then_inc(y1_dve.sem, 1)

                s1_bias(0)
                fill(1)
                s1_bias(1)
                fill(1)
                for b in range(NB):
                    fill(1)
                    y1_out(b)
                    if b + 2 < NB:
                        s1_bias(b + 2)
                    fill(1)
                fill(1)
                if not do_b:
                    dve.wait_ge(w_late.sem, W_LATE)
                    V.tensor_scalar(moa_qb[:, :], moa_qb[:, :], HD ** -0.5, None, ALU.mult)
                    for b in range(NB):
                        V.tensor_copy(krel[:, b, T + T - 1 - MAXP:T + T + MAXP], rel[:, :])
                        V.tensor_copy(krel[:, b, T:T + T - 1 - MAXP], rel[:, 0:1].broadcast_to((128, T - 1 - MAXP)))
                        V.tensor_copy(krel[:, b, T + T + MAXP:KW], rel[:, NREL - 1:NREL].broadcast_to((128, T - 1 - MAXP)))
                    V.tensor_copy(sel[:, :, :].rearrange("p e f -> p (e f)"), sel32[:, :]).then_inc(const_done.sem, 1)
                dve.wait_ge(proj_ps.sem, proj_ps.at(g, 1))
                V.tensor_tensor(h_res[:, 0:2, :], h_new[:, 0:2, :], pa[2][0:TT, :].rearrange("p (t d) -> p t d", t=2),
                                ALU.add).then_inc(res_dve.sem, 1)
                dve.wait_ge(proj_ps.sem, proj_ps.at(g, 2))
                V.tensor_tensor(h_res[:, 2, :], h_new[:, 2, :], pa[3][0:TT, 0:D], ALU.add).then_inc(res_dve.sem, 1)
                dve.wait_ge(res_dve.sem, res_dve.at(g, 2))
                fill(1)
                if do_b:
                    dve.wait_ge(out_free.sem, out_free.at(gb, 16))
                normalise(g, h_res, src, 2, None)
                fill(3)
                normalise(g, src, normed, 3, norm_dve)
                fill(3)
                fill(1)
                dve.wait_ge(lg1_ps.sem, lg1_ps.at(g, 1))
                V.tensor_copy(lg[0:T, 0:NB * EA], pa[0][0:T, 0:NB * EA]).then_inc(lg_dve.sem, 1)
                dve.wait_ge(v2_ps.sem, v2_ps.at(g, 1))
                V.tensor_tensor(v2[:, :, :], pa[2][0:T, :].rearrange("p (b d) -> p b d", b=NB),
                                moa_vb[:, :].unsqueeze(1).broadcast_to((T, NB, HD)), ALU.add).then_inc(v2_dve.sem, 1)
                dve.wait_ge(lg_dve.sem, lg_dve.at(g, 1))
                two_best(T, NB, EA, 1)

                def s2_out(b):
                    for i in range(2):
                        dve.wait_ge(sr_ps.sem, sr_ps.at(g, 4 * b + i + 3))
                        V.tensor_copy(sr[:, b, 4 + 2 * i:6 + 2 * i, :],
                                      pa[2 + i][0:T, 0:2 * KW].rearrange("p (e k) -> p e k", e=2)).then_inc(sr_dve.sem, 1)

                def s2_top(b):
                    dve.wait_ge(s2_add.sem, s2_add.at(g, b + 1))
                    V.tensor_reduce(s2max[:, b, :], sr[:, b, :, 0:T], AX.X, ALU.max).then_inc(s2_max.sem, 1)

                def s2_factor(b):
                    dve.wait_ge(s2_exp.sem, s2_exp.at(g, b + 1))
                    step(g, V.tensor_reduce(s2sum[:, b, :], sr[:, b, :, 0:T], AX.X, ALU.add))
                    step(g, V.reciprocal(s2rec[:, b, :], s2sum[:, b, :]))
                    V.tensor_tensor(s2fac[:, b, :], s2rec[:, b, :], gates1[:, b, :],
                                    ALU.mult).then_inc(s2_fac.sem, 1)

                def ctx_out(b):
                    dve.wait_ge(ctx_ps.sem, ctx_ps.at(g, 2 * b + 2))
                    V.tensor_copy(ctxT[:, 4:8, b * T:(b + 1) * T],
                                  pa[3][:, 0:4 * T].rearrange("p (e t) -> p e t", e=4)).then_inc(ctx_dve.sem, 1)

                s2_out(0)
                gate_values(T, NB, EA, 1, gates1[:, :, :], gates1_dve)
                dve.wait_ge(gates1_dve.sem, gates1_dve.at(g, 1))
                for b in range(1, NB):
                    s2_out(b)
                s2_top(0)
                s2_factor(0)
                s2_top(1)
                fill(3)
                for b in range(NB):
                    fill(1)
                    if b + 1 < NB:
                        s2_factor(b + 1)
                    if b + 2 < NB:
                        s2_top(b + 2)
                    fill(1)
                    ctx_out(b)
                if do_next:
                    hidden(g + 1)
                dve.wait_ge(moa_ps.sem, moa_ps.at(g, 1))
                V.tensor_tensor(moa_x[:, 0:2, :], src[:, 0:2, :], pa[2][0:TT, :].rearrange("p (t d) -> p t d", t=2),
                                ALU.add).then_inc(moa_dve.sem, 1)
                if do_next:
                    tokens(g + 1)
                    dve.wait_ge(hres_dve.sem, hres_dve.at(g + 1, 2))
                    normalise(g, h_new, normed1, 4, norm1_dve)
                dve.wait_ge(moa_ps.sem, moa_ps.at(g, 2))
                V.tensor_tensor(moa_x[:, 2, :], src[:, 2, :], pa[3][0:TT, 0:D], ALU.add).then_inc(moa_dve.sem, 1)
                dve.wait_ge(moa_dve.sem, moa_dve.at(g, 2))
                fill(2 * EF)
                normalise(g, moa_x, normed, 5 if do_next else 4, norm_dve, meanwhile=b_end)
                if do_b:
                    dve.wait_ge(out_dve.sem, out_dve.at(gb, 2))
                V.tensor_tensor(base[:, :, :], h_res[:, :, :], moa_x[:, :, :], ALU.add)
                dve.wait_ge(lg2_ps.sem, lg2_ps.at(g, 1))
                V.tensor_copy(lg[:, 0:NT * EF], p_acc[0][0:TT, 0:NT * EF]).then_inc(lg_dve.sem, 1)
                dve.wait_ge(lg_dve.sem, lg_dve.at(g, 2))
                two_best(TT, NT, EF, 2)
                gate_values(TT, NT, EF, 2, gates2[:, :, :], None)
                step(g, V.tensor_copy(ghi[:, :, :], gates2[:, :, :]))
                V.tensor_copy(gparts[:, :, 0, :], ghi[:, :, :])
                step(g, V.tensor_tensor(gates2[:, :, :], gates2[:, :, :], ghi[:, :, :], ALU.subtract))
                step(g, V.tensor_copy(gmid[:, :, :], gates2[:, :, :]))
                V.tensor_copy(gparts[:, :, 1, :], gmid[:, :, :])
                V.tensor_tensor(gparts[:, :, 2, :], gates2[:, :, :], gmid[:, :, :],
                                ALU.subtract).then_inc(gparts_dve.sem, 1)
                if do_next:
                    assert steps[0] == FIRST_STEPS + BODY_STEPS, steps[0]
                else:
                    gb = g
                    left = iter(UNITS)
                    fill(2 * EF)
                    b_end()

            hidden(0)
            tokens(0)
            dve.wait_ge(hres_dve.sem, hres_dve.at(0, 2))
            normalise(0, h_new, normed1, 1, norm1_dve)
            assert steps[0] == FIRST_STEPS
            loop(dve, body)





def kernel(x, txt, L0_tok_W1, L0_tok_b1, L0_tok_W2, L0_tok_b2, L0_attn_w_attn, L0_attn_w_proj, L0_ffn_ln1_w,
           L0_ffn_ln1_b, L0_ffn_ln2_w, L0_ffn_ln2_b, L0_ffn_attn_gate_w, L0_ffn_q_w, L0_ffn_q_b, L0_ffn_k_w,
           L0_ffn_k_b, L0_ffn_v_w, L0_ffn_v_b, L0_ffn_o_w, L0_ffn_o_b, L0_ffn_rel_table, L0_ffn_ff_gate_w,
           L0_ffn_ff_w1, L0_ffn_ff_b1, L0_ffn_ff_w2, L0_ffn_ff_b2):
    import numpy as np
    import concourse.bacc as bacc
    from concourse.bass_utils import run_bass_kernel_spmd

    def rows(a, *shape):
        a = np.asarray(a)
        a = a.reshape(-1, 128, *a.shape[1:]).swapaxes(0, 1)
        return a.reshape(shape) if shape else a

    patches = np.asarray(x).reshape(NSEQ, 3, 7, 16, 7, 16).transpose(0, 2, 4, 1, 3, 5).reshape(G, GP, PC, 128)
    text = np.asarray(txt).reshape(G, NB, NTEXT, DC, 128)
    arrays = {
        "x": patches.transpose(0, 3, 2, 1),
        "txt": text.transpose(0, 4, 3, 1, 2),
        "tok_w1": rows(L0_tok_W1), "tok_w2": rows(L0_tok_W2),
        "tok_b1": rows(L0_tok_b1), "tok_b2": rows(L0_tok_b2),
        "wqkv": rows(np.asarray(L0_attn_w_attn).T), "wproj": rows(np.asarray(L0_attn_w_proj).T),
        "ln1": np.stack([rows(L0_ffn_ln1_w), rows(L0_ffn_ln1_b)], 1),
        "ln2": np.stack([rows(L0_ffn_ln2_w), rows(L0_ffn_ln2_b)], 1),
        "moa_gw": rows(L0_ffn_attn_gate_w),
        "moa_qw": np.asarray(L0_ffn_q_w).reshape(EA, DC, 128, HD).transpose(2, 1, 0, 3),
        "moa_qb": np.asarray(L0_ffn_q_b).T,
        "moa_kw": rows(L0_ffn_k_w), "moa_kb": np.asarray(L0_ffn_k_b).reshape(HD, 1),
        "moa_vw": rows(L0_ffn_v_w), "moa_vb": np.asarray(L0_ffn_v_b).reshape(1, HD),
        "moa_ow": np.asarray(L0_ffn_o_w).transpose(1, 0, 2), "moa_ob": np.asarray(L0_ffn_o_b),
        "rel": np.asarray(L0_ffn_rel_table).T,
        "ff_gw": rows(L0_ffn_ff_gate_w),
        "ff_w1": np.asarray(L0_ffn_ff_w1).reshape(EF, DC, 128, FH).transpose(2, 1, 0, 3),
        "ff_b1": np.asarray(L0_ffn_ff_b1).T,
        "ff_w2": np.asarray(L0_ffn_ff_w2).transpose(1, 0, 2), "ff_b2": np.asarray(L0_ffn_ff_b2),
    }
    q, k = np.arange(T)[:, None], np.arange(T)[None, :]
    slopes = (2.0 ** -0.5 * (2.0 ** -0.5) ** np.arange(NH)).astype(np.float32)
    order = [(j % HR) // 2 * 8 + 2 * (j // HR) + j % 2 for j in range(NH)]
    bias = np.where((k <= q)[:, None, :], slopes[order][None, :, None] * (k - q).astype(np.float32)[:, None, :],
                    np.float32(-BIG))
    odd = (np.arange(128) // HD1) % 2
    selectors = np.tile(np.repeat(np.eye(EF, dtype=np.float32), FH, axis=1), (3, 1))
    arrays |= {
        "ident": np.eye(128, dtype=np.float32),
        "alibi": bias.reshape(T, NH * T).astype(np.float32),
        "parity": np.stack([(odd == 0) * HD1 ** -0.5, (odd == 1) * HD1 ** -0.5], 1).astype(np.float32),
        "rank": np.tile(np.arange(EF, 0, -1, dtype=np.float32), (128, 1)),
        "sel32": selectors,
    }
    arrays = {name: np.ascontiguousarray(a) for name, a in arrays.items()}
    nc = bacc.Bacc("TRN2", target_bir_lowering=False, num_devices=1)
    A = {name: nc.dram_tensor(name + "_in", a.shape, F32, kind="ExternalInput").ap() for name, a in arrays.items()}
    o = nc.dram_tensor("out", (G, TT, NT, D), F32, kind="ExternalOutput").ap()
    build(nc, A, o)
    r = run_bass_kernel_spmd(nc, [{name + "_in": a for name, a in arrays.items()}], core_ids=[0])
    got = r.results[0]["out"]
    return got.transpose(0, 2, 1, 3).reshape(NSEQ, T, D)
```

```python
from contextlib import ExitStack
from itertools import islice

import concourse.bass as bass
from concourse import mybir

F32 = mybir.dt.float32
F32R = mybir.dt.float32r
BF16 = mybir.dt.bfloat16
ALU = mybir.AluOpType
ACT = mybir.ActivationFunctionType
AX = mybir.AxisListType

NSEQ, NPATCH, NTEXT = 64, 49, 32
T = NPATCH + NTEXT
D = 256
DC = D // 128
PATCH = 3 * 16 * 16
PC = PATCH // 128
NB = 4
G = NSEQ // NB
GT = NB * T
GP = NB * NPATCH
NT = 3
TT = GT // NT
NH, HD1 = 16, 16
HC = 128 // HD1
EA, HD = 8, 128
MAXP = 64
NREL = 2 * MAXP + 1
RW = 2 * T - 1
KW = T + RW
EF, FH = 16, 128
PT = 108
NP = HC * T // PT
EPS = 1e-5
BIG = 1e30
FIRST_STEPS, BODY_STEPS = 2, 40
GATES_AT = 2
FILL_LN, FILL_S2 = 8, 3
PIECES = [(e, q, (e * T + q) // PT, (e * T + q) % PT, min(T - q, PT - (e * T + q) % PT))
          for e in range(EA // 2) for q in range(T) if q == 0 or (e * T + q) % PT == 0]
UNITS = ([("up", 0), ("up", 1)] + [u for e in range(2, EF) for u in (("up", e), ("down", e - 2))]
         + [("down", EF - 2), ("down", EF - 1)])


class Signal:

    def __init__(self, handle, per):
        self.sem, self.per = handle, per

    def at(self, g, n):
        return g * self.per + n


def build(nc, A, out):
    ctx = ExitStack()
    with ctx:
        def sb(name, shape, dt=F32):
            return ctx.enter_context(nc.sbuf_tensor(name, shape, dt))

        def bank(name):
            return ctx.enter_context(nc.psum_tensor(name, [128, 512], F32))

        def signal(name, per=1):
            return Signal(ctx.enter_context(nc.semaphore(name)), per)

        tok_w1 = sb("tok_w1", [128, PC, D])
        tok_w2 = sb("tok_w2", [128, DC, D])
        tok_b1 = sb("tok_b1", [128, DC])
        tok_b1h = sb("tok_b1h", [128, DC])
        tok_b2 = sb("tok_b2", [128, DC])
        wqkv = sb("wqkv", [128, DC, 3 * D])
        wproj = sb("wproj", [128, DC, D])
        ln1 = sb("ln1", [128, 2, DC])
        ln2 = sb("ln2", [128, 2, DC])
        moa_gw = sb("moa_gw", [128, DC, EA])
        moa_qw = sb("moa_qw", [128, DC, EA, HD])
        moa_qb = sb("moa_qb", [128, EA])
        moa_kw = sb("moa_kw", [128, DC, HD])
        moa_kb = sb("moa_kb", [128, 1])
        moa_vw = sb("moa_vw", [128, DC, HD])
        moa_vb = sb("moa_vb", [T, HD])
        moa_ow = sb("moa_ow", [128, EA, D])
        moa_ob = sb("moa_ob", [EA, D])
        ff_gw = sb("ff_gw", [128, DC, EF])
        w1_hi = sb("w1_hi", [128, EF, DC, FH], F32R)
        w1_lo = sb("w1_lo", [128, EF, DC, FH], F32R)
        ff_b1 = sb("ff_b1", [128, EF])
        ff_w2 = sb("ff_w2", [128, EF, D])
        b2_hi = sb("b2_hi", [3 * EF, D], F32R)
        b2_lo = sb("b2_lo", [3 * EF, D], F32R)
        ident = sb("ident", [128, 128])
        alibi = sb("alibi", [PT, DC, NP * T])
        head_of = sb("head_of", [128, HC])
        sel = sb("sel", [3 * EF, EF, FH], BF16)
        expert_of = sb("expert_of", [3 * EF, EF])
        neg_half = sb("neg_half", [TT, NT])

        xT = sb("xT", [128, PC, GP])
        normed_room = sb("normed_room", [128, 2 * DC * GP])
        normed = normed_room[0:TT, 0:NT * D].rearrange("p (n d) -> p n d", n=NT)
        tanh_t = normed_room[:, 0:DC * GP].rearrange("p (c t) -> p c t", c=DC)
        pre_t = normed_room[:, DC * GP:2 * DC * GP].rearrange("p (c t) -> p c t", c=DC)
        h1T = tanh_t
        hT = sb("hT", [128, DC, NB, T])
        h_res = sb("h_res", [TT, NT, D])
        pad = sb("pad", [TT, 1])
        stats = sb("stats", [TT, NT, 6])
        meanvar = sb("meanvar", [TT, NT, 2])
        vareps = sb("vareps", [TT, NT])
        rstd = sb("rstd", [TT, NT])
        h_new = sb("h_new", [TT, NT, D])
        nT = sb("nT", [128, DC, GT])
        scores_room = sb("scores_room", [PT, NB * NP * T])
        s1 = scores_room[:].rearrange("p (s c i t) -> p s c i t", s=2, c=DC, i=NP)
        p1T = sb("p1T", [T, NH * T])
        y_rec = sb("y_rec", [T, 2, NH])
        yT = sb("yT", [128, DC, GT])
        src = sb("src", [TT, NT, D])
        qeT = sb("qeT", [128, NB, EA * T])
        qe_flat = qeT[:].rearrange("p b e -> p (b e)")
        kT = qe_flat[:, 0:DC * GT].rearrange("p (c t) -> p c t", c=DC)
        q1 = qe_flat[:, DC * GT:(DC + 1) * GT]
        krel = sb("krel", [128, NB, KW])
        v2 = sb("v2", [T, NB, HD])
        two = sb("two", [TT, NB, 8])
        gsum = sb("gsum", [TT, NB])
        grec = sb("grec", [TT, NB])
        gates1 = sb("gates1", [T, NB, EA])
        gates1T = nT[0:EA, 0, :]
        sr_q8 = sb("sr", [128, NB, NP, KW])
        sr = sr_q8[0:PT]
        q8 = sr_q8[:].rearrange("p b e t -> p (b e t)")[:, 0:DC * HC * GT].rearrange("p (c b h) -> p c b h", c=DC, b=NB)
        normed1 = sr_q8[0:TT].rearrange("p b e t -> p (b e t)")[:, 0:NT * D].rearrange("p (n d) -> p n d", n=NT)
        relb = scores_room[:].rearrange("p (b i t) -> p b i t", b=NB, i=NP)
        gate_pairs = sb("gate_pairs", [PT, NB, NP])
        s2max = sb("s2max", [PT, NB, NP])
        s1max = s2max[:].rearrange("p (s c) i -> p s c i", s=2)
        s2fac = sb("s2fac", [PT, NB, NP])
        p2T = p1T[:, 0:EA * T]
        ctxT = sb("ctxT", [128, EA, GT])
        moa_x = sb("moa_x", [TT, NT, D])
        lg, lg2, chosen, less, gexp = (moa_x[:].rearrange("p n d -> p (n d)")[:, i * (EF * NT + NB):(i + 1) * (EF * NT + NB)]
                                       for i in range(5))
        top8 = moa_x[:].rearrange("p n d -> p (n d)")[:, 5 * (EF * NT + NB):5 * (EF * NT + NB) + 8 * NB].rearrange(
            "p (n e) -> p n e", n=NB)
        gates2 = sb("gates2", [TT, NT, EF])
        ghi = sb("ghi", [TT, NT, EF], BF16)
        gmid = sb("gmid", [TT, NT, EF], BF16)
        gparts = sb("gparts", [TT, NT, 3, EF])
        y1 = ctxT[0:T].rearrange("p e t -> p (e t)")[:, 0:NB * D].rearrange("p (b d) -> p b d", b=NB)
        gate_rows = ctxT[0:NB * NP].rearrange("p e t -> p (e t)")[:, EA * GT - PT:EA * GT]
        rel = ctxT[:].rearrange("p e t -> p (e t)")[:, EA * GT - NREL:EA * GT]
        v_aug = ctxT[0:T].rearrange("p e t -> p (e t)")[:, NB * D:NB * (D + NH * (HD1 + 1))].rearrange(
            "p (b h d) -> p b h d", b=NB, h=NH)
        base = sb("base", [TT, NT, D])
        base_room = base[:].rearrange("p n d -> p (n d)")
        xn2_hi = sb("xn2_hi", [128, DC, GT], F32R)
        xn2_lo = sb("xn2_lo", [128, DC, GT], F32R)
        g2T = sb("g2T", [3 * EF, GT], F32R)
        g2Tb = sb("g2Tb", [3 * EF, GT], BF16)
        gated = sb("gated", [128, 2, GT])
        gate = sb("gate", [128, GT])
        hid_hi = sb("hid_hi", [128, 2, GT], F32R)
        hid_lo = sb("hid_lo", [128, 2, GT], F32R)
        w2_hi = sb("w2_hi", [128, 2, D], F32R)
        w2_lo = sb("w2_lo", [128, 2, D], F32R)
        ff_b2 = base_room[0:3 * EF, 0:D]
        xn2T = gated
        w1_stage = [gated[:, i, 0:D] for i in range(2)]
        moeT = yT
        out_t = src

        pa = [bank(f"pa{i}") for i in range(4)]
        p_up = bank("p_up")
        p_gate = bank("p_gate")
        p_acc = [bank(f"p_acc{i}") for i in range(2)]

        rel_dram = nc.dram_tensor("rel_scratch", [NB, EA * T, RW], F32, kind="Internal")
        gate_dram = nc.dram_tensor("gate_scratch", [NB, EA, T], F32, kind="Internal")

        w_first = signal("w_first")
        w_early = signal("w_early")
        w_late = signal("w_late")
        w_ff = signal("w_ff")
        b2_dve = signal("b2_dve")
        w1_in = [signal(f"w1_in{i}") for i in range(2)]
        w1_hi_dve = signal("w1_hi_dve")
        w1_split = signal("w1_split")
        ones_dve = signal("ones_dve")
        x2_dve = signal("x2_dve")
        const_done = signal("const_done")
        pool_const = signal("pool_const")
        x_in = signal("x_in", 16)
        txt_in = signal("txt_in", 16 * DC)
        rel_out = [signal(f"rel_out{b}", 16) for b in range(NB)]
        relb_in = [signal(f"relb_in{b}", 16 * len(PIECES)) for b in range(NB)]
        gates_out = signal("gates_out", 16)
        gates_in = signal("gates_in", 16)
        out_free = signal("out_free", 16)
        u_ps = signal("u_ps", DC)
        emb_ps = signal("emb_ps", DC)
        htok_ps = signal("htok_ps", 2)
        nT_ps = signal("nT_ps", 2)
        qk_ps = signal("qk_ps", 4)
        v_ps = signal("v_ps", NB // 2)
        s1_ps = signal("s1_ps", DC * NB)
        p1T_ps = signal("p1T_ps", 3 * NB)
        y1_ps = signal("y1_ps", NB)
        yT_ps = signal("yT_ps", DC)
        proj_ps = signal("proj_ps", 2)
        xnT_ps = signal("xnT_ps", 2)
        qe_ps = signal("qe_ps", EA)
        k2_ps = signal("k2_ps")
        v2_ps = signal("v2_ps")
        lg1_ps = signal("lg1_ps")
        g1T_ps = signal("g1T_ps")
        gp_ps = signal("gp_ps")
        sr_ps = signal("sr_ps", 3 * NB)
        p2T_ps = signal("p2T_ps", 2 * NB)
        ctx_ps = signal("ctx_ps", 2 * NB)
        moa_ps = signal("moa_ps", 2)
        xn2T_ps = signal("xn2T_ps", 2)
        lg2_ps = signal("lg2_ps")
        g2T_ps = signal("g2T_ps")
        up_ps = signal("up_ps", EF)
        acc_ps = signal("acc_ps", DC)
        out_ps = signal("out_ps", 2)
        u_act = signal("u_act", DC)
        hT_act = signal("hT_act", DC)
        nT_act = signal("nT_act", 2)
        qk_act = signal("qk_act", 4)
        v_act = signal("v_act", NB // 2)
        s1_exp = signal("s1_exp", DC * NB)
        p1T_act = signal("p1T_act", 3 * NB)
        yT_act = signal("yT_act", DC)
        xnT_act = signal("xnT_act", 2)
        qe_act = signal("qe_act", EA)
        k2_act = signal("k2_act")
        g1T_act = signal("g1T_act")
        gexp_act = signal("gexp_act", 2)
        sr_act = signal("sr_act", 2 * NB)
        s2_exp = signal("s2_exp", NB)
        s2_tot = signal("s2_tot", NB)
        s2_first = signal("s2_first")
        p2T_act = signal("p2T_act", 2 * NB)
        ctx_act = signal("ctx_act", 2 * NB)
        xn2T_act = signal("xn2T_act", 2)
        g2T_act = signal("g2T_act")
        acc_act = signal("acc_act", DC)
        a_step = signal("a_step", 0)
        h1_dve = signal("h1_dve", DC)
        hres_dve = signal("hres_dve", 2)
        var_dve = signal("var_dve", 4)
        norm1_dve = signal("norm1_dve")
        norm_dve = signal("norm_dve", 2)
        s1_max = signal("s1_max", DC * NB)
        s1_add = signal("s1_add", DC * NB)
        y1_dve = signal("y1_dve", NB)
        res_dve = signal("res_dve", 2)
        v2_dve = signal("v2_dve")
        lg_dve = signal("lg_dve", 2)
        less_dve = signal("less_dve", 2)
        gates1_dve = signal("gates1_dve")
        sr_dve = signal("sr_dve", 2 * NB)
        s2_max = signal("s2_max", NB - 1)
        p2_dve = signal("p2_dve", NB)
        moa_dve = signal("moa_dve", 2)
        gparts_dve = signal("gparts_dve")
        hid_dve = signal("hid_dve", EF)
        down_ps = signal("down_ps", EF)
        gate_ps = signal("gate_ps", EF)
        gate_act = signal("gate_act", EF)
        hhi_act = signal("hhi_act", EF)
        hlo_dve = signal("hlo_dve", EF)
        w2hi_act = signal("w2hi_act", EF)
        w2lo_pool = signal("w2lo_pool", EF)
        out_dve = signal("out_dve", 2)
        rstd_pool = signal("rstd_pool", 4)
        s1_sub = signal("s1_sub", DC * NB)
        s2_add = signal("s2_add", NB - 1)
        s2_sub = signal("s2_sub", NB - 1)
        
        q8_pool = signal("q8_pool")

        EARLY = [(tok_w2, "tok_w2"), (tok_b2, "tok_b2"), (ident, "ident"),
                 (wqkv, "wqkv"), (head_of, "head_of"), (alibi, "alibi"), (wproj, "wproj")]
        LATE = [(ln1[:], "ln1"), (moa_gw[:], "moa_gw"), (moa_kw[:], "moa_kw"), (moa_kb[:], "moa_kb"), (moa_vw[:], "moa_vw"),
                (moa_qw[:], "moa_qw"), (moa_qb[:], "moa_qb"), (rel, "rel"), (expert_of[:], "expert_of"),
                (moa_ow[:], "moa_ow"), (moa_ob[:], "moa_ob")]
        FF = [(ln2, "ln2"), (ff_gw, "ff_gw"), (ff_b1, "ff_b1"), (ff_w2, "ff_w2")]
        W_EARLY, W_LATE, W_FF = 16 * len(EARLY), 16 * (len(LATE) + 1), 16 * (len(FF) + 3)
        W1_CHUNKS = EF

        def loop(engine, body):
            body(0, False, True)
            with engine.Fori(1, G - 1) as g:
                body(g, True, True)
            body(G - 1, True, False)

        block = ctx.enter_context(nc.Block())

        @block.sync
        def _(sp):
            sp.sem_inc(out_free.sem, 16)
            sp.dma_start(tok_b1[:, :], A["tok_b1"]).then_inc(w_first.sem, 16)
            sp.dma_start(tok_w1[:, :, :], A["tok_w1"]).then_inc(w_first.sem, 16)
            sp.dma_start(xT[:, :, :], A["x"][0]).then_inc(x_in.sem, 16)
            for t, name in EARLY:
                sp.dma_start(t[:], A[name]).then_inc(w_early.sem, 16)
            sp.dma_start(hT[:, 0, :, NPATCH:T], A["txt"][0, :, 0]).then_inc(txt_in.sem, 16)
            sp.dma_start(hT[:, 1, :, NPATCH:T], A["txt"][0, :, 1]).then_inc(txt_in.sem, 16)
            for t, name in LATE:
                sp.dma_start(t, A[name]).then_inc(w_late.sem, 16)
            sp.dma_start(moa_vb[:, :], A["moa_vb"].broadcast_to((T, HD))).then_inc(w_late.sem, 16)
            for k in range(W1_CHUNKS):
                if k >= 2:
                    sp.wait_ge(w1_split.sem, k - 1)
                sp.dma_start(w1_stage[k % 2], A["ff_w1"][:, k * D:(k + 1) * D]).then_inc(w1_in[k % 2].sem, 16)
            for t, name in FF:
                sp.dma_start(t[:], A[name]).then_inc(w_ff.sem, 16)
            for i in range(3):
                sp.dma_start(ff_b2[i * EF:(i + 1) * EF], A["ff_b2"]).then_inc(w_ff.sem, 16)

            def body(g, do_b, do_next):
                if do_next:
                    sp.wait_ge(u_ps.sem, u_ps.at(g, DC))
                    sp.dma_start(xT[:, :, :], A["x"][g + 1]).then_inc(x_in.sem, 16)
                    sp.wait_ge(htok_ps.sem, htok_ps.at(g, 2))
                    for c in range(DC):
                        sp.dma_start(hT[:, c, :, NPATCH:T], A["txt"][g + 1, :, c]).then_inc(txt_in.sem, 16)
                def rel_back(b):
                    sp.wait_ge(rel_out[b].sem, rel_out[b].at(g, 16))
                    for e, q, tile, row, rows in PIECES:
                        skewed = bass.AP(tensor=rel_dram, offset=(b * EA * T + e * T + q) * RW + T - 1 - q,
                                         ap=[[RW - 1, rows], [EA // 2 * T * RW, 2], [1, T]])
                        sp.dma_start(relb[row:row + rows, b, tile:tile + NP // 2 + 1:NP // 2, :],
                                     skewed).then_inc(relb_in[b].sem, 16)

                for b in range(NB):
                    sp.wait_ge(sr_act.sem, sr_act.at(g, 2 * b + 2))
                    sp.wait_ge(sr_dve.sem, sr_dve.at(g, 2 * b + 2))
                    sp.dma_start(rel_dram.ap()[b].rearrange("(i p) r -> p i r", p=PT),
                                 sr[:, b, :, T:KW]).then_inc(rel_out[b].sem, 16)
                    if b == 0:
                        sp.wait_ge(g1T_act.sem, g1T_act.at(g, 1))
                        sp.dma_start(gate_dram.ap().rearrange("b e t -> e b t"),
                                     gates1T.rearrange("e (b t) -> e b t", b=NB)).then_inc(gates_out.sem, 16)
                    else:
                        rel_back(b - 1)
                    if b == 1:
                        sp.wait_ge(gates_out.sem, gates_out.at(g, 16))
                        sp.dma_start(gate_rows[:, :], bass.AP(tensor=gate_dram, offset=0,
                                                              ap=[[PT, NB * NP], [1, PT]])).then_inc(gates_in.sem, 16)
                rel_back(NB - 1)

            loop(sp, body)
            sp.wait_ge(out_free.sem, 16 * (G + 1))
            for b in range(NB):
                sp.wait_ge(rel_out[b].sem, 16 * G)
            sp.wait_ge(gates_out.sem, 16 * G)

        @block.tensor
        def _(pe):
            mm = nc.tensor.matmul

            def transpose_tiles(source, banks):
                for m in range(DC):
                    for t in range(NT):
                        last = nc.tensor.transpose(banks[m][:, t * TT:(t + 1) * TT],
                                                   source[:, t, m * 128:(m + 1) * 128], ident[0:TT, 0:TT])
                    yield last

            def patches(g):
                pe.wait_ge(x_in.sem, x_in.at(g, 16))
                for m in range(DC):
                    for c in range(PC):
                        last = mm(pa[m][:, 0:GP], tok_w1[:, c, m * 128:(m + 1) * 128], xT[:, c, :],
                                  start=(c == 0), stop=(c == PC - 1))
                    last.then_inc(u_ps.sem, 1)

            def embeddings(g):
                pe.wait_ge(h1_dve.sem, h1_dve.at(g, DC))
                for m in range(DC):
                    for c in range(DC):
                        last = mm(pa[m][:, 0:GP], tok_w2[:, c, m * 128:(m + 1) * 128], h1T[:, c, :],
                                  start=(c == 0), stop=(c == DC - 1))
                    last.then_inc(emb_ps.sem, 1)

            def token_major(g):
                pe.wait_ge(txt_in.sem, txt_in.at(g, 16 * DC))
                pe.wait_ge(hT_act.sem, hT_act.at(g, DC))
                flat = hT[:, :, :, :].rearrange("p c b t -> p c (b t)")
                for t in range(NT):
                    for m in range(DC):
                        last = nc.tensor.transpose(pa[t // 2][0:TT, (t % 2) * D + m * 128:(t % 2) * D + (m + 1) * 128],
                                                   flat[:, m, t * TT:(t + 1) * TT], ident[:, :])
                    if t:
                        last.then_inc(htok_ps.sem, 1)

            def normed_tokens(g):
                pe.wait_ge(norm1_dve.sem, norm1_dve.at(g, 1))
                for last in transpose_tiles(normed1, pa[0:2]):
                    last.then_inc(nT_ps.sem, 1)

            def queries_keys(g, chunks):
                for i in chunks:
                    for c in range(DC):
                        last = mm(pa[(i + 2) % 4][:, 0:GT], wqkv[:, c, i * 128:(i + 1) * 128], nT[:, c, :],
                                  start=(c == 0), stop=(c == DC - 1))
                    last.then_inc(qk_ps.sem, 1)

            def values(g):
                for b in (2, 3, 0, 1):
                    if b == 2:
                        pe.wait_ge(qk_act.sem, qk_act.at(g, 1))
                    elif b == 0:
                        pe.wait_ge(qk_act.sem, qk_act.at(g, 2))
                    for c in range(DC):
                        last = mm(pa[2 if b < 2 else 3][0:T, (b % 2) * D:(b % 2 + 1) * D], nT[:, c, b * T:(b + 1) * T], wqkv[:, c, 2 * D:3 * D],
                                  start=(c == 0), stop=(c == DC - 1))
                    if b % 2:
                        last.then_inc(v_ps.sem, 1)

            def body(g, do_b, do_next):
                left = iter(UNITS if do_b else [])
                gb = g - 1
                ups = 0

                def fill(n):
                    nonlocal left, gb, ups
                    """The next n units of stage B of the group before."""
                    for kind, e in islice(left, n):
                        if kind == "up":
                            if e == 0:
                                pe.wait_ge(x2_dve.sem, x2_dve.at(gb, 1))
                                pe.wait_ge(g2T_act.sem, g2T_act.at(gb, 1))
                            if e:
                                pe.wait_ge(gate_act.sem, gate_act.at(gb, e))
                            mm(p_gate[:, 0:GT], sel[:, e, :], g2Tb[:, :], start=True, stop=True).then_inc(gate_ps.sem, 1)
                            if e:
                                pe.wait_ge(hid_dve.sem, hid_dve.at(gb, e))
                            for c in range(DC):
                                mm(p_up[:, 0:GT], w1_hi[:, e, c, :], xn2_hi[:, c, :], start=(c == 0), stop=False)
                                mm(p_up[:, 0:GT], w1_lo[:, e, c, :], xn2_hi[:, c, :], start=False, stop=False)
                                last = mm(p_up[:, 0:GT], w1_hi[:, e, c, :], xn2_lo[:, c, :],
                                          start=False, stop=(c == DC - 1))
                            last.then_inc(up_ps.sem, 1)
                            ups = e + 1
                        else:
                            pe.wait_ge(hlo_dve.sem, hlo_dve.at(gb, e + 1))
                            pe.wait_ge(w2lo_pool.sem, w2lo_pool.at(gb, e + 1))
                            for m in range(DC):
                                cols = slice(m * 128, (m + 1) * 128)
                                mm(p_acc[m][:, 0:GT], w2_hi[:, e % 2, cols], hid_hi[:, e % 2, :],
                                   start=(e == 0), stop=False)
                                mm(p_acc[m][:, 0:GT], w2_lo[:, e % 2, cols], hid_hi[:, e % 2, :], start=False, stop=False)
                                last = mm(p_acc[m][:, 0:GT], w2_hi[:, e % 2, cols], hid_lo[:, e % 2, :],
                                          start=False, stop=False)
                            last.then_inc(down_ps.sem, 1)
                            if e == EF - 1:
                                for m in range(DC):
                                    mm(p_acc[m][:, 0:GT], b2_hi[:, m * 128:(m + 1) * 128], g2T[:, :],
                                       start=False, stop=False)
                                    mm(p_acc[m][:, 0:GT], b2_lo[:, m * 128:(m + 1) * 128], g2T[:, :],
                                       start=False, stop=True).then_inc(acc_ps.sem, 1)

                def gates_transposed(gb):
                    pe.wait_ge(gparts_dve.sem, gparts_dve.at(gb, 1))
                    for t in range(NT):
                        last = mm(p_acc[1][0:3 * EF, t * TT:(t + 1) * TT], gparts[:, t].rearrange("p k e -> p (k e)"),
                                  ident[0:TT, 0:TT], start=True, stop=True)
                    last.then_inc(g2T_ps.sem, 1)

                def b_end():
                    if not do_b:
                        return
                    pe.wait_ge(acc_act.sem, acc_act.at(gb, DC))
                    for t in range(NT):
                        dst = (p_up, p_up, p_gate)[t][0:TT, (t % 2) * D:(t % 2 + 1) * D]
                        for m in range(DC):
                            last = nc.tensor.transpose(dst[:, m * 128:(m + 1) * 128],
                                                       moeT[:, m, t * TT:(t + 1) * TT], ident[:, :])
                        if t:
                            last.then_inc(out_ps.sem, 1)

                def s1_scores(b, chunks):
                    for c in chunks:
                        if b == 0 and c == 0:
                            pe.wait_ge(qk_act.sem, qk_act.at(g, 4))
                        elif b == 0:
                            pe.wait_ge(q8_pool.sem, q8_pool.at(g, 1))
                        elif b == 1 and c == 0:
                            pe.wait_ge(v_act.sem, v_act.at(g, 2))
                            pe.wait_ge(ones_dve.sem, ones_dve.at(g, 1))
                        elif c == 1 and b >= 2:
                            pe.wait_ge(y1_dve.sem, y1_dve.at(g, b - 1))
                        for i in range(NP):
                            last = mm(pa[2 * (b % 2) + c][0:PT, i * T:(i + 1) * T], q8[:, c, b, i * PT:(i + 1) * PT],
                                      kT[:, c, b * T:(b + 1) * T], start=True, stop=True)
                        last.then_inc(s1_ps.sem, 1)

                def p1_transposes(b, parts):
                    for k in parts:
                        if k < 2:
                            pe.wait_ge(s1_exp.sem, s1_exp.at(g, 2 * b + k + 1))
                        else:
                            pe.wait_ge(p1T_act.sem, p1T_act.at(g, 3 * b + 1))
                        for i in range(4 * k, 4 * k + 4):
                            last = nc.tensor.transpose(pa[2 * (b % 2) + k % 2][0:T, i % 4 * PT:(i % 4 + 1) * PT],
                                                       s1[:, b % 2, i // NP, i % NP, :], ident[0:PT, 0:PT])
                        last.then_inc(p1T_ps.sem, 1)

                def y1_product(b):
                    for h in range(NH):
                        if h in (0, 5, 10):
                            pe.wait_ge(p1T_act.sem, p1T_act.at(g, 3 * b + h // 5 + 1))
                        if h == 0:
                            pe.wait_ge(p1T_act.sem, p1T_act.at(g, 3 * b + 2))
                        last = mm(pa[2 * (b % 2) + 1][0:T, h * (HD1 + 1):(h + 1) * (HD1 + 1)],
                                  p1T[:, h * T:(h + 1) * T], v_aug[:, b, h, :], start=True, stop=True)
                    last.then_inc(y1_ps.sem, 1)

                s1_scores(0, (0, 1))
                if do_b:
                    gates_transposed(gb)
                s1_scores(1, (0,))
                fill(1)
                s1_scores(1, (1,))
                fill(1)
                for b in range(NB):
                    p1_transposes(b, (0, 1))
                    fill(1)
                    p1_transposes(b, (2,))
                    y1_product(b)
                    if b + 2 < NB:
                        s1_scores(b + 2, (0, 1))
                    fill(1)
                pe.wait_ge(y1_dve.sem, y1_dve.at(g, NB))
                for m in range(DC):
                    for b in range(NB):
                        last = nc.tensor.transpose(pa[m][:, b * T:(b + 1) * T], y1[:, b, m * 128:(m + 1) * 128],
                                                   ident[0:T, 0:T])
                    last.then_inc(yT_ps.sem, 1)
                fill(1)
                pe.wait_ge(yT_act.sem, yT_act.at(g, DC))
                for t in range(NT):
                    for c in range(DC):
                        last = mm(pa[2 + t // 2][0:TT, (t % 2) * D:(t % 2 + 1) * D], yT[:, c, t * TT:(t + 1) * TT],
                                  wproj[:, c, :], start=(c == 0), stop=(c == DC - 1))
                    if t:
                        last.then_inc(proj_ps.sem, 1)
                fill(FILL_LN)
                pe.wait_ge(norm_dve.sem, norm_dve.at(g, 1))
                for last in transpose_tiles(normed, pa[0:2]):
                    last.then_inc(xnT_ps.sem, 1)
                fill(1)
                pe.wait_ge(xnT_act.sem, xnT_act.at(g, 2))
                if not do_b:
                    pe.wait_ge(w_late.sem, W_LATE)
                    pe.wait_ge(const_done.sem, 2)
                for b in range(NB):
                    for c in range(DC):
                        last = mm(pa[0][0:T, b * EA:(b + 1) * EA], nT[:, c, b * T:(b + 1) * T], moa_gw[:, c, :],
                                  start=(c == 0), stop=(c == DC - 1))
                last.then_inc(lg1_ps.sem, 1)
                for c in range(DC):
                    last = mm(pa[1][:, 0:GT], moa_kw[:, c, :], nT[:, c, :], start=(c == 0), stop=(c == DC - 1))
                last.then_inc(k2_ps.sem, 1)
                for b in range(NB):
                    for c in range(DC):
                        last = mm(pa[2][0:T, b * HD:(b + 1) * HD], nT[:, c, b * T:(b + 1) * T], moa_vw[:, c, :],
                                  start=(c == 0), stop=(c == DC - 1))
                last.then_inc(v2_ps.sem, 1)
                for e in range(EA):
                    i = (e + 3) % 4
                    if e == 1:
                        pe.wait_ge(lg_dve.sem, lg_dve.at(g, 1))
                    elif e == 2:
                        pe.wait_ge(k2_act.sem, k2_act.at(g, 1))
                    elif e == 3:
                        pe.wait_ge(v2_dve.sem, v2_dve.at(g, 1))
                    elif e >= 4:
                        pe.wait_ge(qe_act.sem, qe_act.at(g, e - 3))
                    for c in range(DC):
                        last = mm(pa[i][:, 0:GT], moa_qw[:, c, e, :], nT[:, c, :], start=(c == 0), stop=(c == DC - 1))
                    last.then_inc(qe_ps.sem, 1)

                def s2_scores(b):
                    for j in range(3):
                        n = 3 * b + j
                        if n < 3:
                            pe.wait_ge(qe_act.sem, qe_act.at(g, EA - 2 + n))
                        elif n >= 4:
                            before, part = (n - 4) // 3, (n - 4) % 3
                            if part == 1:
                                pe.wait_ge(sr_dve.sem, sr_dve.at(g, 2 * before + 2))
                            else:
                                pe.wait_ge(sr_act.sem, sr_act.at(g, 2 * before + part // 2 + 1))
                        for i in range(2):
                            last = mm(pa[n % 4][0:PT, i * KW:(i + 1) * KW],
                                      qeT[:, b, (2 * j + i) * PT:(2 * j + i + 1) * PT], krel[:, b, :],
                                      start=True, stop=True)
                        last.then_inc(sr_ps.sem, 1)

                def p2_transposes(b):
                    pe.wait_ge(p2_dve.sem, p2_dve.at(g, b + 1))
                    for i in range(2):
                        if b == 0 and do_next:
                            pe.wait_ge(u_act.sem, u_act.at(g + 1, i + 1))
                        for j in range(NP // 2):
                            last = nc.tensor.transpose(pa[i][0:T, j * PT:(j + 1) * PT], sr[:, b, NP // 2 * i + j, 0:T],
                                                       ident[0:PT, 0:PT])
                        last.then_inc(p2T_ps.sem, 1)

                def ctx_product(b):
                    for i in range(2):
                        pe.wait_ge(p2T_act.sem, p2T_act.at(g, 2 * b + i + 1))
                        if b:
                            pe.wait_ge(ctx_act.sem, ctx_act.at(g, 2 * (b - 1) + i + 1))
                        mm(pa[2 + i][:, 0:4 * T], v2[:, b, :], p2T[:, 4 * i * T:4 * (i + 1) * T],
                           start=True, stop=True).then_inc(ctx_ps.sem, 1)

                for b in range(NB):
                    if b == GATES_AT:
                        pe.wait_ge(gates1_dve.sem, gates1_dve.at(g, 1))
                        if do_b:
                            pe.wait_ge(gate_act.sem, gate_act.at(gb, ups))
                        for i in range(NB):
                            last = mm(p_gate[0:EA, i * T:(i + 1) * T], gates1[:, i, :], ident[0:T, 0:T],
                                      start=True, stop=True)
                        last.then_inc(g1T_ps.sem, 1)
                    s2_scores(b)
                if do_next:
                    pe.wait_ge(sr_act.sem, sr_act.at(g, 2 * NB - 1))
                    patches(g + 1)
                pe.wait_ge(sr_act.sem, sr_act.at(g, 2 * NB))
                pe.wait_ge(sr_dve.sem, sr_dve.at(g, 2 * NB))
                pe.wait_ge(g1T_act.sem, g1T_act.at(g, 1))
                pe.wait_ge(gates_in.sem, gates_in.at(g, 16))
                mm(pa[2][0:PT, 0:NB * NP], gate_rows[:, :], ident[0:NB * NP, 0:NB * NP],
                   start=True, stop=True).then_inc(gp_ps.sem, 1)
                fill(FILL_S2)
                for b in range(NB):
                    fill(1)
                    p2_transposes(b)
                    fill(1)
                    ctx_product(b)
                if do_next:
                    pe.wait_ge(p2T_act.sem, p2T_act.at(g, 2 * NB))
                    embeddings(g + 1)
                pe.wait_ge(ctx_act.sem, ctx_act.at(g, 2 * NB))

                def moa_output(t):
                    dst = pa[2 + t // 2][0:TT, (t % 2) * D:(t % 2 + 1) * D]
                    for e in range(EA):
                        mm(dst, ctxT[:, e, t * TT:(t + 1) * TT], moa_ow[:, e, :], start=(e == 0), stop=False)
                    last = mm(dst, gates1T[:, t * TT:(t + 1) * TT], moa_ob[:, :], start=False, stop=True)
                    if t:
                        last.then_inc(moa_ps.sem, 1)

                moa_output(0)
                if do_next:
                    token_major(g + 1)
                moa_output(1)
                moa_output(2)
                fill(2 * EF)
                if do_next:
                    normed_tokens(g + 1)
                b_end()
                if do_next:
                    pe.wait_ge(moa_dve.sem, moa_dve.at(g, 2))
                    pe.wait_ge(nT_act.sem, nT_act.at(g + 1, 2))
                    queries_keys(g + 1, (1, 0))
                pe.wait_ge(norm_dve.sem, norm_dve.at(g, 2))
                if do_b:
                    pe.wait_ge(out_dve.sem, out_dve.at(gb, 2))
                for last in transpose_tiles(normed, (p_up, p_gate)):
                    last.then_inc(xn2T_ps.sem, 1)
                if do_next:
                    queries_keys(g + 1, (2, 3))
                pe.wait_ge(xn2T_act.sem, xn2T_act.at(g, 2))
                if not do_b:
                    pe.wait_ge(w_ff.sem, W_FF)
                for t in range(NT):
                    for c in range(DC):
                        last = mm(p_acc[0][0:TT, t * EF:(t + 1) * EF], xn2T[:, c, t * TT:(t + 1) * TT], ff_gw[:, c, :],
                                  start=(c == 0), stop=(c == DC - 1))
                last.then_inc(lg2_ps.sem, 1)
                if do_next:
                    values(g + 1)
                else:
                    gb = g
                    left = iter(UNITS)
                    gates_transposed(gb)
                    fill(2 * EF)
                    b_end()

            pe.wait_ge(w_first.sem, 32)
            patches(0)
            pe.wait_ge(w_early.sem, W_EARLY)
            embeddings(0)
            token_major(0)
            normed_tokens(0)
            pe.wait_ge(nT_act.sem, nT_act.at(0, 2))
            queries_keys(0, (1, 0, 2, 3))
            values(0)
            loop(pe, body)

        @block.scalar
        def _(act):
            A_ = nc.scalar.activation

            def hidden(g, chunks=range(DC)):
                for m in chunks:
                    act.wait_ge(u_ps.sem, u_ps.at(g, m + 1))
                    A_(tanh_t[:, m, :], pa[m][:, 0:GP], ACT.Tanh, bias=tok_b1h[:, m:m + 1], scale=0.5)
                    A_(pre_t[:, m, :], pa[m][:, 0:GP], ACT.Identity, bias=tok_b1[:, m:m + 1]).then_inc(u_act.sem, 1)

            def embedded(g):
                for m in range(DC):
                    act.wait_ge(emb_ps.sem, emb_ps.at(g, m + 1))
                    A_(hT[:, m, :, 0:NPATCH], pa[m][:, 0:GP].rearrange("p (b t) -> p b t", b=NB), ACT.Identity,
                       bias=tok_b2[:, m:m + 1], scale=0.5).then_inc(hT_act.sem, 1)

            def normed_tokens(g):
                for m in range(DC):
                    act.wait_ge(nT_ps.sem, nT_ps.at(g, m + 1))
                    A_(nT[:, m, :], pa[m][:, 0:GT], ACT.Copy).then_inc(nT_act.sem, 1)

            def queries1(g):
                act.wait_ge(qk_ps.sem, qk_ps.at(g, 1))
                A_(q1, pa[3][:, 0:GT], ACT.Copy).then_inc(qk_act.sem, 1)

            def queries0(g, heads):
                act.wait_ge(qk_ps.sem, qk_ps.at(g, 2))
                for h in heads:
                    last = A_(q8[:, 0, :, h * T:(h + 1) * T], pa[2][:, 0:GT].rearrange("p (b t) -> p b t", b=NB),
                              ACT.Copy, scale=head_of[:, h:h + 1])
                if heads[-1] == HC - 1:
                    last.then_inc(qk_act.sem, 1)

            def keys(g):
                for c in range(DC):
                    act.wait_ge(qk_ps.sem, qk_ps.at(g, DC + c + 1))
                    A_(kT[:, c, :], pa[c][:, 0:GT], ACT.Copy).then_inc(qk_act.sem, 1)

            def values(g, n):
                act.wait_ge(v_ps.sem, v_ps.at(g, n))
                b, i = ((2, 3), (0, 2))[n - 1]
                A_(v_aug[:, b:b + 2, :, 0:HD1], pa[i][0:T, :].rearrange("p (b h d) -> p b h d", b=2, h=NH),
                   ACT.Copy).then_inc(v_act.sem, 1)

            def body(g, do_b, do_next):
                left = iter(UNITS if do_b else [])
                gb = g - 1

                def hidden_high(e):
                    act.wait_ge(hid_dve.sem, hid_dve.at(gb, e + 1))
                    if e >= 2:
                        act.wait_ge(down_ps.sem, down_ps.at(gb, e - 1))
                    A_(hid_hi[:, e % 2, :], gated[:, e % 2, :], ACT.Relu).then_inc(hhi_act.sem, 1)

                def w2_high(e):
                    if e >= 2:
                        act.wait_ge(down_ps.sem, down_ps.at(gb, e - 1))
                    A_(w2_hi[:, e % 2, :], ff_w2[:, e, :], ACT.Copy).then_inc(w2hi_act.sem, 1)

                def fill(n):
                    nonlocal left, gb
                    for kind, e in islice(left, n):
                        if kind == "up":
                            act.wait_ge(gate_ps.sem, gate_ps.at(gb, e + 1))
                            if e:
                                act.wait_ge(hid_dve.sem, hid_dve.at(gb, e))
                            A_(gate[:, :], p_gate[:, 0:GT], ACT.Copy).then_inc(gate_act.sem, 1)
                            if e in (1, 2):
                                hidden_high(e - 1)
                            if e < 2:
                                w2_high(e)
                        elif e + 2 < EF:
                            hidden_high(e + 2)
                            w2_high(e + 2)

                def b_end():
                    if do_b:
                        for m in range(DC):
                            act.wait_ge(acc_ps.sem, acc_ps.at(gb, m + 1))
                            A_(moeT[:, m, :], p_acc[m][:, 0:GT], ACT.Copy).then_inc(acc_act.sem, 1)

                def store():
                    if do_b:
                        act.wait_ge(out_dve.sem, out_dve.at(gb, 2))
                        act.dma_start(out[gb], out_t[:, :, :]).then_inc(out_free.sem, 16)

                def s1_soft(b, chunks):
                    for c in chunks:
                        act.wait_ge(s1_sub.sem, s1_sub.at(g, 2 * b + c + 1))
                        A_(s1[:, b % 2, c], s1[:, b % 2, c], ACT.Exp).then_inc(s1_exp.sem, 1)

                def p1_out(b, parts):
                    for k in parts:
                        act.wait_ge(p1T_ps.sem, p1T_ps.at(g, 3 * b + k + 1))
                        A_(p1T[:, 4 * k * PT:4 * (k + 1) * PT], pa[2 * (b % 2) + k % 2][0:T, 0:4 * PT],
                           ACT.Copy).then_inc(p1T_act.sem, 1)

                def gates2_out():
                    act.wait_ge(g2T_ps.sem, g2T_ps.at(gb, 1))
                    A_(g2T[:, :], p_acc[1][0:3 * EF, 0:GT], ACT.Copy)
                    A_(g2Tb[:, :], p_acc[1][0:3 * EF, 0:GT], ACT.Copy).then_inc(g2T_act.sem, 1)

                if do_b:
                    gates2_out()
                s1_soft(0, (0,))
                fill(1)
                s1_soft(0, (1,))
                fill(1)
                for b in range(NB):
                    p1_out(b, (0, 1))
                    fill(1)
                    p1_out(b, (2,))
                    if b + 1 < NB:
                        s1_soft(b + 1, (0, 1))
                    fill(1)
                for m in range(DC):
                    act.wait_ge(yT_ps.sem, yT_ps.at(g, m + 1))
                    A_(yT[:, m, :], pa[m][:, 0:GT], ACT.Copy).then_inc(yT_act.sem, 1)
                fill(1)
                fill(FILL_LN)
                for m in range(DC):
                    act.wait_ge(xnT_ps.sem, xnT_ps.at(g, m + 1))
                    if not do_b:
                        act.wait_ge(w_late.sem, W_LATE)
                    A_(nT[:, m, :], pa[m][:, 0:GT], ACT.Identity, scale=ln1[:, 0, m:m + 1],
                       bias=ln1[:, 1, m:m + 1]).then_inc(xnT_act.sem, 1)
                fill(1)
                act.wait_ge(k2_ps.sem, k2_ps.at(g, 1))
                A_(krel[:, :, 0:T], pa[1][:, 0:GT].rearrange("p (b t) -> p b t", b=NB), ACT.Identity,
                   bias=moa_kb[:, 0:1]).then_inc(k2_act.sem, 1)
                for e in range(EA):
                    act.wait_ge(qe_ps.sem, qe_ps.at(g, e + 1))
                    A_(qeT[:, :, e * T:(e + 1) * T], pa[(e + 3) % 4][:, 0:GT].rearrange("p (b t) -> p b t", b=NB),
                       ACT.Identity, scale=HD ** -0.5,
                       bias=moa_qb[:, e:e + 1]).then_inc(qe_act.sem, 1)

                def s2_out(b):
                    for j in (0, 2):
                        act.wait_ge(sr_ps.sem, sr_ps.at(g, 3 * b + j + 1))
                        A_(sr[:, b, 2 * j:2 * j + 2, :], pa[(3 * b + j) % 4][0:PT, 0:2 * KW].rearrange("p (i k) -> p i k", i=2),
                           ACT.Copy).then_inc(sr_act.sem, 1)

                def s2_soft(b):
                    if b == 0:
                        act.wait_ge(s2_first.sem, s2_first.at(g, 1))
                    else:
                        act.wait_ge(s2_sub.sem, s2_sub.at(g, b))
                    A_(sr[:, b, :, 0:T], sr[:, b, :, 0:T], ACT.Exp).then_inc(s2_exp.sem, 1)

                def p2_out(b):
                    for i in range(2):
                        act.wait_ge(p2T_ps.sem, p2T_ps.at(g, 2 * b + i + 1))
                        A_(p2T[:, 4 * i * T:4 * (i + 1) * T], pa[i][0:T, 0:4 * T], ACT.Copy).then_inc(p2T_act.sem, 1)

                def ctx_out(b):
                    for i in range(2):
                        act.wait_ge(ctx_ps.sem, ctx_ps.at(g, 2 * b + i + 1))
                        A_(ctxT[:, 4 * i:4 * i + 4, b * T:(b + 1) * T], pa[2 + i][:, 0:4 * T].rearrange("p (e t) -> p e t", e=4),
                           ACT.Copy).then_inc(ctx_act.sem, 1)

                s2_out(0)
                act.wait_ge(less_dve.sem, less_dve.at(g, 1))
                A_(gexp[0:T, 0:NB * (EA + 1)], less[0:T, 0:NB * (EA + 1)], ACT.Exp).then_inc(gexp_act.sem, 1)
                for b in range(1, NB):
                    if b == GATES_AT:
                        act.wait_ge(g1T_ps.sem, g1T_ps.at(g, 1))
                        A_(gates1T, p_gate[0:EA, 0:GT], ACT.Copy).then_inc(g1T_act.sem, 1)
                    s2_out(b)
                if do_next:
                    hidden(g + 1, (0,))
                s2_soft(0)
                if do_next:
                    hidden(g + 1, (1,))
                fill(FILL_S2)
                for b in range(NB):
                    if b == 0:
                        p2_out(b)
                    if b < NB - 1:
                        s2_soft(b + 1)
                    fill(1)
                    if b:
                        p2_out(b)
                    fill(1)
                    ctx_out(b)
                if do_next:
                    embedded(g + 1)
                fill(2 * EF)
                b_end()
                if do_next:
                    normed_tokens(g + 1)
                    queries1(g + 1)
                    queries0(g + 1, range(2))
                for m in range(DC):
                    act.wait_ge(xn2T_ps.sem, xn2T_ps.at(g, m + 1))
                    if not do_b:
                        act.wait_ge(w_ff.sem, W_FF)
                    A_(xn2T[:, m, :], (p_up, p_gate)[m][:, 0:GT], ACT.Identity, scale=ln2[:, 0, m:m + 1],
                       bias=ln2[:, 1, m:m + 1]).then_inc(xn2T_act.sem, 1)
                store()
                if do_next:
                    queries0(g + 1, range(2, HC))
                    keys(g + 1)
                    values(g + 1, 1)
                act.wait_ge(less_dve.sem, less_dve.at(g, 2))
                A_(gexp[:, 0:NT * (EF + 1)], less[:, 0:NT * (EF + 1)], ACT.Exp).then_inc(gexp_act.sem, 1)
                if do_next:
                    values(g + 1, 2)
                else:
                    gb = g
                    left = iter(UNITS)
                    gates2_out()
                    fill(2 * EF)
                    b_end()
                    store()

            act.wait_ge(w_first.sem, 32)
            act.wait_ge(const_done.sem, 1)
            hidden(0)
            act.wait_ge(w_early.sem, W_EARLY)
            embedded(0)
            normed_tokens(0)
            queries1(0)
            queries0(0, range(HC))
            keys(0)
            values(0, 1)
            values(0, 2)
            loop(act, body)

        @block.gpsimd
        def _(pool):
            nc.gpsimd.memset(neg_half[:, :], -0.5).then_inc(pool_const.sem, 1)
            nc.gpsimd.memset(two[:, :, :], BIG).then_inc(pool_const.sem, 1)

            def power(g, n):
                pool.wait_ge(var_dve.sem, var_dve.at(g, n))
                nc.gpsimd.tensor_tensor(rstd[:, :], vareps[:, :], neg_half[:, :], ALU.pow).then_inc(rstd_pool.sem, 1)

            def queries1(g):
                pool.wait_ge(qk_act.sem, qk_act.at(g, 1))
                for b in range(NB):
                    last = nc.gpsimd.tensor_tensor(q8[:, 1, b].rearrange("p (h t) -> p h t", h=HC),
                                                   q1[:, b * T:(b + 1) * T].unsqueeze(1).broadcast_to((128, HC, T)),
                                                   head_of[:, :].unsqueeze(2).broadcast_to((128, HC, T)), ALU.mult)
                last.then_inc(q8_pool.sem, 1)

            def body(g, do_b, do_next):
                left = iter(UNITS if do_b else [])
                gb = g - 1

                def w2_low(e):
                    pool.wait_ge(w2hi_act.sem, w2hi_act.at(gb, e + 1))
                    nc.gpsimd.tensor_tensor(w2_lo[:, e % 2, :], ff_w2[:, e, :], w2_hi[:, e % 2, :].bitcast(F32),
                                            ALU.subtract).then_inc(w2lo_pool.sem, 1)

                def fill(n):
                    nonlocal left, gb
                    for kind, e in islice(left, n):
                        if kind == "up" and e < 2:
                            w2_low(e)
                        if kind == "down" and e + 2 < EF:
                            w2_low(e + 2)

                def s1_less_max(b, chunks):
                    for c in chunks:
                        pool.wait_ge(s1_max.sem, s1_max.at(g, 2 * b + c + 1))
                        nc.gpsimd.tensor_tensor(s1[:, b % 2, c], s1[:, b % 2, c],
                                                s1max[:, b % 2, c].unsqueeze(2).broadcast_to((PT, NP, T)),
                                                ALU.subtract).then_inc(s1_sub.sem, 1)

                s1_less_max(0, (0, 1))
                s1_less_max(1, (0,))
                fill(1)
                s1_less_max(1, (1,))
                fill(1)
                for b in range(NB):
                    fill(1)
                    if b + 2 < NB:
                        s1_less_max(b + 2, (0, 1))
                    fill(1)
                fill(1)
                power(g, 2)
                fill(4)
                power(g, 3)
                fill(FILL_LN - 4)
                fill(1)

                def s2_sum(b):
                    pool.wait_ge(relb_in[b].sem, relb_in[b].at(g, 16 * len(PIECES)))
                    nc.gpsimd.tensor_tensor(sr[:, b, :, 0:T], sr[:, b, :, 0:T], relb[:, b],
                                            ALU.add).then_inc(s2_add.sem, 1)

                def s2_less_max(b):
                    pool.wait_ge(s2_max.sem, s2_max.at(g, b))
                    nc.gpsimd.tensor_tensor(sr[:, b, :, 0:T], sr[:, b, :, 0:T],
                                            s2max[:, b].unsqueeze(2).broadcast_to((PT, NP, T)),
                                            ALU.subtract).then_inc(s2_sub.sem, 1)

                s2_sum(1)
                fill(2)
                s2_less_max(1)
                s2_sum(2)
                fill(FILL_S2 - 2)
                for b in range(NB):
                    if b + 2 < NB:
                        s2_less_max(b + 2)
                    fill(1)
                    if b + 3 < NB:
                        s2_sum(b + 3)
                    fill(1)
                fill(2 * EF)
                if do_next:
                    power(g, 4)
                power(g, 5 if do_next else 4)
                if do_next:
                    queries1(g + 1)
                else:
                    gb = g
                    left = iter(UNITS)
                    fill(2 * EF)

            pool.wait_ge(pool_const.sem, 2)
            power(0, 1)
            pool.wait_ge(w_early.sem, W_EARLY)
            queries1(0)
            loop(pool, body)

        @block.vector
        def _(dve):
            V = nc.vector

            dve.wait_ge(w_first.sem, 32)
            V.tensor_scalar(tok_b1h[:, :], tok_b1[:, :], 0.5, None, ALU.mult).then_inc(const_done.sem, 1)

            def ones():
                V.memset(v_aug[:, :, :, HD1:HD1 + 1], 1.0).then_inc(ones_dve.sem, 1)

            ones()
            steps = [0]

            def step(g, ins):
                steps[0] += 1
                ins.then_inc(a_step.sem, 1)
                dve.wait_ge(a_step.sem, g * BODY_STEPS + steps[0])

            def normalise(g, source, target, n, done, meanwhile=None):
                for t in range(NT):
                    last = V.bn_stats(stats[:, t, :], source[:, t, :])
                step(g, last)
                V.memset(pad[:, :], 0.0)
                for t in range(NT):
                    last = V.bn_aggr(meanvar[:, t, :], stats[:, t, :])
                step(g, last)
                V.tensor_scalar(vareps[:, :], meanvar[:, :, 1], EPS, None, ALU.add).then_inc(var_dve.sem, 1)
                if meanwhile:
                    meanwhile()
                dve.wait_ge(rstd_pool.sem, rstd_pool.at(g, n))
                for t in range(NT):
                    last = V.tensor_scalar(target[:, t, :], source[:, t, :], meanvar[:, t, 0:1], rstd[:, t:t + 1],
                                           ALU.subtract, ALU.mult)
                if done is None:
                    step(g, last)
                else:
                    last.then_inc(done.sem, 1)

            def hidden(g, chunks=range(DC)):
                for m in chunks:
                    dve.wait_ge(u_act.sem, u_act.at(g, m + 1))
                    V.scalar_tensor_tensor(h1T[:, m, :], tanh_t[:, m, :], 1.0, pre_t[:, m, :], ALU.add,
                                           ALU.mult).then_inc(h1_dve.sem, 1)

            def tokens(g):
                dve.wait_ge(htok_ps.sem, htok_ps.at(g, 1))
                V.tensor_copy(h_new[:, 0:2, :], pa[0][0:TT, :].rearrange("p (t d) -> p t d", t=2)).then_inc(hres_dve.sem, 1)
                dve.wait_ge(htok_ps.sem, htok_ps.at(g, 2))
                V.tensor_copy(h_new[:, 2, :], pa[1][0:TT, 0:D]).then_inc(hres_dve.sem, 1)

            def body(g, do_b, do_next):
                steps[0] = FIRST_STEPS
                left = iter(UNITS if do_b else [])
                gb = g - 1

                def hidden_low(e):
                    dve.wait_ge(hhi_act.sem, hhi_act.at(gb, e + 1))
                    V.scalar_tensor_tensor(hid_lo[:, e % 2, :], gated[:, e % 2, :], 0.0, hid_hi[:, e % 2, :].bitcast(F32),
                                           ALU.max, ALU.subtract).then_inc(hlo_dve.sem, 1)

                split = iter(range(0 if do_b else W1_CHUNKS))

                def fill(n):
                    nonlocal left, gb
                    for k in islice(split, 2):
                        half = 1 + k // 2
                        dve.wait_ge(w1_in[k % 2].sem, 16 * half)
                        hi = w1_hi[:, k].rearrange("p c f -> p (c f)")
                        lo = w1_lo[:, k].rearrange("p c f -> p (c f)")
                        V.tensor_copy(hi, w1_stage[k % 2]).then_inc(w1_hi_dve.sem, 1)
                        dve.wait_ge(w1_hi_dve.sem, k + 1)
                        V.tensor_tensor(lo, w1_stage[k % 2], hi.bitcast(F32), ALU.subtract).then_inc(w1_split.sem, 1)
                    for kind, e in islice(left, n):
                        if (kind, e) == ("down", EF - 3):
                            hidden_low(EF - 1)
                        if kind == "up":
                            dve.wait_ge(up_ps.sem, up_ps.at(gb, e + 1))
                            dve.wait_ge(gate_act.sem, gate_act.at(gb, e + 1))
                            if e >= 2:
                                dve.wait_ge(hlo_dve.sem, hlo_dve.at(gb, e - 1))
                            V.scalar_tensor_tensor(gated[:, e % 2, :], p_up[:, 0:GT], ff_b1[:, e:e + 1], gate[:, :],
                                                   ALU.add, ALU.mult).then_inc(hid_dve.sem, 1)
                            if e:
                                hidden_low(e - 1)

                def b_end():
                    if do_b:
                        dve.wait_ge(out_ps.sem, out_ps.at(gb, 1))
                        dve.wait_ge(out_free.sem, out_free.at(gb, 16))
                        V.tensor_tensor(out_t[:, 0:2, :], base[:, 0:2, :], p_up[0:TT, :].rearrange("p (t d) -> p t d", t=2),
                                        ALU.add).then_inc(out_dve.sem, 1)
                        dve.wait_ge(out_ps.sem, out_ps.at(gb, 2))
                        V.tensor_tensor(out_t[:, 2, :], base[:, 2, :], p_gate[0:TT, 0:D], ALU.add).then_inc(out_dve.sem, 1)

                def gates_of(P, n, E, k, target, done, meanwhile):
                    def v(t):
                        return t[0:P, 0:n * E].rearrange("p (n e) -> p n e", n=n)

                    def wide(t):
                        return t.broadcast_to((P, n, E))

                    V.memset(pad[:, :], 0.0)
                    for i in range(n):
                        last = V.max(top8[0:P, i, :], lg[0:P, i * E:(i + 1) * E])
                    step(g, last)
                    V.tensor_tensor(v(less), v(lg), wide(top8[0:P, 0:n, 0:1]), ALU.subtract)
                    V.tensor_tensor(less[0:P, n * E:n * E + n], top8[0:P, 0:n, 1], top8[0:P, 0:n, 0],
                                    ALU.subtract).then_inc(less_dve.sem, 1)
                    step(g, V.tensor_copy(two[0:P, 0:n, 0:2], top8[0:P, 0:n, 0:2]))
                    V.memset(pad[:, :], 0.0)
                    for i in range(n):
                        last = V.match_replace(lg2[0:P, i * E:(i + 1) * E], two[0:P, i, :], lg[0:P, i * E:(i + 1) * E], -BIG)
                    step(g, last)
                    step(g, V.tensor_tensor(v(chosen), v(lg2), v(lg), ALU.is_lt))
                    meanwhile()
                    dve.wait_ge(gexp_act.sem, gexp_act.at(g, k))
                    step(g, V.tensor_scalar(gsum[0:P, 0:n], gexp[0:P, n * E:n * E + n], 1.0, None, ALU.add))
                    V.reciprocal(grec[0:P, 0:n], gsum[0:P, 0:n])
                    step(g, V.tensor_tensor(v(chosen), v(chosen), v(gexp), ALU.mult))
                    last = V.tensor_tensor(target, v(chosen), wide(grec[0:P, 0:n].unsqueeze(2)), ALU.mult)
                    if done is None:
                        step(g, last)
                    else:
                        last.then_inc(done.sem, 1)

                def s1_bias(b, chunks):
                    for c in chunks:
                        if c == 0 and (b >= 2 or do_b):
                            dve.wait_ge(p1T_ps.sem, p1T_ps.at(g, 3 * (b - 1)))
                        dve.wait_ge(s1_ps.sem, s1_ps.at(g, 2 * b + c + 1))
                        V.tensor_tensor(s1[:, b % 2, c], pa[2 * (b % 2) + c][0:PT, 0:NP * T].rearrange("p (i t) -> p i t", i=NP),
                                        alibi[:, c].rearrange("p (i t) -> p i t", i=NP), ALU.add).then_inc(s1_add.sem, 1)
                        dve.wait_ge(s1_add.sem, s1_add.at(g, 2 * b + c + 1))
                        V.tensor_reduce(s1max[:, b % 2, c], s1[:, b % 2, c], AX.X, ALU.max).then_inc(s1_max.sem, 1)

                def y1_out(b):
                    dve.wait_ge(y1_ps.sem, y1_ps.at(g, b + 1))
                    y = pa[2 * (b % 2) + 1][0:T, 0:NH * (HD1 + 1)].rearrange("p (h d) -> p h d", h=NH)
                    step(g, V.reciprocal(y_rec[:, b % 2], y[:, :, HD1]))
                    V.tensor_tensor(y1[:, b, :].rearrange("p (h d) -> p h d", h=NH), y[:, :, 0:HD1],
                                    y_rec[:, b % 2].unsqueeze(2).broadcast_to((T, NH, HD1)), ALU.mult).then_inc(y1_dve.sem, 1)

                s1_bias(0, (0, 1))
                s1_bias(1, (0,))
                fill(1)
                s1_bias(1, (1,))
                fill(1)
                for b in range(NB):
                    fill(1)
                    y1_out(b)
                    if b + 2 < NB:
                        s1_bias(b + 2, (0, 1))
                    fill(1)
                fill(1)
                if not do_b:
                    dve.wait_ge(w_late.sem, W_LATE)
                    V.tensor_scalar(moa_qb[:, :], moa_qb[:, :], HD ** -0.5, None, ALU.mult)
                    for b in range(NB):
                        V.tensor_copy(krel[:, b, T + T - 1 - MAXP:T + T + MAXP], rel)
                        V.tensor_copy(krel[:, b, T:T + T - 1 - MAXP], rel[:, 0:1].broadcast_to((128, T - 1 - MAXP)))
                        V.tensor_copy(krel[:, b, T + T + MAXP:KW], rel[:, NREL - 1:NREL].broadcast_to((128, T - 1 - MAXP)))
                    V.tensor_copy(sel[:, :, :],
                                  expert_of[:, :].unsqueeze(2).broadcast_to((3 * EF, EF, FH))).then_inc(const_done.sem, 1)
                dve.wait_ge(proj_ps.sem, proj_ps.at(g, 1))
                V.tensor_tensor(h_res[:, 0:2, :], h_new[:, 0:2, :], pa[2][0:TT, :].rearrange("p (t d) -> p t d", t=2),
                                ALU.add).then_inc(res_dve.sem, 1)
                dve.wait_ge(proj_ps.sem, proj_ps.at(g, 2))
                V.tensor_tensor(h_res[:, 2, :], h_new[:, 2, :], pa[3][0:TT, 0:D], ALU.add).then_inc(res_dve.sem, 1)
                dve.wait_ge(res_dve.sem, res_dve.at(g, 2))
                if do_b:
                    dve.wait_ge(out_free.sem, out_free.at(gb, 16))
                normalise(g, h_res, src, 2, None, meanwhile=lambda: fill(2))
                fill(2)
                normalise(g, src, normed, 3, norm_dve, meanwhile=lambda: fill(2))
                fill(FILL_LN - 6)
                fill(1)
                dve.wait_ge(lg1_ps.sem, lg1_ps.at(g, 1))
                V.tensor_copy(lg[0:T, 0:NB * EA], pa[0][0:T, 0:NB * EA]).then_inc(lg_dve.sem, 1)
                dve.wait_ge(v2_ps.sem, v2_ps.at(g, 1))
                V.tensor_tensor(v2[:, :, :], pa[2][0:T, :].rearrange("p (b d) -> p b d", b=NB),
                                moa_vb[:, :].unsqueeze(1).broadcast_to((T, NB, HD)), ALU.add).then_inc(v2_dve.sem, 1)
                dve.wait_ge(lg_dve.sem, lg_dve.at(g, 1))
                def s2_out(b):
                    dve.wait_ge(sr_ps.sem, sr_ps.at(g, 3 * b + 2))
                    V.tensor_copy(sr[:, b, 2:4, :], pa[(3 * b + 1) % 4][0:PT, 0:2 * KW].rearrange("p (i k) -> p i k", i=2)
                                  ).then_inc(sr_dve.sem, 2)

                def s2_top(b):
                    dve.wait_ge(s2_add.sem, s2_add.at(g, b))
                    V.tensor_reduce(s2max[:, b, :], sr[:, b, :, 0:T], AX.X, ALU.max).then_inc(s2_max.sem, 1)

                def s2_total(b):
                    dve.wait_ge(s2_exp.sem, s2_exp.at(g, b + 1))
                    V.tensor_reduce(s2fac[:, b, :], sr[:, b, :, 0:T], AX.X, ALU.add).then_inc(s2_tot.sem, 1)

                def s2_factor(b):
                    if b == 0:
                        dve.wait_ge(gp_ps.sem, gp_ps.at(g, 1))
                        V.tensor_copy(gate_pairs[:, :, :], pa[2][0:PT, 0:NB * NP].rearrange("p (b i) -> p b i", b=NB))
                    dve.wait_ge(s2_tot.sem, s2_tot.at(g, b + 1))
                    step(g, V.reciprocal(s2fac[:, b, :], s2fac[:, b, :]))
                    step(g, V.tensor_tensor(s2fac[:, b, :], s2fac[:, b, :], gate_pairs[:, b, :], ALU.mult))
                    V.tensor_tensor(sr[:, b, :, 0:T], sr[:, b, :, 0:T],
                                    s2fac[:, b].unsqueeze(2).broadcast_to((PT, NP, T)), ALU.mult).then_inc(p2_dve.sem, 1)

                gates_of(T, NB, EA, 1, gates1[:, :, :], gates1_dve, lambda: s2_out(0))
                dve.wait_ge(gates1_dve.sem, gates1_dve.at(g, 1))
                for b in range(1, NB):
                    s2_out(b)
                dve.wait_ge(relb_in[0].sem, relb_in[0].at(g, 16 * len(PIECES)))
                step(g, V.tensor_tensor(sr[:, 0, :, 0:T], sr[:, 0, :, 0:T], relb[:, 0], ALU.add))
                step(g, V.tensor_reduce(s2max[:, 0, :], sr[:, 0, :, 0:T], AX.X, ALU.max))
                V.tensor_tensor(sr[:, 0, :, 0:T], sr[:, 0, :, 0:T], s2max[:, 0].unsqueeze(2).broadcast_to((PT, NP, T)),
                                ALU.subtract).then_inc(s2_first.sem, 1)
                if do_next:
                    hidden(g + 1, (0,))
                s2_total(0)
                if do_next:
                    hidden(g + 1, (1,))
                fill(1)
                s2_factor(0)
                fill(1)
                s2_top(1)
                fill(FILL_S2 - 2)
                for b in range(NB):
                    fill(1)
                    if b + 1 < NB:
                        s2_total(b + 1)
                    if b + 2 < NB:
                        s2_top(b + 2)
                    if b + 1 < NB:
                        s2_factor(b + 1)
                    fill(1)
                dve.wait_ge(moa_ps.sem, moa_ps.at(g, 1))
                V.tensor_tensor(moa_x[:, 0:2, :], src[:, 0:2, :], pa[2][0:TT, :].rearrange("p (t d) -> p t d", t=2),
                                ALU.add).then_inc(moa_dve.sem, 1)
                if do_next:
                    tokens(g + 1)
                    dve.wait_ge(hres_dve.sem, hres_dve.at(g + 1, 2))
                    normalise(g, h_new, normed1, 4, norm1_dve)
                dve.wait_ge(moa_ps.sem, moa_ps.at(g, 2))
                V.tensor_tensor(moa_x[:, 2, :], src[:, 2, :], pa[3][0:TT, 0:D], ALU.add).then_inc(moa_dve.sem, 1)
                if do_next:
                    ones()
                dve.wait_ge(moa_dve.sem, moa_dve.at(g, 2))
                fill(2 * EF)
                normalise(g, moa_x, normed, 5 if do_next else 4, norm_dve, meanwhile=b_end)
                if do_b:
                    dve.wait_ge(out_dve.sem, out_dve.at(gb, 2))
                else:
                    dve.wait_ge(w_ff.sem, W_FF)
                    V.tensor_copy(b2_hi[:, :], ff_b2).then_inc(b2_dve.sem, 1)
                    dve.wait_ge(b2_dve.sem, 1)
                    V.tensor_tensor(b2_lo[:, :], ff_b2, b2_hi[:, :].bitcast(F32), ALU.subtract).then_inc(b2_dve.sem, 1)
                    dve.wait_ge(b2_dve.sem, 2)
                V.tensor_tensor(base[:, :, :], h_res[:, :, :], moa_x[:, :, :], ALU.add)
                dve.wait_ge(xn2T_act.sem, xn2T_act.at(g, 2))
                step(g, V.tensor_copy(xn2_hi[:, :, :], xn2T[:, :, :]))
                V.tensor_tensor(xn2_lo[:, :, :], xn2T[:, :, :], xn2_hi[:, :, :].bitcast(F32), ALU.subtract).then_inc(x2_dve.sem, 1)
                dve.wait_ge(lg2_ps.sem, lg2_ps.at(g, 1))
                V.tensor_copy(lg[:, 0:NT * EF], p_acc[0][0:TT, 0:NT * EF]).then_inc(lg_dve.sem, 1)
                dve.wait_ge(lg_dve.sem, lg_dve.at(g, 2))
                gates_of(TT, NT, EF, 2, gates2[:, :, :], None, lambda: None)
                step(g, V.tensor_copy(ghi[:, :, :], gates2[:, :, :]))
                V.tensor_copy(gparts[:, :, 0, :], ghi[:, :, :])
                step(g, V.tensor_tensor(gates2[:, :, :], gates2[:, :, :], ghi[:, :, :], ALU.subtract))
                step(g, V.tensor_copy(gmid[:, :, :], gates2[:, :, :]))
                V.tensor_copy(gparts[:, :, 1, :], gmid[:, :, :])
                V.tensor_tensor(gparts[:, :, 2, :], gates2[:, :, :], gmid[:, :, :],
                                ALU.subtract).then_inc(gparts_dve.sem, 1)
                if do_next:
                    assert steps[0] == FIRST_STEPS + BODY_STEPS, steps[0]
                else:
                    gb = g
                    left = iter(UNITS)
                    fill(2 * EF)
                    b_end()

            hidden(0)
            dve.wait_ge(w_early.sem, W_EARLY)
            tokens(0)
            dve.wait_ge(hres_dve.sem, hres_dve.at(0, 2))
            normalise(0, h_new, normed1, 1, norm1_dve)
            assert steps[0] == FIRST_STEPS
            loop(dve, body)





def kernel(x, txt, L0_tok_W1, L0_tok_b1, L0_tok_W2, L0_tok_b2, L0_attn_w_attn, L0_attn_w_proj, L0_ffn_ln1_w,
           L0_ffn_ln1_b, L0_ffn_ln2_w, L0_ffn_ln2_b, L0_ffn_attn_gate_w, L0_ffn_q_w, L0_ffn_q_b, L0_ffn_k_w,
           L0_ffn_k_b, L0_ffn_v_w, L0_ffn_v_b, L0_ffn_o_w, L0_ffn_o_b, L0_ffn_rel_table, L0_ffn_ff_gate_w,
           L0_ffn_ff_w1, L0_ffn_ff_b1, L0_ffn_ff_w2, L0_ffn_ff_b2):
    import numpy as np
    import concourse.bacc as bacc
    from concourse.bass_utils import run_bass_kernel_spmd

    def rows(a, *shape):
        a = np.asarray(a)
        a = a.reshape(-1, 128, *a.shape[1:]).swapaxes(0, 1)
        return a.reshape(shape) if shape else a

    patches = np.asarray(x).reshape(NSEQ, 3, 7, 16, 7, 16).transpose(0, 2, 4, 1, 3, 5).reshape(G, GP, PC, 128)
    text = np.asarray(txt).reshape(G, NB, NTEXT, DC, 128)
    arrays = {
        "x": patches.transpose(0, 3, 2, 1),
        "txt": text.transpose(0, 4, 3, 1, 2),
        "tok_w1": rows(L0_tok_W1), "tok_w2": rows(L0_tok_W2),
        "tok_b1": rows(L0_tok_b1), "tok_b2": rows(L0_tok_b2),
        "wqkv": rows(np.asarray(L0_attn_w_attn).T), "wproj": rows(np.asarray(L0_attn_w_proj).T),
        "ln1": np.stack([rows(L0_ffn_ln1_w), rows(L0_ffn_ln1_b)], 1),
        "ln2": np.stack([rows(L0_ffn_ln2_w), rows(L0_ffn_ln2_b)], 1),
        "moa_gw": rows(L0_ffn_attn_gate_w),
        "moa_qw": np.asarray(L0_ffn_q_w).reshape(EA, DC, 128, HD).transpose(2, 1, 0, 3),
        "moa_qb": np.asarray(L0_ffn_q_b).T,
        "moa_kw": rows(L0_ffn_k_w), "moa_kb": np.asarray(L0_ffn_k_b).reshape(HD, 1),
        "moa_vw": rows(L0_ffn_v_w), "moa_vb": np.asarray(L0_ffn_v_b).reshape(1, HD),
        "moa_ow": np.asarray(L0_ffn_o_w).transpose(1, 0, 2), "moa_ob": np.asarray(L0_ffn_o_b),
        "rel": np.asarray(L0_ffn_rel_table).T,
        "ff_gw": rows(L0_ffn_ff_gate_w),
        "ff_w1": np.asarray(L0_ffn_ff_w1).reshape(EF, DC, 128, FH).transpose(2, 0, 1, 3).reshape(128, EF * D),
        "ff_b1": np.asarray(L0_ffn_ff_b1).T,
        "ff_w2": np.asarray(L0_ffn_ff_w2).transpose(1, 0, 2), "ff_b2": np.asarray(L0_ffn_ff_b2),
    }
    q, k = np.arange(T)[:, None], np.arange(T)[None, :]
    slopes = (2.0 ** -0.5 * (2.0 ** -0.5) ** np.arange(NH)).astype(np.float32)
    bias = np.where((k <= q)[:, None, :], slopes[None, :, None] * (k - q).astype(np.float32)[:, None, :],
                    np.float32(-BIG))
    arrays |= {
        "ident": np.eye(128, dtype=np.float32),
        "alibi": bias.astype(np.float32).swapaxes(0, 1).reshape(DC, NP, PT, T).transpose(2, 0, 1, 3).reshape(PT, DC, NP * T),
        "head_of": np.repeat(np.eye(HC, dtype=np.float32), HD1, axis=0) * np.float32(HD1 ** -0.5),
        "expert_of": np.tile(np.eye(EF, dtype=np.float32), (3, 1)),
    }
    arrays = {name: np.ascontiguousarray(a) for name, a in arrays.items()}
    nc = bacc.Bacc("TRN2", target_bir_lowering=False, num_devices=1)
    A = {name: nc.dram_tensor(name + "_in", a.shape, F32, kind="ExternalInput").ap() for name, a in arrays.items()}
    o = nc.dram_tensor("out", (G, TT, NT, D), F32, kind="ExternalOutput").ap()
    build(nc, A, o)
    r = run_bass_kernel_spmd(nc, [{name + "_in": a for name, a in arrays.items()}], core_ids=[0])
    got = r.results[0]["out"]
    return got.transpose(0, 2, 1, 3).reshape(NSEQ, T, D)
```
